# Optimizing a Trainium2 kernel written in Bass

```python
import numpy as np
import jax
import jax.numpy as jnp

def _softmax(x, axis=-1):
    return jax.nn.softmax(x, axis=axis)

def _gelu(x):
    return jax.nn.gelu(x, approximate=True)

def _silu(x):
    return jax.nn.silu(x)

def _sigmoid(x):
    return jax.nn.sigmoid(x)

def _layernorm(x, axis=-1, eps=1e-05):
    m = jnp.mean(x, axis=axis, keepdims=True)
    v = jnp.var(x, axis=axis, keepdims=True)
    return (x - m) / jnp.sqrt(v + eps)

def _scatter_add(tgt, idx, src, axis=0):
    return tgt.at[idx].add(src)

def _segment_sum(src, seg, n):
    return jax.ops.segment_sum(src, seg, n)
kernel_name = 'mk_xattn_ffn_d4_seqx_r8_039bb1'

def setup_inputs(seed: int=0):
    np.random.seed(seed)
    _w = jnp.asarray

    def _rec_inputs():
        import jax
        import jax.numpy as jnp
        _rk = jax.random.key(seed)
        x = 7.22e-05 + 1 * jax.random.normal(jax.random.fold_in(_rk, 1), (32, 128, 128), jnp.float32)
        _lenS = 128 - jax.random.randint(jax.random.fold_in(_rk, 7), (32,), 0, max(1, 128 // 4) + 1, jnp.int32)
        _lenS2 = 77 - jax.random.randint(jax.random.fold_in(_rk, 8), (32,), 0, max(1, 77 // 4) + 1, jnp.int32)
        _ctx_768P = jax.random.normal(jax.random.fold_in(_rk, 11), (32, 16, 96), jnp.float32)
        _ctx_768c = jax.random.dirichlet(jax.random.fold_in(_rk, 511), 0.3 * jnp.ones((16,), jnp.float32), (32, 77))
        _ctx_768t = jnp.einsum('bsk,bkd->bsd', _ctx_768c, _ctx_768P)
        _ctx_768t = _ctx_768t * jax.lax.rsqrt(jnp.mean(jnp.square(_ctx_768t)) + 1e-12) * 0.953939
        ctx_768 = 2.09791e-05 + 1.00001 * (_ctx_768t + 0.3 * jax.random.normal(jax.random.fold_in(_rk, 611), (32, 77, 96), jnp.float32))
        _validS = jnp.arange(128)[None, :] < _lenS[:, None]
        _validS2 = jnp.arange(77)[None, :] < _lenS2[:, None]
        _causal = jnp.tril(jnp.ones((128, 128), dtype=bool))
        mask_BxS2_bk0 = jnp.logical_not(jnp.broadcast_to(_validS2[:, :], (32, 77)))
        return (x, ctx_768, mask_BxS2_bk0)
    x, ctx_768, mask_BxS2_bk0 = _rec_inputs()

    def _L0_xattn_setup():
        import jax, jax.numpy as jnp
        import numpy as np
        NUM_HEADS = 16
        key = jax.random.key(seed)
        ks = jax.random.split(key, 8)
        dim, cond_dim = (128, 96)
        B, N, condN = (4, 256, 128)
        s = lambda k, shp, fan: jax.random.normal(k, shp, dtype=jnp.float32) * fan ** (-0.5)
        return {'x': jax.random.normal(ks[0], (B, N, dim), dtype=jnp.float32), 'cond': jax.random.normal(ks[1], (B, condN, cond_dim), dtype=jnp.float32), 'q_w': s(ks[2], (dim, dim), dim), 'q_b': jnp.zeros((dim,), jnp.float32), 'kv_w': s(ks[3], (cond_dim, 2 * dim), cond_dim), 'kv_b': jnp.zeros((2 * dim,), jnp.float32), 'proj_w': s(ks[4], (dim, dim), dim), 'proj_b': jnp.zeros((dim,), jnp.float32)}
    _L0_xattn_all = _L0_xattn_setup()
    _L0_xattn_in = {k: v for k, v in _L0_xattn_all.items() if k in ('q_w', 'q_b', 'kv_w', 'kv_b', 'proj_w', 'proj_b')}
    del _L0_xattn_all

    def _L0_ffn_setup():
        import jax, jax.numpy as jnp
        import numpy as np
        D = 128
        E = 8
        K = 2
        DF = 512
        B, S = (2, 256)
        EPS_LN = 1e-05
        EPS_TOPK = 1e-08

        def _xavier(key, shape, fan_in, fan_out, dtype=jnp.float32):
            bound = float(np.sqrt(6.0 / (fan_in + fan_out)))
            return jax.random.uniform(key, shape, dtype, -bound, bound)
        key = jax.random.key(seed)
        kx, kg, k1, k2 = jax.random.split(key, 4)
        return {'x': jax.random.normal(kx, (B, S, D), jnp.float32), 'gamma': jnp.ones((D,), jnp.float32), 'beta': jnp.zeros((D,), jnp.float32), 'Wg': _xavier(kg, (E, D), D, E), 'bg': jnp.zeros((E,), jnp.float32), 'W1': _xavier(k1, (E, DF, D), D, DF), 'b1': jnp.zeros((E, DF), jnp.float32), 'W2': _xavier(k2, (E, D, DF), DF, D), 'b2': jnp.zeros((E, D), jnp.float32)}
    _L0_ffn_all = _L0_ffn_setup()
    _L0_ffn_in = {k: v for k, v in _L0_ffn_all.items() if k in ('gamma', 'beta', 'Wg', 'bg', 'W1', 'b1', 'W2', 'b2')}
    del _L0_ffn_all

    def _L1_xattn_setup():
        import jax, jax.numpy as jnp
        import numpy as np
        HEADS = 16
        DIM_HEAD = 64
        SCALE = DIM_HEAD ** (-0.5)
        key = jax.random.key(seed)
        ks = jax.random.split(key, 7)
        B, Nq, Dq = (16, 512, 128)
        Nc, Dc = (77, 96)
        inner = HEADS * DIM_HEAD
        return {'x': jax.random.normal(ks[0], (B, Nq, Dq), jnp.float32), 'context': jax.random.normal(ks[1], (B, Nc, Dc), jnp.float32), 'Wq': jax.random.normal(ks[2], (Dq, inner), jnp.float32) * Dq ** (-0.5), 'Wk': jax.random.normal(ks[3], (Dc, inner), jnp.float32) * Dc ** (-0.5), 'Wv': jax.random.normal(ks[4], (Dc, inner), jnp.float32) * Dc ** (-0.5), 'Wo': jax.random.normal(ks[5], (inner, Dq), jnp.float32) * inner ** (-0.5), 'bo': jnp.zeros((Dq,), jnp.float32)}
    _L1_xattn_all = _L1_xattn_setup()
    _L1_xattn_in = {k: v for k, v in _L1_xattn_all.items() if k in ('Wq', 'Wk', 'Wv', 'Wo', 'bo')}
    del _L1_xattn_all

    def _L1_ffn_setup():
        import math
        import jax, jax.numpy as jnp
        import numpy as np
        E = 24

        def layer_norm(x, w, b, eps=1e-06):
            m = x.mean(-1, keepdims=True)
            v = x.var(-1, keepdims=True)
            return (x - m) / jnp.sqrt(v + eps) * w + b

        def top2_dispatch(x, Wg, C):
            logits = x @ Wg
            gates = jax.nn.softmax(logits, axis=-1)
            idx1 = jnp.argmax(gates, axis=-1)
            m1 = jax.nn.one_hot(idx1, E, dtype=x.dtype)
            masked = jnp.where(m1 > 0, -jnp.inf, logits)
            idx2 = jnp.argmax(masked, axis=-1)
            m2 = jax.nn.one_hot(idx2, E, dtype=x.dtype)
            loc1 = jnp.cumsum(m1, axis=0) - m1
            loc2 = jnp.cumsum(m2, axis=0) - m2 + jnp.sum(m1, axis=0, keepdims=True)
            m1 = m1 * (loc1 < C)
            m2 = m2 * (loc2 < C)
            g1 = jnp.sum(gates * m1, axis=-1)
            g2 = jnp.sum(gates * m2, axis=-1)
            denom = jnp.maximum(g1 + g2, 1e-09)
            g1, g2 = (g1 / denom, g2 / denom)
            p1 = jnp.sum(loc1 * m1, axis=-1).astype(jnp.int32)
            p2 = jnp.sum(loc2 * m2, axis=-1).astype(jnp.int32)
            c1 = g1[:, None, None] * m1[:, :, None] * jax.nn.one_hot(p1, C, dtype=x.dtype)[:, None, :]
            c2 = g2[:, None, None] * m2[:, :, None] * jax.nn.one_hot(p2, C, dtype=x.dtype)[:, None, :]
            combine = c1 + c2
            dispatch = (combine > 0).astype(x.dtype)
            return (combine, dispatch)

        def moe_apply(x, combine, dispatch, W, b):
            disp = jnp.einsum('sec,sd->ecd', dispatch, x)
            h = jnp.einsum('ecd,edf->ecf', disp, W) + b[:, None, :]
            return jnp.einsum('sec,ecf->sf', combine, h)
        b, seq, d_in, d_hid = (4, 256, 128, 512)
        ks = jax.random.split(jax.random.key(seed), 6)
        s = 0.02
        return {'x': jax.random.normal(ks[0], (b, seq, d_in), dtype=jnp.float32), 'Wg': jax.random.normal(ks[1], (d_in, E), dtype=jnp.float32) * s, 'W1': jax.random.normal(ks[2], (E, d_in, d_hid), dtype=jnp.float32) * s, 'b1': jnp.zeros((E, d_hid), dtype=jnp.float32), 'W2': jax.random.normal(ks[3], (E, d_hid, d_in), dtype=jnp.float32) * s, 'b2': jnp.zeros((E, d_in), dtype=jnp.float32), 'ln_hid_w': jnp.ones((4, d_hid), dtype=jnp.float32), 'ln_hid_b': jnp.zeros((4, d_hid), dtype=jnp.float32), 'ln_out_w': jnp.ones((d_in,), dtype=jnp.float32), 'ln_out_b': jnp.zeros((d_in,), dtype=jnp.float32)}
    _L1_ffn_all = _L1_ffn_setup()
    _L1_ffn_in = {k: v for k, v in _L1_ffn_all.items() if k in ('Wg', 'W1', 'b1', 'W2', 'b2', 'ln_hid_w', 'ln_hid_b', 'ln_out_w', 'ln_out_b')}
    del _L1_ffn_all

    def _L2_xattn_setup():
        import jax, jax.numpy as jnp
        import numpy as np
        DIM_IN, DIM_LAT, DIM_HEAD = (96, 128, 64)
        INNER = max(DIM_LAT, DIM_IN)
        HEADS = INNER // DIM_HEAD
        SCALE = DIM_HEAD ** (-0.5)
        RMS_EPS = 1e-08
        LN_EPS = 1e-05

        def layernorm(x, g, b):
            mu = jnp.mean(x, axis=-1, keepdims=True)
            var = jnp.mean((x - mu) ** 2, axis=-1, keepdims=True)
            return (x - mu) * jax.lax.rsqrt(var + LN_EPS) * g + b

        def rmsnorm(x, gamma):
            norm = jnp.sqrt(jnp.sum(x * x, axis=-1, keepdims=True)) * x.shape[-1] ** (-0.5)
            return x / jnp.maximum(norm, RMS_EPS) * gamma
        key = jax.random.key(seed)
        ks = jax.random.split(key, 12)
        b, n, m = (4, 512, 64)
        x = jax.random.normal(ks[0], (b, n, DIM_IN), jnp.float32)
        latents = jax.random.normal(ks[1], (b, m, DIM_LAT), jnp.float32)
        mask = jax.random.randint(ks[2], (b, n), 0, 2).astype(bool)
        s = lambda k, sh, fan: jax.random.normal(k, sh, jnp.float32) * fan ** (-0.5)
        return {'x': x, 'latents': latents, 'mask': mask, 'ln_x_g': jnp.ones((DIM_IN,), jnp.float32), 'ln_x_b': jnp.zeros((DIM_IN,), jnp.float32), 'ln_l_g': jnp.ones((DIM_LAT,), jnp.float32), 'ln_l_b': jnp.zeros((DIM_LAT,), jnp.float32), 'qn_g': jnp.ones((DIM_HEAD,), jnp.float32), 'kn_g': jnp.ones((DIM_HEAD,), jnp.float32), 'Wq': s(ks[3], (INNER, DIM_LAT), DIM_LAT), 'Wkv': s(ks[4], (2 * INNER, DIM_IN), DIM_IN), 'Wlkv': s(ks[5], (2 * INNER, DIM_LAT), DIM_LAT), 'Wo': s(ks[6], (DIM_LAT, INNER), INNER), 'bo': jnp.zeros((DIM_LAT,), jnp.float32)}
    _L2_xattn_all = _L2_xattn_setup()
    _L2_xattn_in = {k: v for k, v in _L2_xattn_all.items() if k in ('ln_x_g', 'ln_x_b', 'ln_l_g', 'ln_l_b', 'qn_g', 'kn_g', 'Wq', 'Wkv', 'Wlkv', 'Wo', 'bo')}
    del _L2_xattn_all

    def _L2_ffn_setup():
        import jax, jax.numpy as jnp
        import numpy as np
        B, T, D, FF, E, TOP_K = (4, 256, 128, 512, 8, 2)
        key = jax.random.key(seed)
        k0, k1, k2, k3 = jax.random.split(key, 4)
        x = jax.random.normal(k0, (B, T, D), dtype=jnp.float32)
        router_w = jax.random.normal(k1, (E, D), dtype=jnp.float32) * D ** (-0.5)
        w1 = jax.random.normal(k2, (E, D, FF), dtype=jnp.float32) * D ** (-0.5)
        w2 = jax.random.normal(k3, (E, FF, D), dtype=jnp.float32) * FF ** (-0.5)
        return {'x': x, 'router_w': router_w, 'w1': w1, 'w2': w2}
    _L2_ffn_all = _L2_ffn_setup()
    _L2_ffn_in = {k: v for k, v in _L2_ffn_all.items() if k in ('router_w', 'w1', 'w2')}
    del _L2_ffn_all

    def _L3_xattn_setup():
        import jax, jax.numpy as jnp
        import numpy as np
        QUERY_DIM = 128
        CONTEXT_DIM = 96
        HEADS = 8
        DIM_HEAD = 64
        INNER = HEADS * DIM_HEAD
        key = jax.random.key(seed)
        ks = jax.random.split(key, 7)
        B, S, L = (8, 512, 77)
        x = jax.random.normal(ks[0], (B, S, QUERY_DIM), dtype=jnp.float32)
        context = jax.random.normal(ks[1], (B, L, CONTEXT_DIM), dtype=jnp.float32)
        Wq = jax.random.normal(ks[2], (QUERY_DIM, INNER), dtype=jnp.float32) * QUERY_DIM ** (-0.5)
        Wk = jax.random.normal(ks[3], (CONTEXT_DIM, INNER), dtype=jnp.float32) * CONTEXT_DIM ** (-0.5)
        Wv = jax.random.normal(ks[4], (CONTEXT_DIM, INNER), dtype=jnp.float32) * CONTEXT_DIM ** (-0.5)
        Wo = jax.random.normal(ks[5], (INNER, QUERY_DIM), dtype=jnp.float32) * INNER ** (-0.5)
        bo = jax.random.normal(ks[6], (QUERY_DIM,), dtype=jnp.float32) * 0.01
        return {'x': x, 'context': context, 'Wq': Wq, 'Wk': Wk, 'Wv': Wv, 'Wo': Wo, 'bo': bo}
    _L3_xattn_all = _L3_xattn_setup()
    _L3_xattn_in = {k: v for k, v in _L3_xattn_all.items() if k in ('Wq', 'Wk', 'Wv', 'Wo', 'bo')}
    del _L3_xattn_all

    def _L3_ffn_setup():
        import jax, jax.numpy as jnp
        import numpy as np
        D_MODEL = 128
        NHEAD = 16
        HEAD_DIM = D_MODEL // NHEAD
        FF = 256
        NUM_EXPERTS = 8
        EPS = 1e-05

        def _ln(x, g, b):
            m = x.mean(-1, keepdims=True)
            v = ((x - m) ** 2).mean(-1, keepdims=True)
            return (x - m) / jnp.sqrt(v + EPS) * g + b

        def _attention(src, Wq, bq, Wk, bk, Wv, bv, Wo, bo):
            B, T, d = src.shape
            scale = HEAD_DIM ** (-0.5)
            q = (src @ Wq + bq).reshape(B, T, NHEAD, HEAD_DIM)
            k = (src @ Wk + bk).reshape(B, T, NHEAD, HEAD_DIM)
            v = (src @ Wv + bv).reshape(B, T, NHEAD, HEAD_DIM)
            scores = jnp.einsum('bqhd,bkhd->bhqk', q, k) * scale
            probs = jax.nn.softmax(scores, axis=-1)
            out = jnp.einsum('bhqk,bkhd->bqhd', probs, v).reshape(B, T, d)
            return out @ Wo + bo

        def _moe(x, gW, gb, W1, b1, W2, b2):
            B, T, d = x.shape
            xf = x.reshape(-1, d)
            gates = jax.nn.softmax(xf @ gW + gb, axis=-1)
            top2_scores, top2_idx = jax.lax.top_k(gates, 2)
            w = (jax.nn.one_hot(top2_idx, NUM_EXPERTS, dtype=xf.dtype) * top2_scores[..., None]).sum(1)
            h = jax.nn.relu(jnp.einsum('nd,edf->enf', xf, W1) + b1[:, None, :])
            y = jnp.einsum('enf,efd->end', h, W2) + b2[:, None, :]
            out = jnp.einsum('ne,end->nd', w, y)
            return out.reshape(B, T, d)
        key = jax.random.key(seed)
        ks = jax.random.split(key, 12)
        s = 0.02
        d, f, E = (D_MODEL, FF, NUM_EXPERTS)
        return {'src': jax.random.normal(ks[0], (8, 64, d), dtype=jnp.float32), 'Wq': jax.random.normal(ks[1], (d, d), dtype=jnp.float32) * s, 'bq': jnp.zeros((d,), jnp.float32), 'Wk': jax.random.normal(ks[2], (d, d), dtype=jnp.float32) * s, 'bk': jnp.zeros((d,), jnp.float32), 'Wv': jax.random.normal(ks[3], (d, d), dtype=jnp.float32) * s, 'bv': jnp.zeros((d,), jnp.float32), 'Wo': jax.random.normal(ks[4], (d, d), dtype=jnp.float32) * s, 'bo': jnp.zeros((d,), jnp.float32), 'gW': jax.random.normal(ks[5], (d, E), dtype=jnp.float32) * s, 'gb': jnp.zeros((E,), jnp.float32), 'W1': jax.random.normal(ks[6], (E, d, f), dtype=jnp.float32) * s, 'b1': jnp.zeros((E, f), jnp.float32), 'W2': jax.random.normal(ks[7], (E, f, d), dtype=jnp.float32) * s, 'b2': jnp.zeros((E, d), jnp.float32), 'ln1_g': jnp.ones((d,), jnp.float32), 'ln1_b': jnp.zeros((d,), jnp.float32), 'ln2_g': jnp.ones((d,), jnp.float32), 'ln2_b': jnp.zeros((d,), jnp.float32)}
    _L3_ffn_all = _L3_ffn_setup()
    _L3_ffn_in = {k: v for k, v in _L3_ffn_all.items() if k in ('Wq', 'bq', 'Wk', 'bk', 'Wv', 'bv', 'Wo', 'bo', 'gW', 'gb', 'W1', 'b1', 'W2', 'b2', 'ln1_g', 'ln1_b', 'ln2_g', 'ln2_b')}
    del _L3_ffn_all
    return {'x': x, 'ctx_768': ctx_768, 'mask_BxS2_bk0': mask_BxS2_bk0, 'L0_xattn_q_w': _L0_xattn_in['q_w'], 'L0_xattn_q_b': _L0_xattn_in['q_b'], 'L0_xattn_kv_w': _L0_xattn_in['kv_w'], 'L0_xattn_kv_b': _L0_xattn_in['kv_b'], 'L0_xattn_proj_w': _L0_xattn_in['proj_w'], 'L0_xattn_proj_b': _L0_xattn_in['proj_b'], 'L0_ffn_gamma': _L0_ffn_in['gamma'], 'L0_ffn_beta': _L0_ffn_in['beta'], 'L0_ffn_Wg': _L0_ffn_in['Wg'], 'L0_ffn_bg': _L0_ffn_in['bg'], 'L0_ffn_W1': _L0_ffn_in['W1'], 'L0_ffn_b1': _L0_ffn_in['b1'], 'L0_ffn_W2': _L0_ffn_in['W2'], 'L0_ffn_b2': _L0_ffn_in['b2'], 'L1_xattn_Wq': _L1_xattn_in['Wq'], 'L1_xattn_Wk': _L1_xattn_in['Wk'], 'L1_xattn_Wv': _L1_xattn_in['Wv'], 'L1_xattn_Wo': _L1_xattn_in['Wo'], 'L1_xattn_bo': _L1_xattn_in['bo'], 'L1_ffn_Wg': _L1_ffn_in['Wg'], 'L1_ffn_W1': _L1_ffn_in['W1'], 'L1_ffn_b1': _L1_ffn_in['b1'], 'L1_ffn_W2': _L1_ffn_in['W2'], 'L1_ffn_b2': _L1_ffn_in['b2'], 'L1_ffn_ln_hid_w': _L1_ffn_in['ln_hid_w'], 'L1_ffn_ln_hid_b': _L1_ffn_in['ln_hid_b'], 'L1_ffn_ln_out_w': _L1_ffn_in['ln_out_w'], 'L1_ffn_ln_out_b': _L1_ffn_in['ln_out_b'], 'L2_xattn_ln_x_g': _L2_xattn_in['ln_x_g'], 'L2_xattn_ln_x_b': _L2_xattn_in['ln_x_b'], 'L2_xattn_ln_l_g': _L2_xattn_in['ln_l_g'], 'L2_xattn_ln_l_b': _L2_xattn_in['ln_l_b'], 'L2_xattn_qn_g': _L2_xattn_in['qn_g'], 'L2_xattn_kn_g': _L2_xattn_in['kn_g'], 'L2_xattn_Wq': _L2_xattn_in['Wq'], 'L2_xattn_Wkv': _L2_xattn_in['Wkv'], 'L2_xattn_Wlkv': _L2_xattn_in['Wlkv'], 'L2_xattn_Wo': _L2_xattn_in['Wo'], 'L2_xattn_bo': _L2_xattn_in['bo'], 'L2_ffn_router_w': _L2_ffn_in['router_w'], 'L2_ffn_w1': _L2_ffn_in['w1'], 'L2_ffn_w2': _L2_ffn_in['w2'], 'L3_xattn_Wq': _L3_xattn_in['Wq'], 'L3_xattn_Wk': _L3_xattn_in['Wk'], 'L3_xattn_Wv': _L3_xattn_in['Wv'], 'L3_xattn_Wo': _L3_xattn_in['Wo'], 'L3_xattn_bo': _L3_xattn_in['bo'], 'L3_ffn_Wq': _L3_ffn_in['Wq'], 'L3_ffn_bq': _L3_ffn_in['bq'], 'L3_ffn_Wk': _L3_ffn_in['Wk'], 'L3_ffn_bk': _L3_ffn_in['bk'], 'L3_ffn_Wv': _L3_ffn_in['Wv'], 'L3_ffn_bv': _L3_ffn_in['bv'], 'L3_ffn_Wo': _L3_ffn_in['Wo'], 'L3_ffn_bo': _L3_ffn_in['bo'], 'L3_ffn_gW': _L3_ffn_in['gW'], 'L3_ffn_gb': _L3_ffn_in['gb'], 'L3_ffn_W1': _L3_ffn_in['W1'], 'L3_ffn_b1': _L3_ffn_in['b1'], 'L3_ffn_W2': _L3_ffn_in['W2'], 'L3_ffn_b2': _L3_ffn_in['b2'], 'L3_ffn_ln1_g': _L3_ffn_in['ln1_g'], 'L3_ffn_ln1_b': _L3_ffn_in['ln1_b'], 'L3_ffn_ln2_g': _L3_ffn_in['ln2_g'], 'L3_ffn_ln2_b': _L3_ffn_in['ln2_b']}

def reference(x, ctx_768, mask_BxS2_bk0, L0_xattn_q_w, L0_xattn_q_b, L0_xattn_kv_w, L0_xattn_kv_b, L0_xattn_proj_w, L0_xattn_proj_b, L0_ffn_gamma, L0_ffn_beta, L0_ffn_Wg, L0_ffn_bg, L0_ffn_W1, L0_ffn_b1, L0_ffn_W2, L0_ffn_b2, L1_xattn_Wq, L1_xattn_Wk, L1_xattn_Wv, L1_xattn_Wo, L1_xattn_bo, L1_ffn_Wg, L1_ffn_W1, L1_ffn_b1, L1_ffn_W2, L1_ffn_b2, L1_ffn_ln_hid_w, L1_ffn_ln_hid_b, L1_ffn_ln_out_w, L1_ffn_ln_out_b, L2_xattn_ln_x_g, L2_xattn_ln_x_b, L2_xattn_ln_l_g, L2_xattn_ln_l_b, L2_xattn_qn_g, L2_xattn_kn_g, L2_xattn_Wq, L2_xattn_Wkv, L2_xattn_Wlkv, L2_xattn_Wo, L2_xattn_bo, L2_ffn_router_w, L2_ffn_w1, L2_ffn_w2, L3_xattn_Wq, L3_xattn_Wk, L3_xattn_Wv, L3_xattn_Wo, L3_xattn_bo, L3_ffn_Wq, L3_ffn_bq, L3_ffn_Wk, L3_ffn_bk, L3_ffn_Wv, L3_ffn_bv, L3_ffn_Wo, L3_ffn_bo, L3_ffn_gW, L3_ffn_gb, L3_ffn_W1, L3_ffn_b1, L3_ffn_W2, L3_ffn_b2, L3_ffn_ln1_g, L3_ffn_ln1_b, L3_ffn_ln2_g, L3_ffn_ln2_b):
    import jax
    import jax.numpy as jnp

    def _L0_xattn_ref(x, cond, q_w, q_b, kv_w, kv_b, proj_w, proj_b):
        import jax, jax.numpy as jnp
        import numpy as np
        NUM_HEADS = 16
        B, N, C = x.shape
        condN = cond.shape[1]
        H = NUM_HEADS
        hd = C // H
        scale = hd ** (-0.5)
        q = (x @ q_w + q_b).reshape(B, N, H, hd).transpose(0, 2, 1, 3)
        kv = (cond @ kv_w + kv_b).reshape(B, condN, 2, H, hd)
        k = kv[:, :, 0].transpose(0, 2, 1, 3)
        v = kv[:, :, 1].transpose(0, 2, 1, 3)
        attn = jnp.einsum('bhnd,bhmd->bhnm', q * scale, k)
        attn = jax.nn.softmax(attn, axis=-1)
        out = jnp.einsum('bhnm,bhmd->bhnd', attn, v)
        out = out.transpose(0, 2, 1, 3).reshape(B, N, C)
        return out @ proj_w + proj_b

    def _L0_ffn_ref(x, gamma, beta, Wg, bg, W1, b1, W2, b2):
        import jax, jax.numpy as jnp
        import numpy as np
        D = 128
        E = 8
        K = 2
        DF = 512
        B, S = (2, 256)
        EPS_LN = 1e-05
        EPS_TOPK = 1e-08

        def _xavier(key, shape, fan_in, fan_out, dtype=jnp.float32):
            bound = float(np.sqrt(6.0 / (fan_in + fan_out)))
            return jax.random.uniform(key, shape, dtype, -bound, bound)
        b, s, d = x.shape
        mu = jnp.mean(x, axis=-1, keepdims=True)
        var = jnp.mean((x - mu) ** 2, axis=-1, keepdims=True)
        xn = (x - mu) / jnp.sqrt(var + EPS_LN) * gamma + beta
        xf = xn.reshape(-1, d)
        logits = xf @ Wg.T + bg
        probs = jax.nn.softmax(logits, axis=-1)
        tp, ti = jax.lax.top_k(probs, K)
        tp = tp / (jnp.sum(tp, axis=-1, keepdims=True) + EPS_TOPK)
        w = jnp.sum(jax.nn.one_hot(ti, E, dtype=xf.dtype) * tp[..., None], axis=1)
        h = jax.nn.gelu(jnp.einsum('td,efd->tef', xf, W1) + b1, approximate=False)
        y = jnp.einsum('tef,edf->ted', h, W2) + b2
        out = jnp.einsum('ted,te->td', y, w)
        return x + out.reshape(b, s, d)

    def _L1_xattn_ref(x, context, Wq, Wk, Wv, Wo, bo):
        import jax, jax.numpy as jnp
        import numpy as np
        HEADS = 16
        DIM_HEAD = 64
        SCALE = DIM_HEAD ** (-0.5)
        B, Nq, _ = x.shape
        Nc = context.shape[1]
        q = (x @ Wq).reshape(B, Nq, HEADS, DIM_HEAD).transpose(0, 2, 1, 3)
        k = (context @ Wk).reshape(B, Nc, HEADS, DIM_HEAD).transpose(0, 2, 1, 3)
        v = (context @ Wv).reshape(B, Nc, HEADS, DIM_HEAD).transpose(0, 2, 1, 3)
        sim = jnp.einsum('bhid,bhjd->bhij', q, k) * SCALE
        attn = jax.nn.softmax(sim, axis=-1)
        out = jnp.einsum('bhij,bhjd->bhid', attn, v)
        out = out.transpose(0, 2, 1, 3).reshape(B, Nq, HEADS * DIM_HEAD)
        return out @ Wo + bo

    def _L1_ffn_ref(x, Wg, W1, b1, W2, b2, ln_hid_w, ln_hid_b, ln_out_w, ln_out_b):
        import math
        import jax, jax.numpy as jnp
        import numpy as np
        E = 24

        def layer_norm(x, w, b, eps=1e-06):
            m = x.mean(-1, keepdims=True)
            v = x.var(-1, keepdims=True)
            return (x - m) / jnp.sqrt(v + eps) * w + b

        def top2_dispatch(x, Wg, C):
            logits = x @ Wg
            gates = jax.nn.softmax(logits, axis=-1)
            idx1 = jnp.argmax(gates, axis=-1)
            m1 = jax.nn.one_hot(idx1, E, dtype=x.dtype)
            masked = jnp.where(m1 > 0, -jnp.inf, logits)
            idx2 = jnp.argmax(masked, axis=-1)
            m2 = jax.nn.one_hot(idx2, E, dtype=x.dtype)
            loc1 = jnp.cumsum(m1, axis=0) - m1
            loc2 = jnp.cumsum(m2, axis=0) - m2 + jnp.sum(m1, axis=0, keepdims=True)
            m1 = m1 * (loc1 < C)
            m2 = m2 * (loc2 < C)
            g1 = jnp.sum(gates * m1, axis=-1)
            g2 = jnp.sum(gates * m2, axis=-1)
            denom = jnp.maximum(g1 + g2, 1e-09)
            g1, g2 = (g1 / denom, g2 / denom)
            p1 = jnp.sum(loc1 * m1, axis=-1).astype(jnp.int32)
            p2 = jnp.sum(loc2 * m2, axis=-1).astype(jnp.int32)
            c1 = g1[:, None, None] * m1[:, :, None] * jax.nn.one_hot(p1, C, dtype=x.dtype)[:, None, :]
            c2 = g2[:, None, None] * m2[:, :, None] * jax.nn.one_hot(p2, C, dtype=x.dtype)[:, None, :]
            combine = c1 + c2
            dispatch = (combine > 0).astype(x.dtype)
            return (combine, dispatch)

        def moe_apply(x, combine, dispatch, W, b):
            disp = jnp.einsum('sec,sd->ecd', dispatch, x)
            h = jnp.einsum('ecd,edf->ecf', disp, W) + b[:, None, :]
            return jnp.einsum('sec,ecf->sf', combine, h)
        bsz, seq, d = x.shape
        H = 4
        n = seq // H
        S = bsz * n
        C = math.ceil(2 * S / E)
        xg = x.reshape(bsz, H, n, d).transpose(1, 0, 2, 3).reshape(H, S, d)

        def per_group(xf, lw, lb):
            combine, dispatch = top2_dispatch(xf, Wg, C)
            h = moe_apply(xf, combine, dispatch, W1, b1)
            h = layer_norm(h, lw, lb)
            h = jax.nn.relu(h)
            return moe_apply(h, combine, dispatch, W2, b2)
        out = jax.vmap(per_group)(xg, ln_hid_w, ln_hid_b)
        out = out.reshape(H, bsz, n, d).transpose(1, 0, 2, 3).reshape(bsz, seq, d)
        return layer_norm(out + x, ln_out_w, ln_out_b)

    def _L2_xattn_ref(x, latents, mask, ln_x_g, ln_x_b, ln_l_g, ln_l_b, qn_g, kn_g, Wq, Wkv, Wlkv, Wo, bo):
        import jax, jax.numpy as jnp
        import numpy as np
        DIM_IN, DIM_LAT, DIM_HEAD = (96, 128, 64)
        INNER = max(DIM_LAT, DIM_IN)
        HEADS = INNER // DIM_HEAD
        SCALE = DIM_HEAD ** (-0.5)
        RMS_EPS = 1e-08
        LN_EPS = 1e-05

        def layernorm(x, g, b):
            mu = jnp.mean(x, axis=-1, keepdims=True)
            var = jnp.mean((x - mu) ** 2, axis=-1, keepdims=True)
            return (x - mu) * jax.lax.rsqrt(var + LN_EPS) * g + b

        def rmsnorm(x, gamma):
            norm = jnp.sqrt(jnp.sum(x * x, axis=-1, keepdims=True)) * x.shape[-1] ** (-0.5)
            return x / jnp.maximum(norm, RMS_EPS) * gamma
        b, n, _ = x.shape
        m = latents.shape[1]
        xn = layernorm(x, ln_x_g, ln_x_b)
        ln = layernorm(latents, ln_l_g, ln_l_b)
        q = ln @ Wq.T
        kv = jnp.concatenate([xn @ Wkv.T, ln @ Wlkv.T], axis=1)
        k, v = (kv[..., :INNER], kv[..., INNER:])
        split_heads = lambda t: t.reshape(t.shape[0], t.shape[1], HEADS, DIM_HEAD).transpose(0, 2, 1, 3)
        q, k, v = (split_heads(q), split_heads(k), split_heads(v))
        qn = rmsnorm(q, qn_g) * SCALE
        kn = rmsnorm(k, kn_g)
        attn = jnp.einsum('bhid,bhjd->bhij', qn, kn)
        full_mask = jnp.pad(mask, ((0, 0), (0, m)), constant_values=True)
        attn = jnp.where(full_mask[:, None, None, :], attn, -jnp.finfo(attn.dtype).max)
        attn = jax.nn.softmax(attn, axis=-1)
        out = jnp.einsum('bhij,bhjd->bhid', attn, v)
        out = out.transpose(0, 2, 1, 3).reshape(b, m, INNER)
        return out @ Wo.T + bo

    def _L2_ffn_ref(x, router_w, w1, w2):
        import jax, jax.numpy as jnp
        import numpy as np
        B, T, D, FF, E, TOP_K = (4, 256, 128, 512, 8, 2)
        b, t, d = x.shape
        e, k = (router_w.shape[0], TOP_K)
        xf = x.reshape(-1, d)
        n = xf.shape[0]
        logits = xf @ router_w.T
        topv, topi = jax.lax.top_k(logits, k)
        topw = jax.nn.softmax(topv.astype(jnp.float32), axis=-1).astype(x.dtype)
        idx_flat = topi.reshape(-1)
        w_flat = topw.reshape(-1)
        sort_idx = jnp.argsort(idx_flat)
        src = jnp.repeat(jnp.arange(n), k)
        rev = src[sort_idx]
        sw = w_flat[sort_idx]
        perm = xf[rev]
        chunks = perm.reshape(e, n * k // e, d)
        h = jax.nn.gelu(jnp.einsum('ecd,edf->ecf', chunks, w1), approximate=False)
        y = jnp.einsum('ecf,efd->ecd', h, w2).reshape(n * k, d)
        y = y * sw[:, None]
        out = jnp.zeros((n, d), dtype=x.dtype).at[rev].add(y)
        return out.reshape(b, t, d)

    def _L3_xattn_ref(x, context, Wq, Wk, Wv, Wo, bo):
        import jax, jax.numpy as jnp
        import numpy as np
        QUERY_DIM = 128
        CONTEXT_DIM = 96
        HEADS = 8
        DIM_HEAD = 64
        INNER = HEADS * DIM_HEAD
        B, S, _ = x.shape
        L = context.shape[1]
        scale = DIM_HEAD ** (-0.5)
        q = (x @ Wq).reshape(B, S, HEADS, DIM_HEAD).transpose(0, 2, 1, 3)
        k = (context @ Wk).reshape(B, L, HEADS, DIM_HEAD).transpose(0, 2, 1, 3)
        v = (context @ Wv).reshape(B, L, HEADS, DIM_HEAD).transpose(0, 2, 1, 3)
        attn = jnp.einsum('bhsd,bhld->bhsl', q, k) * scale
        attn = jax.nn.softmax(attn, axis=-1)
        out = jnp.einsum('bhsl,bhld->bhsd', attn, v)
        out = out.transpose(0, 2, 1, 3).reshape(B, S, INNER)
        return out @ Wo + bo

    def _L3_ffn_ref(src, Wq, bq, Wk, bk, Wv, bv, Wo, bo, gW, gb, W1, b1, W2, b2, ln1_g, ln1_b, ln2_g, ln2_b):
        import jax, jax.numpy as jnp
        import numpy as np
        D_MODEL = 128
        NHEAD = 16
        HEAD_DIM = D_MODEL // NHEAD
        FF = 256
        NUM_EXPERTS = 8
        EPS = 1e-05

        def _ln(x, g, b):
            m = x.mean(-1, keepdims=True)
            v = ((x - m) ** 2).mean(-1, keepdims=True)
            return (x - m) / jnp.sqrt(v + EPS) * g + b

        def _attention(src, Wq, bq, Wk, bk, Wv, bv, Wo, bo):
            B, T, d = src.shape
            scale = HEAD_DIM ** (-0.5)
            q = (src @ Wq + bq).reshape(B, T, NHEAD, HEAD_DIM)
            k = (src @ Wk + bk).reshape(B, T, NHEAD, HEAD_DIM)
            v = (src @ Wv + bv).reshape(B, T, NHEAD, HEAD_DIM)
            scores = jnp.einsum('bqhd,bkhd->bhqk', q, k) * scale
            probs = jax.nn.softmax(scores, axis=-1)
            out = jnp.einsum('bhqk,bkhd->bqhd', probs, v).reshape(B, T, d)
            return out @ Wo + bo

        def _moe(x, gW, gb, W1, b1, W2, b2):
            B, T, d = x.shape
            xf = x.reshape(-1, d)
            gates = jax.nn.softmax(xf @ gW + gb, axis=-1)
            top2_scores, top2_idx = jax.lax.top_k(gates, 2)
            w = (jax.nn.one_hot(top2_idx, NUM_EXPERTS, dtype=xf.dtype) * top2_scores[..., None]).sum(1)
            h = jax.nn.relu(jnp.einsum('nd,edf->enf', xf, W1) + b1[:, None, :])
            y = jnp.einsum('enf,efd->end', h, W2) + b2[:, None, :]
            out = jnp.einsum('ne,end->nd', w, y)
            return out.reshape(B, T, d)
        attn_out = _attention(src, Wq, bq, Wk, bk, Wv, bv, Wo, bo)
        x = _ln(src + attn_out, ln1_g, ln1_b)
        ff = _moe(x, gW, gb, W1, b1, W2, b2)
        return _ln(x + ff, ln2_g, ln2_b)
    x = x + _L0_xattn_ref(_layernorm(x, axis=-1), ctx_768, L0_xattn_q_w, L0_xattn_q_b, L0_xattn_kv_w, L0_xattn_kv_b, L0_xattn_proj_w, L0_xattn_proj_b)
    x = x + _L0_ffn_ref(_layernorm(x, axis=-1), L0_ffn_gamma, L0_ffn_beta, L0_ffn_Wg, L0_ffn_bg, L0_ffn_W1, L0_ffn_b1, L0_ffn_W2, L0_ffn_b2)
    x = x + _L1_xattn_ref(_layernorm(x, axis=-1), ctx_768, L1_xattn_Wq, L1_xattn_Wk, L1_xattn_Wv, L1_xattn_Wo, L1_xattn_bo)
    x = x + _L1_ffn_ref(_layernorm(x, axis=-1), L1_ffn_Wg, L1_ffn_W1, L1_ffn_b1, L1_ffn_W2, L1_ffn_b2, L1_ffn_ln_hid_w, L1_ffn_ln_hid_b, L1_ffn_ln_out_w, L1_ffn_ln_out_b)
    x = x + _L2_xattn_ref(ctx_768, _layernorm(x, axis=-1), mask_BxS2_bk0, L2_xattn_ln_x_g, L2_xattn_ln_x_b, L2_xattn_ln_l_g, L2_xattn_ln_l_b, L2_xattn_qn_g, L2_xattn_kn_g, L2_xattn_Wq, L2_xattn_Wkv, L2_xattn_Wlkv, L2_xattn_Wo, L2_xattn_bo)
    x = x + _L2_ffn_ref(_layernorm(x, axis=-1), L2_ffn_router_w, L2_ffn_w1, L2_ffn_w2)
    x = x + _L3_xattn_ref(_layernorm(x, axis=-1), ctx_768, L3_xattn_Wq, L3_xattn_Wk, L3_xattn_Wv, L3_xattn_Wo, L3_xattn_bo)
    x = x + _L3_ffn_ref(_layernorm(x, axis=-1), L3_ffn_Wq, L3_ffn_bq, L3_ffn_Wk, L3_ffn_bk, L3_ffn_Wv, L3_ffn_bv, L3_ffn_Wo, L3_ffn_bo, L3_ffn_gW, L3_ffn_gb, L3_ffn_W1, L3_ffn_b1, L3_ffn_W2, L3_ffn_b2, L3_ffn_ln1_g, L3_ffn_ln1_b, L3_ffn_ln2_g, L3_ffn_ln2_b)
    return x

_drawn_inputs = setup_inputs


def setup_inputs(seed=0):
    import zlib

    import numpy as np

    out = dict(_drawn_inputs(seed))
    spreads = {'L0_xattn_q_b': (0.0, 0.1),
     'L0_xattn_kv_b': (0.0, 0.1),
     'L0_xattn_proj_b': (0.0, 0.1),
     'L0_ffn_gamma': (1.0, 0.2),
     'L0_ffn_beta': (0.0, 0.1),
     'L0_ffn_bg': (0.0, 0.1),
     'L0_ffn_b1': (0.0, 0.1),
     'L0_ffn_b2': (0.0, 0.1),
     'L1_xattn_bo': (0.0, 0.1),
     'L1_ffn_b1': (0.0, 0.1),
     'L1_ffn_b2': (0.0, 0.1),
     'L1_ffn_ln_hid_w': (1.0, 0.6),
     'L1_ffn_ln_hid_b': (0.0, 0.444),
     'L1_ffn_ln_out_w': (1.0, 0.2),
     'L1_ffn_ln_out_b': (0.0, 0.1),
     'L2_xattn_ln_x_g': (1.0, 0.6),
     'L2_xattn_ln_x_b': (0.0, 0.464),
     'L2_xattn_ln_l_g': (1.0, 0.2),
     'L2_xattn_ln_l_b': (0.0, 0.1),
     'L2_xattn_qn_g': (1.0, 0.6),
     'L2_xattn_kn_g': (1.0, 0.6),
     'L2_xattn_bo': (0.0, 0.1),
     'L3_ffn_bq': (0.0, 0.8),
     'L3_ffn_bk': (0.0, 0.8),
     'L3_ffn_bv': (0.0, 0.8),
     'L3_ffn_bo': (0.0, 0.314),
     'L3_ffn_gb': (0.0, 0.8),
     'L3_ffn_b1': (0.0, 0.8),
     'L3_ffn_b2': (0.0, 0.8),
     'L3_ffn_ln1_g': (1.0, 0.2),
     'L3_ffn_ln1_b': (0.0, 0.322),
     'L3_ffn_ln2_g': (1.0, 0.2),
     'L3_ffn_ln2_b': (0.0, 0.349)}
    factors = {'L3_xattn_bo': 8.0,
     'L3_ffn_Wq': 8.0,
     'L3_ffn_Wk': 8.0,
     'L3_ffn_Wv': 8.0,
     'L3_ffn_Wo': 6.726,
     'L3_ffn_gW': 8.0,
     'L3_ffn_W1': 8.0,
     'L3_ffn_W2': 8.0}
    for name, (base, spread) in spreads.items():
        noise = np.random.default_rng([zlib.crc32(name.encode()), seed]).standard_normal(out[name].shape)
        drawn = base * np.exp(spread * noise) if base else spread * noise
        out[name] = jnp.asarray(drawn.astype(out[name].dtype))
    for name, factor in factors.items():
        out[name] = (out[name] * factor).astype(out[name].dtype)
    return out
```

```python
from contextlib import ExitStack

import numpy as np

import concourse.bass as bass
from concourse import mybir

F32 = mybir.dt.float32
BF16 = mybir.dt.bfloat16
U8 = mybir.dt.uint8
U32 = mybir.dt.uint32
I32 = mybir.dt.int32
ALU = mybir.AluOpType
ACT = mybir.ActivationFunctionType
AX_X = mybir.AxisListType.X

P = 128
NBATCH = 32
NTURN = NBATCH // 4
NKEY = 77
CTX = 96
EPS = 1e-5


class Link:

    def __init__(self, eng, sem, turn, length):
        self.eng, self.sem, self.turn, self.length, self.count = eng, sem, turn, length, 0

    def __call__(self, instruction):
        self.count += 1
        instruction.then_inc(self.sem, 1)
        self.eng.wait_ge(self.sem, self.turn * self.length + self.count)

    def end(self):
        assert self.count == self.length, (self.count, self.length)


class Net:

    def __init__(self, nc, ctx):
        self.nc, self.ctx = nc, ctx
        self.semaphores = []

    def sb(self, name, shape, dt=F32):
        return self.ctx.enter_context(self.nc.sbuf_tensor(name, shape, dt))

    def sem(self, name):
        self.semaphores.append(self.nc.alloc_semaphore(name))
        return self.semaphores[-1]

    def release_semaphores(self):
        self.nc.all_engine_barrier()
        self.nc.clear_and_free_semaphores(self.semaphores)
        self.nc.all_engine_barrier()
        self.semaphores = []


def attention_stage(nc, net, spec, w):
    name, heads, hd, kind, biased = (spec[k] for k in ("name", "heads", "hd", "kind", "biased"))
    scale = float(hd) ** -0.5
    inner = heads * hd
    NC = inner // P
    KEYS = {"cross": [NKEY], "self": [P], "latent": [NKEY, P]}[kind]
    NK = sum(KEYS)
    OFF = [0, NKEY][: len(KEYS)]
    U = min(4, heads)
    NU = heads // U
    NP = (NC + 3) // 4
    SLOTS = [(i, e) for i in range(U) for e in range(len(KEYS))]

    with ExitStack() as ctx:
        def sb(n, shape, dt=F32):
            return ctx.enter_context(nc.sbuf_tensor(f"{name}_{n}", shape, dt))

        def sem(n):
            return net.sem(f"{name}_{n}")

        x = net.x
        dst = net.x1 if kind == "self" else net.x
        ident, ones_row = net.ident, net.ones_row
        score_bank, turn_bank, out_bank, proj_bank = net.banks[0:3], net.banks[3:5], net.banks[5:7], net.banks[7]

        KD = P if kind == "self" else CTX
        wo = sb("wo", [P, NC, P]); bo = sb("bo", [1, P])
        loads = [(wo[:, :, :], w["wo"]), (bo[:, :], w["bo"])]
        if kind != "latent":
            wq = sb("wq", [P, inner]); wk = sb("wk", [KD, inner]); wv = sb("wv", [KD, inner])
            loads = [(wq[:, :], w["wq"]), (wk[:, :], w["wk"]), (wv[:, :], w["wv"])] + loads
        if biased:
            bq = sb("bq", [P, 1]); bk = sb("bk", [P, 1]); bv = sb("bv", [1, P])
            loads += [(bq[:, :], w["bq"]), (bk[:, :], w["bk"]), (bv[:, :], w["bv"])]
        if hd == 8:
            diag = sb("diag", [P, 4]); loads.append((diag[:, :], w["diag"]))

        if kind == "latent":
            wqkv_lat = sb("wqkv_lat", [P, 3 * P]); wkv_ctx = sb("wkv_ctx", [CTX, 2 * P])
            gamma = sb("gamma", [P, 4, 64]); lat_g = sb("lat_g", [P, 1]); lat_b = sb("lat_b", [P, 1])
            ctx_g = sb("ctx_g", [CTX, 1]); ctx_b = sb("ctx_b", [CTX, 1])
            ctx_tok = sb("ctx_tok", [NKEY, NBATCH, CTX])
            mask8 = sb("mask8", [1, NBATCH * NKEY], U8); mask_row = sb("mask_row", [1, NBATCH, 2, NK])
            loads += [(wqkv_lat[:, 0:P], w["wq"]), (wqkv_lat[:, P:3 * P], w["wlkv"]),
                      (wkv_ctx[:, :], w["wkv"]), (gamma[:, :, :], w["gamma"]), (lat_g[:, :], w["lat_g"]),
                      (lat_b[:, :], w["lat_b"]), (ctx_g[:, :], w["ctx_g"]), (ctx_b[:, :], w["ctx_b"]),
                      (ctx_tok[:, :, :], w["ctx_tok"]), (mask8[:, :], w["mask"])]

        stats = sb("stats", [P, 4, 6]); mean_var = sb("mean_var", [P, 4, 2]); rstd = sb("rstd", [P, 4])
        idle = sb("idle", [P, 1])
        xn = sb("xn", [P, 4, P]); xT = sb("xT", [P, 4 * P])
        qT = sb("qT", [P, NC, 4 * P])
        ctxg = sb("ctxg", [CTX, 4, NKEY])
        if hd == 8:
            kbd = sb("kbd", [P, 4, 4, NK])
            vals = [sb("vals", [KEYS[0], 4, heads, 32])]
        else:
            kbd = sb("kbd", [P, NC, 4, 2, NK])
            if kind == "latent":
                raw_lat = sb("raw_lat", [P, 4, 3 * P]); raw_ctx = sb("raw_ctx", [NKEY, 4, 2 * P])
                vals = [raw_ctx[:, :, P:2 * P], raw_lat[:, :, 2 * P:3 * P]]
                sq_lat = sb("sq_lat", [P, 4, 2 * P]); sq_ctx = sb("sq_ctx", [NKEY, 4, P])
                xn2 = sb("xn2", [P, 4, P]); cn = sb("cn", [NKEY, 4, CTX]); cT = sb("cT", [CTX, 4, NKEY])
                stats_ctx = sb("stats_ctx", [NKEY, 4, 6]); mv_ctx = sb("mv_ctx", [NKEY, 4, 2])
                rstd_ctx = sb("rstd_ctx", [NKEY, 4])
                rms_lat = sb("rms_lat", [P, 16]); rms_ctx = sb("rms_ctx", [NKEY, 8])
                qk_tok = sb("qk_tok", [P, 4, 4, 64]); kc_tok = sb("kc_tok", [NKEY, 4, 2, 64])
            else:
                vals = [sb("vals", [KEYS[0], 4, inner])]
        NB = 3
        soft = [sb(f"soft{i}", [P, heads, NK]) for i in range(NB)]
        mx = [sb(f"mx{i}", [P, U]) for i in range(2)]
        rsum = [sb(f"rsum{i}", [P, heads]) for i in range(2)]
        rinv = [sb(f"rinv{i}", [P, heads]) for i in range(2)]
        probsT = [sb(f"probsT{i}", [P, 4, P]) for i in range(2)]
        attnT = sb("attnT", [P, NC, P])

        loaded, constants, dve_chain = sem("loaded"), sem("constants"), sem("dve_chain")
        var_ready, rstd_ready, normed = sem("var_ready"), sem("rstd_ready"), sem("normed")
        xT_ps, xT_ready, ctx_ready = sem("xT_ps"), sem("xT_ready"), sem("ctx_ready")
        a_ps, a_done = sem("a_ps"), sem("a_done")
        d_ps, d_done = sem("d_ps"), sem("d_done")
        scores_ready, max_ready, shifted = sem("scores_ready"), sem("max_ready"), sem("shifted")
        exp_done, sum_ready, inv_ready, probs_ready = sem("exp_done"), sem("sum_ready"), sem("inv_ready"), sem("probs_ready")
        turned, turned_out, values_done = sem("turned"), sem("turned_out"), sem("values_done")
        attnT_ready, proj_done, added = sem("attnT_ready"), sem("proj_done"), sem("added")
        var2_ready, rstd2_ready = sem("var2_ready"), sem("rstd2_ready")
        mask_zero = sem("mask_zero")
        qkv_ps, qkv_out, squared = sem("qkv_ps"), sem("qkv_out"), sem("squared")
        ss_ready, rms_ready, qk_ready, qkT_ps = sem("ss_ready"), sem("rms_ready"), sem("qk_ready"), sem("qkT_ps")

        if inner == P:
            vjobs = [([0, 1, 2, 3], 0, P)]
        else:
            vjobs = [([b], c, 512) for b in range(4) for c in range(0, inner, 512)]
        NA, ND = NC + len(vjobs), NC
        TU = 4 * NU

        def shift(dve, it, b):
            for u in range(NU):
                n = b * NU + u
                ps = score_bank[n % 3][:, 0:U * NK].rearrange("p (h k) -> p h k", h=U)
                dve.wait_ge(scores_ready, it * TU + n + 1)
                if n >= 2:
                    dve.wait_ge(shifted, it * TU + n - 1)
                dve.tensor_reduce(mx[n % 2][:, :], ps, AX_X, ALU.max).then_inc(max_ready, 1)
                dve.wait_ge(max_ready, it * TU + n + 1)
                if u == 0 and b >= NB:
                    dve.wait_ge(turned, it * TU + (b - NB + 1) * NU)
                dve.tensor_tensor(soft[b % NB][:, u * U:(u + 1) * U, :], ps,
                                  mx[n % 2][:, :].unsqueeze(2).to_broadcast([P, U, NK]),
                                  ALU.subtract).then_inc(shifted, 1)

        def row_sums(dve, it, b):
            g = it * 4 + b
            dve.wait_ge(exp_done, g + 1)
            if b >= 2:
                dve.wait_ge(probs_ready, g - 1)
            dve.tensor_reduce(rsum[b % 2][:, :], soft[b % NB][:, :, :], AX_X, ALU.add).then_inc(sum_ready, 1)
            dve.wait_ge(sum_ready, g + 1)
            dve.reciprocal(rinv[b % 2][:, :], rsum[b % 2][:, :]).then_inc(inv_ready, 1)

        def latent_dve(dve, it):
            link = Link(dve, dve_chain, it, 8)
            for b in range(4):
                dve.bn_stats(stats[:, b, :], x[:, it * 4 + b, :])
                last = dve.bn_stats(stats_ctx[:, b, :], ctx_tok[:, it * 4 + b, :])
            link(last)
            dve.memset(idle[:, :], 0.0)
            for b in range(4):
                dve.bn_aggr(mean_var[:, b, :], stats[:, b, :])
                last = dve.bn_aggr(mv_ctx[:, b, :], stats_ctx[:, b, :])
            link(last)
            dve.tensor_scalar(rstd[:, :], mean_var[:, :, 1], EPS, None, ALU.add)
            dve.tensor_scalar(rstd_ctx[:, :], mv_ctx[:, :, 1], EPS, None, ALU.add).then_inc(var_ready, 1)
            dve.wait_ge(rstd_ready, it + 1)
            for b in range(4):
                dve.tensor_scalar(cn[:, b, :], ctx_tok[:, it * 4 + b, :], mv_ctx[:, b, 0:1],
                                  rstd_ctx[:, b:b + 1], ALU.subtract, ALU.mult)
            for b in range(4):
                last = dve.tensor_scalar(xn[:, b, :], x[:, it * 4 + b, :], mean_var[:, b, 0:1],
                                         rstd[:, b:b + 1], ALU.subtract, ALU.mult)
            link(last)
            for b in range(4):
                last = dve.bn_stats(stats[:, b, :], xn[:, b, :])
            link(last)
            dve.memset(idle[:, :], 0.0)
            for b in range(4):
                last = dve.bn_aggr(mean_var[:, b, :], stats[:, b, :])
            link(last)
            dve.tensor_scalar(rstd[:, :], mean_var[:, :, 1], EPS, None, ALU.add).then_inc(var2_ready, 1)
            dve.wait_ge(rstd2_ready, it + 1)
            for b in range(4):
                last = dve.tensor_scalar(xn2[:, b, :], xn[:, b, :], mean_var[:, b, 0:1],
                                         rstd[:, b:b + 1], ALU.subtract, ALU.mult)
            last.then_inc(normed, 1)
            dve.wait_ge(squared, it + 1)
            dve.tensor_reduce(rms_lat[:, :], sq_lat[:, :, :].rearrange("p b (g d) -> p (b g) d", d=64), AX_X, ALU.add)
            dve.tensor_reduce(rms_ctx[:, :], sq_ctx[:, :, :].rearrange("p b (g d) -> p (b g) d", d=64),
                              AX_X, ALU.add).then_inc(ss_ready, 1)
            dve.wait_ge(rms_ready, it + 1)
            dve.tensor_scalar(rms_lat[:, :], rms_lat[:, :], 0.125, 1e-8, ALU.mult, ALU.max)
            link(dve.tensor_scalar(rms_ctx[:, :], rms_ctx[:, :], 0.125, 1e-8, ALU.mult, ALU.max))
            dve.reciprocal(rms_lat[:, :], rms_lat[:, :])
            link(dve.reciprocal(rms_ctx[:, :], rms_ctx[:, :]))
            dve.tensor_tensor(qk_tok[:, :, :, :], raw_lat[:, :, 0:2 * P].rearrange("p b (g d) -> p b g d", d=64),
                              rms_lat[:, :].rearrange("p (b g) -> p b g", b=4).unsqueeze(3).to_broadcast([P, 4, 4, 64]),
                              ALU.mult)
            link(dve.tensor_tensor(kc_tok[:, :, :, :], raw_ctx[:, :, 0:P].rearrange("p b (g d) -> p b g d", d=64),
                                   rms_ctx[:, :].rearrange("p (b g) -> p b g", b=4).unsqueeze(3).to_broadcast([NKEY, 4, 2, 64]),
                                   ALU.mult))
            dve.tensor_tensor(qk_tok[:, :, :, :], qk_tok[:, :, :, :],
                              gamma[:, :, :].unsqueeze(1).to_broadcast([P, 4, 4, 64]), ALU.mult)
            dve.tensor_tensor(kc_tok[:, :, :, :], kc_tok[:, :, :, :],
                              gamma[0:NKEY, 2:4, :].unsqueeze(1).to_broadcast([NKEY, 4, 2, 64]),
                              ALU.mult).then_inc(qk_ready, 1)
            link.end()
            dve.wait_ge(qkT_ps, it + 1)
            lat = score_bank[0][:, :].rearrange("p (b t) -> p b t", b=4)
            con = score_bank[1][:, 0:4 * NKEY].rearrange("p (b t) -> p b t", b=4)
            for i in range(2):
                dve.tensor_copy(kbd[64 * i:64 * i + 64, 0, :, i, NKEY:NK], lat[64 * i:64 * i + 64, :, :])
                last = dve.tensor_copy(kbd[64 * i:64 * i + 64, 0, :, i, 0:NKEY], con[64 * i:64 * i + 64, :, :])
            last.then_inc(d_done, 1)

        def latent_act(act, it):
            act.wait_ge(xT_ps, it + 1)
            act.activation(xT[:, :], out_bank[0][:, :], ACT.Identity, scale=lat_g[:, 0:1], bias=lat_b[:, 0:1])
            act.activation(cT[:, :, :], out_bank[1][0:CTX, 0:4 * NKEY].rearrange("p (b t) -> p b t", b=4),
                           ACT.Identity, scale=ctx_g[:, 0:1], bias=ctx_b[:, 0:1]).then_inc(xT_ready, 1)
            for b in range(4):
                act.wait_ge(qkv_ps, it * 6 + b + 1)
                last = act.copy(raw_lat[:, b, :], [*score_bank, turn_bank[0]][b][:, 0:3 * P])
            for i in range(2):
                act.wait_ge(qkv_ps, it * 6 + 5 + i)
                last = act.copy(raw_ctx[:, 2 * i:2 * i + 2, :],
                                [turn_bank[1], proj_bank][i][0:NKEY, :].rearrange("p (b f) -> p b f", b=2))
            last.then_inc(qkv_out, 1)
            act.wait_ge(qkv_out, it + 1)
            act.activation(sq_lat[:, :, :], raw_lat[:, :, 0:2 * P], ACT.Square)
            act.activation(sq_ctx[:, :, :], raw_ctx[:, :, 0:P], ACT.Square).then_inc(squared, 1)
            act.wait_ge(qkT_ps, it + 1)
            act.copy(qT[:, 0, :], turn_bank[0][:, :]).then_inc(a_done, 1)

        def latent_pe(pe, it):
            pe.wait_ge(normed, it + 1)
            for b in range(4):
                pe.transpose(out_bank[1][0:CTX, b * NKEY:(b + 1) * NKEY], cn[:, b, :], ident[0:NKEY, 0:NKEY])
            for b in range(4):
                last = pe.transpose(out_bank[0][:, b * P:(b + 1) * P], xn2[:, b, :], ident[:, :])
            last.then_inc(xT_ps, 1)
            pe.wait_ge(xT_ready, it + 1)
            pe.wait_ge(added, it * 4)
            for b in range(4):
                pe.matmul([*score_bank, turn_bank[0]][b][:, 0:3 * P], xT[:, b * P:(b + 1) * P], wqkv_lat[:, :],
                          start=True, stop=True).then_inc(qkv_ps, 1)
            for b in range(4):
                last = pe.matmul([turn_bank[1], proj_bank][b // 2][0:NKEY, b % 2 * 2 * P:(b % 2 + 1) * 2 * P],
                                 cT[:, b, :], wkv_ctx[:, :], start=True, stop=True)
                if b % 2:
                    last.then_inc(qkv_ps, 1)
            pe.wait_ge(qk_ready, it + 1)
            for b in range(4):
                pe.transpose(turn_bank[0][:, b * P:(b + 1) * P],
                             qk_tok[:, b, 0:2, :].rearrange("p g d -> p (g d)"), ident[:, :])
                pe.transpose(score_bank[0][:, b * P:(b + 1) * P],
                             qk_tok[:, b, 2:4, :].rearrange("p g d -> p (g d)"), ident[:, :])
                last = pe.transpose(score_bank[1][:, b * NKEY:(b + 1) * NKEY],
                                    kc_tok[:, b, :, :].rearrange("p g d -> p (g d)"), ident[0:NKEY, 0:NKEY])
            last.then_inc(qkT_ps, 1)
            pe.wait_ge(a_done, it + 1)
            pe.wait_ge(d_done, it + 1)

        block = ctx.enter_context(nc.Block())

        @block.sync
        def _(sp):
            for dst_ap, src in loads:
                sp.dma_start(dst_ap, src).then_inc(loaded, 16)

        @block.gpsimd
        def _(pool):
            with pool.Fori(0, NTURN) as it:
                if kind == "cross":
                    pool.wait_ge(a_done, it * NA)
                    pool.tensor_copy(ctxg[:, :, :], net.ctxT[:, bass.ds(it * 4, 4), :]).then_inc(ctx_ready, 1)
                if kind != "latent":
                    pool.wait_ge(var_ready, it + 1)
                    pool.tensor_tensor(rstd[:, :], rstd[:, :], net.minus_half[:, 0:4], ALU.pow).then_inc(rstd_ready, 1)
                if kind == "latent":
                    half = net.minus_half
                    pool.wait_ge(var_ready, it + 1)
                    pool.tensor_tensor(rstd[:, :], rstd[:, :], half[:, 0:4], ALU.pow)
                    pool.tensor_tensor(rstd_ctx[:, :], rstd_ctx[:, :], half[0:NKEY, 0:4], ALU.pow).then_inc(rstd_ready, 1)
                    pool.wait_ge(var2_ready, it + 1)
                    pool.tensor_tensor(rstd[:, :], rstd[:, :], half[:, 0:4], ALU.pow).then_inc(rstd2_ready, 1)
                    pool.wait_ge(ss_ready, it + 1)
                    pool.tensor_tensor(rms_lat[:, :], rms_lat[:, :], net.plus_half[:, 0:16], ALU.pow)
                    pool.tensor_tensor(rms_ctx[:, :], rms_ctx[:, :], net.plus_half[0:NKEY, 0:8], ALU.pow).then_inc(rms_ready, 1)
                for b in range(4):
                    tile = soft[b % NB][:, :, :]
                    pool.wait_ge(inv_ready, it * 4 + b + 1)
                    pool.tensor_tensor(tile, tile, rinv[b % 2][:, :].unsqueeze(2).to_broadcast([P, heads, NK]),
                                       ALU.mult).then_inc(probs_ready, 1)

        @block.vector
        def _(dve):
            dve.wait_ge(loaded, 16 * len(loads))
            if kind == "latent":
                dve.memset(mask_row[:, :, :, :], 0.0).then_inc(mask_zero, 1)
                dve.wait_ge(mask_zero, 1)
                for i in range(2):
                    dve.tensor_scalar(mask_row[:, :, i, 0:NKEY], mask8[:, :].rearrange("p (b t) -> p b t", t=NKEY),
                                      1.0, 1e30, ALU.subtract, ALU.mult)
            if hd == 8:
                dve.memset(vals[0][:, :, :, :], 0.0).then_inc(constants, 1)
            else:
                dve.memset(kbd[0:64, :, :, 1, :], 0.0)
                dve.memset(kbd[64:P, :, :, 0, :], 0.0).then_inc(constants, 1)
            with dve.Fori(0, NTURN) as it:
                if kind != "latent":
                    for b in range(4):
                        last = dve.bn_stats(stats[:, b, :], x[:, it * 4 + b, :])
                    last.then_inc(dve_chain, 1)
                    dve.wait_ge(dve_chain, it * 2 + 1)
                    dve.memset(idle[:, :], 0.0)
                    for b in range(4):
                        last = dve.bn_aggr(mean_var[:, b, :], stats[:, b, :])
                    last.then_inc(dve_chain, 1)
                    dve.wait_ge(dve_chain, it * 2 + 2)
                    dve.tensor_scalar(rstd[:, :], mean_var[:, :, 1], EPS, None, ALU.add).then_inc(var_ready, 1)
                    dve.wait_ge(rstd_ready, it + 1)
                    dve.wait_ge(added, it * 4)
                    for b in range(4):
                        last = dve.tensor_scalar(xn[:, b, :], x[:, it * 4 + b, :], mean_var[:, b, 0:1],
                                                 rstd[:, b:b + 1], ALU.subtract, ALU.mult)
                    last.then_inc(normed, 1)
                if kind == "latent":
                    latent_dve(dve, it)
                else:
                    for c in range(NC):
                        kps = score_bank[c % 2][:, 0:4 * NK].rearrange("p (b k) -> p b k", b=4)
                        dve.wait_ge(d_ps, it * ND + c + 1)
                        if hd == 8:
                            for b in range(4):
                                last = dve.scalar_tensor_tensor(
                                    kbd[:, b, :, :], kps[:, b:b + 1, :].to_broadcast([P, 4, NK]), bk[:, 0:1],
                                    diag[:, :].unsqueeze(2).to_broadcast([P, 4, NK]), ALU.add, ALU.mult)
                        else:
                            dve.tensor_copy(kbd[0:64, c, :, 0, :], kps[0:64, :, :])
                            last = dve.tensor_copy(kbd[64:P, c, :, 1, :], kps[64:P, :, :])
                        last.then_inc(d_done, 1)
                for s in range(7):
                    if s < 4:
                        shift(dve, it, s)
                    if 1 <= s <= 4:
                        row_sums(dve, it, s - 1)
                    if s >= 3:
                        g = it * 4 + s - 3
                        dve.wait_ge(proj_done, g + 1)
                        inp = xn[:, s - 3, :] if kind == "self" else x[:, g, :]
                        dve.tensor_tensor(dst[:, g, :], inp, proj_bank[:, 0:P], ALU.add).then_inc(added, 1)

        @block.scalar
        def _(act):
            act.wait_ge(loaded, 16 * len(loads))
            act.wait_ge(constants, 1)
            with act.Fori(0, NTURN) as it:
                if kind == "latent":
                    latent_act(act, it)
                else:
                    act.wait_ge(xT_ps, it + 1)
                    act.copy(xT[:, :], out_bank[0][:, :]).then_inc(xT_ready, 1)
                    for c in range(NC):
                        act.wait_ge(a_ps, it * NA + c + 1)
                        if biased:
                            act.activation(qT[:, c, :], turn_bank[c % 2][:, :], ACT.Identity,
                                           bias=bq[:, 0:1]).then_inc(a_done, 1)
                        else:
                            act.copy(qT[:, c, :], turn_bank[c % 2][:, :]).then_inc(a_done, 1)
                    for v, (bs, c0, cols) in enumerate(vjobs):
                        bank = turn_bank[(NC + v) % 2][0:KEYS[0], 0:len(bs) * cols]
                        act.wait_ge(a_ps, it * NA + NC + v + 1)
                        if hd == 8:
                            ps = bank.rearrange("p (b r j d) -> p b r j d", b=4, r=4, j=4)
                            out = vals[0][:, :, :, :].rearrange("p b (r j) d -> p b r j d", j=4)
                            for j in range(4):
                                for b in range(4):
                                    last = act.copy(out[:, b, :, j, 8 * j:8 * j + 8], ps[:, b, :, j, :])
                        else:
                            last = act.copy(vals[0][:, bs[0], c0:c0 + cols], bank)
                        last.then_inc(a_done, 1)
                for s in range(1, 6):
                    if s <= 4:
                        tile = soft[(s - 1) % NB][:, :, :].rearrange("p h k -> p (h k)")
                        act.wait_ge(shifted, it * TU + s * NU)
                        act.activation(tile, tile, ACT.Exp, scale=scale).then_inc(exp_done, 1)
                    if s >= 2:
                        b = s - 2
                        for u in range(NU):
                            n = b * NU + u
                            act.wait_ge(turned, it * TU + n + 1)
                            if n >= 2:
                                act.wait_ge(values_done, it * TU + n - 1)
                            ps = turn_bank[n % 2][:, :].rearrange("p (m t) -> p m t", m=4)
                            for e, nk in enumerate(KEYS):
                                last = act.copy(probsT[n % 2][0:nk, e:len(SLOTS):len(KEYS), :],
                                                ps[0:nk, e:len(SLOTS):len(KEYS), :])
                            last.then_inc(turned_out, 1)
                        for p in range(NP):
                            nch = min(4, NC - 4 * p)
                            act.wait_ge(values_done, it * TU + b * NU + (p + 1) * (NU // NP))
                            act.copy(attnT[:, 4 * p:4 * p + nch, :],
                                     out_bank[(b * NP + p) % 2][:, 0:nch * P].rearrange("p (c t) -> p c t", c=nch)
                                     ).then_inc(attnT_ready, 1)

        @block.tensor
        def _(pe):
            pe.wait_ge(loaded, 16 * len(loads))
            pe.wait_ge(constants, 1)

            def prep(it):
                pe.wait_ge(normed, it + 1)
                for b in range(4):
                    last = pe.transpose(out_bank[0][:, b * P:(b + 1) * P], xn[:, b, :], ident[:, :])
                last.then_inc(xT_ps, 1)
                if kind == "self":
                    pe.wait_ge(xT_ready, it + 1)
                for c in range(NC):
                    if c >= 2:
                        pe.wait_ge(d_done, it * ND + c - 1)
                    src = xT[:, :] if kind == "self" else net.ctxT[:, bass.ds(it * 4, 4), :]
                    pe.matmul(score_bank[c % 2][:, 0:4 * NK], wk[:, c * P:(c + 1) * P], src,
                              start=True, stop=True).then_inc(d_ps, 1)
                    if c == 0 and kind == "cross":
                        pe.wait_ge(xT_ready, it + 1)
                    if c >= 2:
                        pe.wait_ge(a_done, it * NA + c - 1)
                    pe.matmul(turn_bank[c % 2][:, :], wq[:, c * P:(c + 1) * P], xT[:, :],
                              start=True, stop=True).then_inc(a_ps, 1)
                if kind == "cross":
                    pe.wait_ge(ctx_ready, it + 1)
                for v, (bs, c0, cols) in enumerate(vjobs):
                    n = NC + v
                    if n >= 2:
                        pe.wait_ge(a_done, it * NA + n - 1)
                    for i, b in enumerate(bs):
                        src = xT[:, b * P:(b + 1) * P] if kind == "self" else ctxg[:, b, :]
                        out = turn_bank[n % 2][0:KEYS[0], i * cols:(i + 1) * cols]
                        last = pe.matmul(out, src, wv[:, c0:c0 + cols], start=True, stop=not biased)
                        if biased:
                            last = pe.matmul(out, ones_row[:, 0:KEYS[0]], bv[:, :], start=False, stop=True)
                    last.then_inc(a_ps, 1)
                pe.wait_ge(d_done, (it + 1) * ND)
                pe.wait_ge(a_done, (it + 1) * NA)

            def scores(it, b):
                for u in range(NU):
                    n = b * NU + u
                    bank = score_bank[n % 3]
                    if n >= 3:
                        pe.wait_ge(shifted, it * TU + n - 2)
                    if hd == 8:
                        last = pe.matmul(bank[:, 0:U * NK], qT[32 * u:32 * u + 32, 0, b * P:(b + 1) * P],
                                         kbd[32 * u:32 * u + 32, b, :, :], start=True, stop=True)
                    else:
                        for c in range(u * U // 2, (u + 1) * U // 2):
                            at = (2 * c - u * U) * NK
                            last = pe.matmul(bank[:, at:at + 2 * NK], qT[:, c, b * P:(b + 1) * P],
                                             kbd[:, c, b, :, :], start=True, stop=kind != "latent")
                            if kind == "latent":
                                last = pe.matmul(bank[:, at:at + 2 * NK], ones_row[:, :],
                                                 mask_row[:, it * 4 + b, :, :], start=False, stop=True)
                    last.then_inc(scores_ready, 1)

            def turn(it, b, u):
                n = b * NU + u
                if u == 0:
                    pe.wait_ge(probs_ready, it * 4 + b + 1)
                if n >= 2:
                    pe.wait_ge(turned_out, it * TU + n - 1)
                for m, (i, e) in enumerate(SLOTS):
                    last = pe.transpose(turn_bank[n % 2][0:KEYS[e], m * P:(m + 1) * P],
                                        soft[b % NB][:, u * U + i, OFF[e]:OFF[e] + KEYS[e]], ident[:, :])
                last.then_inc(turned, 1)

            def values(it, b, u):
                n = b * NU + u
                pe.wait_ge(turned_out, it * TU + n + 1)
                if u % (NU // NP) == 0:
                    pe.wait_ge(attnT_ready, max(b * NP + u // (NU // NP) - 1, 0) + it * 4 * NP)
                for m, (i, e) in enumerate(SLOTS):
                    h, nk = u * U + i, KEYS[e]
                    if hd == 8:
                        last = pe.matmul(out_bank[b % 2][32 * u:32 * u + 32, 0:P], vals[0][:, b, h, :],
                                         probsT[n % 2][0:nk, m, :], start=(i == 0), stop=(i == U - 1))
                    else:
                        c = h // 2
                        out = out_bank[(b * NP + c // 4) % 2][64 * (h % 2):64 * (h % 2) + 64, c % 4 * P:(c % 4 + 1) * P]
                        last = pe.matmul(out, vals[e][:, b, h * 64:(h + 1) * 64], probsT[n % 2][0:nk, m, :],
                                         start=(e == 0), stop=(e == len(KEYS) - 1))
                last.then_inc(values_done, 1)

            def project(it, b):
                g = it * 4 + b
                pe.wait_ge(attnT_ready, (g + 1) * NP)
                pe.wait_ge(added, g)
                pe.matmul(proj_bank[:, 0:P], ones_row[:, :], bo[:, :], start=True, stop=False)
                for c in range(NC):
                    last = pe.matmul(proj_bank[:, 0:P], attnT[:, c, :], wo[:, c, :], start=False, stop=(c == NC - 1))
                last.then_inc(proj_done, 1)

            with pe.Fori(0, NTURN) as it:
                if kind == "latent":
                    latent_pe(pe, it)
                else:
                    prep(it)
                for s in range(7):
                    if s < 4:
                        scores(it, s)
                    if s >= 3:
                        project(it, s - 3)
                    if 2 <= s <= 5:
                        for u in range(NU):
                            turn(it, s - 2, u)
                            if u:
                                values(it, s - 2, u - 1)
                        values(it, s - 2, NU - 1)


def top_two(dve, link, net, logits, n, experts, tiles):
    shape = [P, n, experts]
    index = net.index64[:, 0:experts].unsqueeze(1).to_broadcast(shape)
    left = logits
    for rank in range(2):
        top, hot, least = tiles["top"][rank], tiles["hot"][rank], tiles["least"]
        link(dve.tensor_reduce(top, left, AX_X, ALU.max))
        link(dve.tensor_tensor(hot, left, top.unsqueeze(2).to_broadcast(shape), ALU.is_equal))
        link(dve.tensor_tensor(hot, hot, index, ALU.mult))
        link(dve.tensor_reduce(least, hot, AX_X, ALU.min))
        link(dve.tensor_tensor(hot, index, least.unsqueeze(2).to_broadcast(shape), ALU.is_equal))
        if rank == 0:
            left = tiles["left"]
            link(dve.scalar_tensor_tensor(left, hot, -3e38, logits, ALU.mult, ALU.add))


TOP_TWO_LINKS = 11


def dense_moe_stage(nc, net, spec, w):
    name, FF, kind = spec["name"], spec["FF"], spec["kind"]
    E, FC = 8, FF // P
    func = ACT.Gelu if kind == "pre" else ACT.Relu
    post = kind == "post"
    with ExitStack() as ctx:
        def sb(n, shape, dt=F32):
            return ctx.enter_context(nc.sbuf_tensor(f"{name}_{n}", shape, dt))

        def sem(n):
            return net.sem(f"{name}_{n}")

        x, ident, ones_row = net.x, net.ident, net.ones_row
        src = net.x1 if post else net.x
        hid_bank, y_bank, turn_bank, gate_bank = net.banks[0:4], net.banks[4:6], net.banks[6], net.banks[7]
        w1 = sb("w1", [P, E, FF]); w2 = sb("w2", [P, E, FC, P]); b1 = sb("b1", [P, E * FC]); b2 = sb("b2", [E, P])
        wg = sb("wg", [P, E]); bg = sb("bg", [1, E]); g_col = sb("g_col", [P, 1]); b_col = sb("b_col", [P, 1])
        loads = [(wg[:, :], w["wg"]), (bg[:, :], w["bg"]), (g_col[:, :], w["g_col"]), (b_col[:, :], w["b_col"]),
                 (b1[:, :], w["b1"]), (b2[:, :], w["b2"]), (w1[:, :, :], w["w1"]), (w2[:, :, :, :], w["w2"])]
        if post:
            g1, be1, g2, be2 = (sb(n, [P, P]) for n in ("g1", "be1", "g2", "be2"))
            loads += [(g1[:, :], w["g1"]), (be1[:, :], w["be1"]), (g2[:, :], w["g2"]), (be2[:, :], w["be2"])]
            stats2 = sb("stats2", [P, 4, 6]); mv2 = sb("mv2", [P, 4, 2]); rstd2 = sb("rstd2", [P, 4])
            out_n = sb("out_n", [P, 4, P])
        stats = sb("stats", [P, 4, 6]); mean_var = sb("mean_var", [P, 4, 2]); rstd = sb("rstd", [P, 4])
        idle = sb("idle", [P, 1])
        xn = sb("xn", [P, 4, P]); xn2 = sb("xn2", [P, 4, P]); base = sb("base", [P, 4, P])
        xT = [sb(f"xT{i}", [P, 4 * P]) for i in range(2)]
        gates = [sb(f"gates{i}", [P, 4, E]) for i in range(2)]
        acc = [sb(f"acc{i}", [P, 4, P]) for i in range(2)]
        logits = sb("logits", [P, 4, E]); expd = sb("expd", [P, 4, E]); both = sb("both", [P, 4, E])
        small = {n: sb(n, [P, 4]) for n in ("top0", "top1", "least", "total", "gate0", "gate1", "gap")}
        tiles = dict(top=[small["top0"][:, :], small["top1"][:, :]], least=small["least"][:, :],
                     hot=[sb(f"hot{i}", [P, 4, E])[:, :, :] for i in range(2)], left=sb("left", [P, 4, E])[:, :, :])
        gatesT = sb("gatesT", [E, 4 * P]); hT = [sb(f"hT{i}", [P, FC, 4 * P]) for i in range(2)]

        loaded, chain = sem("loaded"), sem("chain")
        var_ready, rstd_ready, normed = sem("var_ready"), sem("rstd_ready"), sem("normed")
        affine_done = sem("affine_done")
        xT_ps, xT_ready, logits_ps = sem("xT_ps"), sem("xT_ready"), sem("logits_ps")
        less_top, exp_done, gates_ready = sem("less_top"), sem("exp_done"), sem("gates_ready")
        gatesT_ps, gatesT_ready, bias_ps, acc_ready = sem("gatesT_ps"), sem("gatesT_ready"), sem("bias_ps"), sem("acc_ready")
        hid_ready, hid_out, y_ready, y_added = sem("hid_ready"), sem("hid_out"), sem("y_ready"), sem("y_added")
        var2_ready, rstd2_ready, finished = sem("var2_ready"), sem("rstd2_ready"), sem("finished")
        NORMS = 1 if post else 2
        LINKS = 1 + TOP_TWO_LINKS + (2 + 4 if post else 6 + 8)
        post_chain = sem("post_chain")

        def norm_dve(dve, t, link, out, inp, i):
            for b in range(4):
                last = dve.bn_stats(stats[:, b, :], inp(b))
            link(last)
            dve.memset(idle[:, :], 0.0)
            for b in range(4):
                last = dve.bn_aggr(mean_var[:, b, :], stats[:, b, :])
            link(last)
            dve.tensor_scalar(rstd[:, :], mean_var[:, :, 1], EPS, None, ALU.add).then_inc(var_ready, 1)
            dve.wait_ge(rstd_ready, t * NORMS + i + 1)
            for b in range(4):
                last = dve.tensor_scalar(out[:, b, :], inp(b), mean_var[:, b, 0:1], rstd[:, b:b + 1],
                                         ALU.subtract, ALU.mult)
            return last

        def prep_dve(dve, t, par, part, link):
            if part == "norm":
                norm_part(dve, t, link)
            elif part == "gates":
                gates_part(dve, t, par, link)
            else:
                start_part(dve, t, par, link)

        def norm_part(dve, t, link):
            last = norm_dve(dve, t, link, xn, lambda b: src[:, t * 4 + b, :], 0)
            if post:
                last.then_inc(normed, 1)
            else:
                link(last)
                norm_dve(dve, t, link, xn2, lambda b: xn[:, b, :], 1).then_inc(normed, 1)
                link(dve.tensor_tensor(base[:, :, :], x[:, bass.ds(t * 4, 4), :], xn[:, :, :], ALU.add))

        def gates_part(dve, t, par, link):
            dve.wait_ge(logits_ps, t + 1)
            link(dve.tensor_copy(logits[:, :, :], gate_bank[:, 0:4 * E].rearrange("p (b e) -> p b e", b=4)))
            top_two(dve, link, net, logits[:, :, :], 4, E, tiles)
            shape = [P, 4, E]
            dve.tensor_tensor(expd[:, :, :], logits[:, :, :], tiles["top"][0].unsqueeze(2).to_broadcast(shape),
                              ALU.subtract).then_inc(less_top, 1)
            dve.wait_ge(exp_done, t + 1)
            link(dve.tensor_reduce(small["total"][:, :], expd[:, :, :], AX_X, ALU.add))
            link(dve.reciprocal(small["gate0"][:, :], small["total"][:, :]))
            link(dve.tensor_tensor(expd[:, :, :], expd[:, :, :],
                                   small["gate0"][:, :].unsqueeze(2).to_broadcast(shape), ALU.mult))
            link(dve.tensor_tensor(both[:, :, :], tiles["hot"][0], tiles["hot"][1], ALU.add))
            gate = gates[par][:, :, :]
            if post:
                dve.tensor_tensor(gate, expd[:, :, :], both[:, :, :], ALU.mult).then_inc(gates_ready, 1)
            else:
                link(dve.tensor_tensor(gate, expd[:, :, :], both[:, :, :], ALU.mult))
                link(dve.tensor_reduce(small["total"][:, :], gate, AX_X, ALU.add))
                link(dve.tensor_scalar(small["total"][:, :], small["total"][:, :], 1e-8, None, ALU.add))
                link(dve.reciprocal(small["gap"][:, :], small["total"][:, :]))
                dve.tensor_tensor(gate, gate, small["gap"][:, :].unsqueeze(2).to_broadcast(shape),
                                  ALU.mult).then_inc(gates_ready, 1)

        def start_part(dve, t, par, link):
            link.end()
            dve.wait_ge(bias_ps, t + 1)
            if post:
                dve.wait_ge(affine_done, t + 1)
            dve.tensor_tensor(acc[par][:, :, :], turn_bank[:, :].rearrange("p (b f) -> p b f", b=4),
                              (xn2 if post else base)[:, :, :], ALU.add).then_inc(acc_ready, 1)

        def prep_pool(pool, t):
            for i in range(NORMS):
                pool.wait_ge(var_ready, t * NORMS + i + 1)
                pool.tensor_tensor(rstd[:, :], rstd[:, :], net.minus_half[:, 0:4], ALU.pow).then_inc(rstd_ready, 1)
            if post:
                pool.wait_ge(normed, t + 1)
                shape = [P, 4, P]
                pool.wait_ge(acc_ready, t)
                pool.tensor_tensor(xn2[:, :, :], xn[:, :, :], g1[:, :].unsqueeze(1).to_broadcast(shape),
                                   ALU.mult).then_inc(affine_half, 1)
                pool.wait_ge(affine_half, t + 1)
                pool.tensor_tensor(xn2[:, :, :], xn2[:, :, :], be1[:, :].unsqueeze(1).to_broadcast(shape),
                                   ALU.add).then_inc(affine_done, 1)

        affine_half, out_half = sem("affine_half"), sem("out_half")

        def prep_act(act, t, par, part):
            if part == "tokens":
                act.wait_ge(xT_ps, t + 1)
                act.activation(xT[par][:, :], turn_bank[:, :], ACT.Identity, scale=g_col[:, 0:1],
                               bias=b_col[:, 0:1]).then_inc(xT_ready, 1)
            elif part == "exp":
                act.wait_ge(less_top, t + 1)
                act.activation(expd[:, :, :], expd[:, :, :], ACT.Exp).then_inc(exp_done, 1)
            else:
                act.wait_ge(gatesT_ps, t + 1)
                act.copy(gatesT[:, :], gate_bank[0:E, :]).then_inc(gatesT_ready, 1)

        def prep_pe(pe, t, par, part):
            if part == 0:
                pe.wait_ge(normed, t + 1)
                for b in range(4):
                    last = pe.transpose(turn_bank[:, b * P:(b + 1) * P], (xn if post else xn2)[:, b, :], ident[:, :])
                last.then_inc(xT_ps, 1)
            if part == 1:
                pe.wait_ge(xT_ready, t + 1)
                for b in range(4):
                    out = gate_bank[:, b * E:(b + 1) * E]
                    pe.matmul(out, xT[par][:, b * P:(b + 1) * P], wg[:, :], start=True, stop=False)
                    last = pe.matmul(out, ones_row[:, :], bg[:, :], start=False, stop=True)
                last.then_inc(logits_ps, 1)
            if part == 2:
                pe.wait_ge(gates_ready, t + 1)
                for b in range(4):
                    last = pe.transpose(gate_bank[0:E, b * P:(b + 1) * P], gates[par][:, b, :], ident[:, :])
                last.then_inc(gatesT_ps, 1)
            if part == 3:
                pe.wait_ge(gatesT_ready, t + 1)
                for b in range(4):
                    last = pe.matmul(turn_bank[:, b * P:(b + 1) * P], gatesT[:, b * P:(b + 1) * P], b2[:, :],
                                     start=True, stop=True)
                last.then_inc(bias_ps, 1)

        def hidden_pe(pe, t, par, e):
            for c in range(FC):
                n = e * FC + c
                if n >= 4:
                    pe.wait_ge(hid_out, t * E * FC + n - 3)
                pe.matmul(hid_bank[n % 4][:, :], w1[:, e, c * P:(c + 1) * P], xT[par][:, :],
                          start=True, stop=True).then_inc(hid_ready, 1)

        def output_pe(pe, t, e):
            pe.wait_ge(hid_out, (t * E + e + 1) * FC)
            pe.wait_ge(y_added, t * E + max(e - 1, 0))
            for b in range(4):
                for c in range(FC):
                    last = pe.matmul(y_bank[e % 2][:, b * P:(b + 1) * P], hT[e % 2][:, c, b * P:(b + 1) * P],
                                     w2[:, e, c, :], start=(c == 0), stop=(c == FC - 1))
            last.then_inc(y_ready, 1)

        def experts_act(act, t, e):
            for c in range(FC):
                n = e * FC + c
                act.wait_ge(hid_ready, t * E * FC + n + 1)
                if c == 0 and e >= 2:
                    act.wait_ge(y_ready, t * E + e - 1)
                act.activation(hT[e % 2][:, c, :], hid_bank[n % 4][:, :], func,
                               bias=b1[:, n:n + 1]).then_inc(hid_out, 1)

        def add_dve(dve, t, par, e):
            dve.wait_ge(y_ready, t * E + e + 1)
            if e == 0:
                dve.wait_ge(acc_ready, t + 1)
            else:
                dve.wait_ge(y_added, t * E + e)
            for b in range(4):
                out = x[:, t * 4 + b, :] if e == E - 1 and not post else acc[par][:, b, :]
                last = dve.scalar_tensor_tensor(out, y_bank[e % 2][:, b * P:(b + 1) * P], gates[par][:, b, e:e + 1],
                                                acc[par][:, b, :], ALU.mult, ALU.add)
            last.then_inc(y_added, 1)

        def finish_dve(dve, t, par):
            link = Link(dve, post_chain, t, 2)
            dve.wait_ge(y_added, (t + 1) * E)
            for b in range(4):
                last = dve.bn_stats(stats2[:, b, :], acc[par][:, b, :])
            link(last)
            dve.memset(idle[:, :], 0.0)
            for b in range(4):
                last = dve.bn_aggr(mv2[:, b, :], stats2[:, b, :])
            link(last)
            dve.tensor_scalar(rstd2[:, :], mv2[:, :, 1], EPS, None, ALU.add).then_inc(var2_ready, 1)
            dve.wait_ge(rstd2_ready, t + 1)
            dve.wait_ge(finished, t)
            for b in range(4):
                last = dve.tensor_scalar(out_n[:, b, :], acc[par][:, b, :], mv2[:, b, 0:1], rstd2[:, b:b + 1],
                                         ALU.subtract, ALU.mult)
            last.then_inc(out_normed, 1)
            link.end()

        out_normed = sem("out_normed")

        def finish_pool(pool, t):
            shape = [P, 4, P]
            pool.wait_ge(var2_ready, t + 1)
            pool.tensor_tensor(rstd2[:, :], rstd2[:, :], net.minus_half[:, 0:4], ALU.pow).then_inc(rstd2_ready, 1)
            pool.wait_ge(out_normed, t + 1)
            pool.tensor_tensor(out_n[:, :, :], out_n[:, :, :], g2[:, :].unsqueeze(1).to_broadcast(shape),
                               ALU.mult).then_inc(out_half, 1)
            pool.wait_ge(out_half, t * 2 + 1)
            pool.tensor_tensor(out_n[:, :, :], out_n[:, :, :], be2[:, :].unsqueeze(1).to_broadcast(shape),
                               ALU.add).then_inc(out_half, 1)
            pool.wait_ge(out_half, t * 2 + 2)
            tokens = x[:, bass.ds(t * 4, 4), :]
            pool.tensor_tensor(tokens, tokens, out_n[:, :, :], ALU.add).then_inc(finished, 1)

        def turns(eng, body, prep):
            prep(0, 0)
            with eng.Fori(0, NTURN // 2 - 1) as i:
                body(i * 2, 0, True)
                body(i * 2 + 1, 1, True)
            body(NTURN - 2, 0, True)
            body(NTURN - 1, 1, False)

        block = ctx.enter_context(nc.Block())

        @block.sync
        def _(sp):
            for dst_ap, s in loads:
                sp.dma_start(dst_ap, s).then_inc(loaded, 16)

        @block.gpsimd
        def _(pool):
            pool.wait_ge(loaded, 16 * len(loads))

            def body(t, par, more):
                if more:
                    prep_pool(pool, t + 1)
                if post:
                    finish_pool(pool, t)

            turns(pool, body, lambda t, par: prep_pool(pool, t))

        @block.vector
        def _(dve):
            dve.wait_ge(loaded, 16 * len(loads))

            def body(t, par, more):
                link = Link(dve, chain, t + 1, LINKS)
                for e in range(E):
                    add_dve(dve, t, par, e)
                    if more and e in (0, 3, 6):
                        prep_dve(dve, t + 1, 1 - par, {0: "norm", 3: "gates", 6: "start"}[e], link)
                if post:
                    finish_dve(dve, t, par)

            def first(t, par):
                link = Link(dve, chain, t, LINKS)
                for part in ("norm", "gates", "start"):
                    prep_dve(dve, t, par, part, link)

            turns(dve, body, first)

        @block.scalar
        def _(act):
            act.wait_ge(loaded, 16 * len(loads))

            def body(t, par, more):
                for e in range(E):
                    experts_act(act, t, e)
                    if more and e in (3, 4, 6):
                        prep_act(act, t + 1, 1 - par, {3: "tokens", 4: "exp", 6: "gates"}[e])

            def first(t, par):
                for part in ("tokens", "exp", "gates"):
                    prep_act(act, t, par, part)

            turns(act, body, first)

        @block.tensor
        def _(pe):
            pe.wait_ge(loaded, 16 * len(loads))

            def body(t, par, more):
                hidden_pe(pe, t, par, 0)
                for e in range(E):
                    if e + 1 < E:
                        hidden_pe(pe, t, par, e + 1)
                    output_pe(pe, t, e)
                    if more and e in (2, 3, 5, 6):
                        prep_pe(pe, t + 1, 1 - par, (2, 3, 5, 6).index(e))

            def first(t, par):
                for part in range(4):
                    prep_pe(pe, t, par, part)

            turns(pe, body, first)


SLOTS_1 = 24 * 384
SLOTS_2 = 2 * NBATCH * P


class Routed:

    def __init__(self, nc, ctx, name):
        def sb(n, shape, dt=F32):
            return ctx.enter_context(nc.sbuf_tensor(f"{name}_{n}", shape, dt))

        self.xn = sb("xn_all", [P, NBATCH, P])
        self.gate = sb("gate", [P, 2, NBATCH])
        self.write = sb("slot_write", [P, NBATCH, 2], U32)
        self.read = sb("slot_read", [P, NBATCH, 2], U32)


def norm_and_logits(nc, net, name, E, wg_dram, routed, logits):
    with ExitStack() as ctx:
        def sb(n, shape, dt=F32):
            return ctx.enter_context(nc.sbuf_tensor(f"{name}n_{n}", shape, dt))

        def sem(n):
            return net.sem(f"{name}n_{n}")

        x, xn_all = net.x, routed.xn
        wg = sb("wg", [P, E]); idle = sb("idle", [P, 1])
        stats = sb("stats", [P, 4, 6]); mean_var = sb("mean_var", [P, 4, 2]); rstd = sb("rstd", [P, 4])
        xn = [sb(f"xn{i}", [P, 4, P]) for i in range(2)]
        xT = [sb(f"xT{i}", [P, 4 * P]) for i in range(2)]
        turn_bank, logit_bank = net.banks[0:2], net.banks[2:4]
        loaded, chain = sem("loaded"), sem("chain")
        var_ready, rstd_ready, normed = sem("var_ready"), sem("rstd_ready"), sem("normed")
        xT_ps, xT_ready, logits_ps, logits_out, kept = (
            sem("xT_ps"), sem("xT_ready"), sem("logits_ps"), sem("logits_out"), sem("kept"))

        block = ctx.enter_context(nc.Block())

        @block.sync
        def _(sp):
            sp.dma_start(wg[:, :], wg_dram).then_inc(loaded, 16)
            sp.wait_ge(loaded, 16)

        @block.gpsimd
        def _(pool):
            with pool.Fori(0, NTURN // 2) as i:
                for par in range(2):
                    t = i * 2 + par
                    pool.wait_ge(var_ready, t + 1)
                    pool.tensor_tensor(rstd[:, :], rstd[:, :], net.minus_half[:, 0:4], ALU.pow).then_inc(rstd_ready, 1)
                    pool.wait_ge(normed, t + 1)
                    pool.tensor_copy(xn[par][:, :, :], xn_all[:, bass.ds(t * 4, 4), :]).then_inc(kept, 1)

        @block.vector
        def _(dve):
            with dve.Fori(0, NTURN // 2) as i:
                link = Link(dve, chain, i, 4)
                for par in range(2):
                    t = i * 2 + par
                    for b in range(4):
                        last = dve.bn_stats(stats[:, b, :], x[:, t * 4 + b, :])
                    link(last)
                    dve.memset(idle[:, :], 0.0)
                    for b in range(4):
                        last = dve.bn_aggr(mean_var[:, b, :], stats[:, b, :])
                    link(last)
                    dve.tensor_scalar(rstd[:, :], mean_var[:, :, 1], EPS, None, ALU.add).then_inc(var_ready, 1)
                    dve.wait_ge(rstd_ready, t + 1)
                    for b in range(4):
                        last = dve.tensor_scalar(xn_all[:, t * 4 + b, :], x[:, t * 4 + b, :], mean_var[:, b, 0:1],
                                                 rstd[:, b:b + 1], ALU.subtract, ALU.mult)
                    last.then_inc(normed, 1)
                for par in range(2):
                    t = i * 2 + par
                    dve.wait_ge(logits_ps, t + 1)
                    dve.tensor_copy(logits[:, :, bass.ds(t * 4, 4)],
                                    logit_bank[par][:, 0:4 * E].rearrange("p (b e) -> p e b", b=4)
                                    ).then_inc(logits_out, 1)
                link.end()

        @block.scalar
        def _(act):
            with act.Fori(0, NTURN // 2) as i:
                for par in range(2):
                    act.wait_ge(xT_ps, i * 2 + par + 1)
                    act.copy(xT[par][:, :], turn_bank[par][:, :]).then_inc(xT_ready, 1)

        @block.tensor
        def _(pe):
            pe.wait_ge(loaded, 16)
            with pe.Fori(0, NTURN // 2) as i:
                for par in range(2):
                    pe.wait_ge(kept, i * 2 + par + 1)
                    for b in range(4):
                        last = pe.transpose(turn_bank[par][:, b * P:(b + 1) * P], xn[par][:, b, :], net.ident[:, :])
                    last.then_inc(xT_ps, 1)
                pe.wait_ge(logits_out, i * 2)
                for par in range(2):
                    pe.wait_ge(xT_ready, i * 2 + par + 1)
                    for b in range(4):
                        last = pe.matmul(logit_bank[par][:, b * E:(b + 1) * E], xT[par][:, b * P:(b + 1) * P],
                                         wg[:, :], start=True, stop=True)
                    last.then_inc(logits_ps, 1)


def route(nc, net, name, E, capacity, consts, routed, logits):
    grouped = capacity is not None
    with ExitStack() as ctx:
        def sb(n, shape, dt=F32):
            return ctx.enter_context(nc.sbuf_tensor(f"{name}r_{n}", shape, dt))

        def sem(n):
            return net.sem(f"{name}r_{n}")

        B, W = NBATCH, E * NBATCH
        lower = sb("lower", [P, P]); whole = sb("whole", [P, P]); reset = sb("reset", [P, E, B])
        base = sb("base", [P, E]); one = sb("one", [P, E])
        hot = [sb(f"hot{i}", [P, E, B]) for i in range(2)]
        left = sb("left", [P, E, B]); count = [sb(f"count{i}", [P, E, B]) for i in range(2)]
        top = [sb(f"top{i}", [P, B]) for i in range(2)]
        least = sb("least", [P, B]); gap = sb("gap", [P, 2, B]); total = sb("total", [P, B])
        rank = sb("rank", [P, 2, B]); start = sb("start", [P, 2, B]); keep = sb("keep", [P, 2, B])
        slot = sb("slot", [P, 2, B]); sizes = sb("sizes", [P, E])
        loaded, chain = sem("loaded"), sem("chain")
        less_top, exp_done, counts_ready, ranks_ps = (
            sem("less_top"), sem("exp_done"), sem("counts_ready"), sem("ranks_ps"))
        shape = [P, B, E]

        def by_token(tile):
            return tile[:, :, :].rearrange("p e b -> p b e")

        def flat(tile):
            return tile[:, :, :].rearrange("p e b -> p (e b)")

        sets = hot if grouped else [left]
        half = W // 2 if grouped else W
        banks = [net.banks[2 * r:2 * r + 2] if grouped else [net.banks[0]] for r in range(len(sets))]

        block = ctx.enter_context(nc.Block())

        @block.sync
        def _(sp):
            for dst_ap, s in ((lower[:, :], consts["lower"]), (whole[:, :], consts["whole"]),
                              (reset[:, :, :], consts["reset"]), (base[:, :], consts["base"])):
                sp.dma_start(dst_ap, s).then_inc(loaded, 16)
            sp.wait_ge(loaded, 64)

        @block.scalar
        def _(act):
            act.wait_ge(less_top, 1)
            if grouped:
                act.activation(flat(left), flat(left), ACT.Exp)
            act.activation(gap[:, 0, :], gap[:, 0, :], ACT.Exp).then_inc(exp_done, 1)

        @block.vector
        def _(dve):
            link = Link(dve, chain, 0, 0)
            dve.wait_ge(loaded, 64)
            top_two(dve, link, net, by_token(logits), B, E,
                    dict(top=[top[0][:, :], top[1][:, :]], hot=[by_token(hot[0]), by_token(hot[1])],
                         least=least[:, :], left=by_token(left)))
            if grouped:
                link(dve.tensor_tensor(by_token(left), by_token(logits),
                                       top[0][:, :].unsqueeze(2).to_broadcast(shape), ALU.subtract))
            dve.tensor_tensor(gap[:, 0, :], top[1][:, :], top[0][:, :], ALU.subtract).then_inc(less_top, 1)
            dve.wait_ge(exp_done, 1)
            if grouped:
                link(dve.tensor_reduce(total[:, :], by_token(left), AX_X, ALU.add))
            else:
                link(dve.tensor_scalar(total[:, :], gap[:, 0, :], 1.0, None, ALU.add))
            link(dve.reciprocal(routed.gate[:, 0, :], total[:, :]))
            link(dve.tensor_tensor(routed.gate[:, 1, :], gap[:, 0, :], routed.gate[:, 0, :], ALU.mult))
            if not grouped:
                link(dve.tensor_tensor(flat(left), flat(hot[0]), flat(hot[1]), ALU.add))
                link(dve.memset(one[:, :], 1.0))
            for r, s in enumerate(sets):
                link(dve.tensor_tensor_scan(flat(count[r]), flat(reset), flat(s), 0.0, ALU.mult, ALU.add))
            link(dve.tensor_copy(sizes[:, :], count[0][:, :, B - 1]))
            for r, s in enumerate(sets):
                link(dve.tensor_tensor(flat(count[r]), flat(count[r]), flat(s), ALU.subtract))
            if grouped:
                link(dve.tensor_tensor(count[1][:, :, :], count[1][:, :, :],
                                       sizes[:, :].unsqueeze(2).to_broadcast([P, E, B]), ALU.add))
            dve.sem_inc(counts_ready, 1)
            dve.wait_ge(ranks_ps, 1)
            if not grouped:
                link(dve.tensor_copy(sizes[:, :], net.banks[1][:, 0:E]))
                link(dve.tensor_tensor_scan(base[:, :], one[:, :], sizes[:, :], 0.0, ALU.mult, ALU.add))
                link(dve.tensor_tensor(base[:, :], base[:, :], sizes[:, :], ALU.subtract))
            for r in range(2):
                n = r if grouped else 0
                step = half // B
                for i, bank in enumerate(banks[n]):
                    link(dve.tensor_tensor(left[:, i * step:(i + 1) * step, :], hot[r][:, i * step:(i + 1) * step, :],
                                           bank[:, 0:half].rearrange("p (e b) -> p e b", b=B), ALU.mult))
                link(dve.tensor_reduce(rank[:, r, :], by_token(left), AX_X, ALU.add))
                link(dve.tensor_tensor(left[:, :, :], hot[r][:, :, :],
                                       base[:, :].unsqueeze(2).to_broadcast([P, E, B]), ALU.mult))
                link(dve.tensor_reduce(start[:, r, :], by_token(left), AX_X, ALU.add))
            link(dve.tensor_tensor(slot[:, :, :], rank[:, :, :], start[:, :, :], ALU.add))
            if grouped:
                link(dve.tensor_scalar(keep[:, :, :], rank[:, :, :], float(capacity), None, ALU.is_lt))
                link(dve.tensor_tensor(routed.gate[:, :, :], routed.gate[:, :, :], keep[:, :, :], ALU.mult))
                link(dve.tensor_tensor(total[:, :], routed.gate[:, 0, :], routed.gate[:, 1, :], ALU.add))
                link(dve.tensor_scalar(total[:, :], total[:, :], 1e-9, None, ALU.max))
                link(dve.reciprocal(least[:, :], total[:, :]))
                link(dve.tensor_tensor(routed.gate[:, :, :], routed.gate[:, :, :],
                                       least[:, :].unsqueeze(1).to_broadcast([P, 2, B]), ALU.mult))
                for out, other in ((routed.write, SLOTS_1 + 1), (routed.read, SLOTS_1)):
                    link(dve.tensor_scalar(start[:, :, :], slot[:, :, :], -float(other), None, ALU.add))
                    link(dve.tensor_tensor(start[:, :, :], start[:, :, :], keep[:, :, :], ALU.mult))
                    link(dve.tensor_scalar(out[:, :, :].rearrange("p b r -> p r b"), start[:, :, :],
                                           float(other), None, ALU.add))
            else:
                link(dve.tensor_copy(routed.write[:, :, :].rearrange("p b r -> p r b"), slot[:, :, :]))
                link(dve.tensor_copy(routed.read[:, :, :].rearrange("p b r -> p r b"), slot[:, :, :]))

        @block.tensor
        def _(pe):
            pe.wait_ge(counts_ready, 1)
            for r, s in enumerate(sets):
                for i, bank in enumerate(banks[r]):
                    at = slice(i * half, (i + 1) * half)
                    pe.matmul(bank[:, 0:half], lower[:, :], flat(s)[:, at], start=True, stop=False)
                    last = pe.matmul(bank[:, 0:half], whole[:, :], flat(count[r])[:, at], start=False, stop=True)
            if not grouped:
                last = pe.matmul(net.banks[1][:, 0:E], whole[:, :], sizes[:, :], start=True, stop=True)
            last.then_inc(ranks_ps, 1)


def carry_wait(pool, net, idle, carried, before):
    pool.wait_ge(carried, before)
    pool.tensor_tensor(idle[:, :], net.plus_half[:, 0:1], net.plus_half[:, 0:1], ALU.mult).then_inc(carried, 1)


def scatter_rows(nc, net, name, routed, slots_dram, n_slots):
    with ExitStack() as ctx:
        def sb(n, shape, dt=F32):
            return ctx.enter_context(nc.sbuf_tensor(f"{name}s_{n}", shape, dt))

        rows = [sb(f"rows{i}", [P, 4, P]) for i in range(2)]
        where = [sb(f"where{i}", [P, 4, 2], U32) for i in range(2)]
        idle = sb("idle", [P, 1])
        staged, carried = net.sem(f"{name}s_staged"), net.sem(f"{name}s_carried")
        written = [net.sem(f"{name}s_written{i}") for i in range(2)]
        block = ctx.enter_context(nc.Block())

        @block.vector
        def _(dve):
            with dve.Fori(0, NTURN // 2) as i:
                for par in range(2):
                    t = i * 2 + par
                    dve.wait_ge(written[par], i * 8 * 16)
                    dve.tensor_copy(rows[par][:, :, :], routed.xn[:, bass.ds(t * 4, 4), :])
                    dve.tensor_copy(where[par][:, :, :], routed.write[:, bass.ds(t * 4, 4), :]).then_inc(staged, 1)

        @block.gpsimd
        def _(pool):
            with pool.Fori(0, NTURN // 2) as i:
                for par in range(2):
                    pool.wait_ge(staged, i * 2 + par + 1)
                    carry_wait(pool, net, idle, carried, i * 2 + par)
                    for b in range(4):
                        for r in range(2):
                            pool.indirect_dma_start(
                                slots_dram[:, :], bass.IndirectOffsetOnAxis(where[par][:, b, r:r + 1], 0),
                                rows[par][:, b, :], None, bounds_check=n_slots - 1,
                                oob_is_err=False).then_inc(written[par], 16)
            for par in range(2):
                pool.wait_ge(written[par], NTURN // 2 * 8 * 16)


def combine_rows(nc, net, name, routed, rows_dram, n_rows, final):
    with ExitStack() as ctx:
        def sb(n, shape, dt=F32):
            return ctx.enter_context(nc.sbuf_tensor(f"{name}c_{n}", shape, dt))

        def sem(n):
            return net.sem(f"{name}c_{n}")

        x = net.x
        got = [[sb(f"got{i}{r}", [P, 4, P]) for r in range(2)] for i in range(2)]
        where = [sb(f"where{i}", [P, 4, 2], U32) for i in range(2)]
        acc = sb("acc", [P, 4, P]); stats = sb("stats", [P, 4, 6]); mean_var = sb("mean_var", [P, 4, 2])
        rstd = sb("rstd", [P, 4]); idle = sb("idle", [P, 1]); pool_idle = sb("pool_idle", [P, 1])
        gain = sb("gain", [P, P]); offset = sb("offset", [P, P])
        loaded, staged, chain, used = sem("loaded"), sem("staged"), sem("chain"), sem("used")
        var_ready, rstd_ready = sem("var_ready"), sem("rstd_ready")
        chain2, carried = sem("chain2"), sem("carried")
        gathered = [sem(f"gathered{i}") for i in range(2)]
        LINKS = 7 if final else 2
        block = ctx.enter_context(nc.Block())

        if final:
            @block.sync
            def _(sp):
                sp.dma_start(gain[:, :], final[0]).then_inc(loaded, 16)
                sp.dma_start(offset[:, :], final[1]).then_inc(loaded, 16)
                sp.wait_ge(loaded, 32)

        @block.scalar
        def _(act):
            with act.Fori(0, NTURN // 2) as i:
                for par in range(2):
                    t = i * 2 + par
                    act.wait_ge(gathered[par], i * 8 * 16)
                    act.copy(where[par][:, :, :],
                             routed.read[:, bass.ds(t * 4, 4), :]).then_inc(staged, 1)

        @block.gpsimd
        def _(pool):
            with pool.Fori(0, NTURN // 2) as i:
                for par in range(2):
                    t = i * 2 + par
                    pool.wait_ge(staged, t + 1)
                    pool.wait_ge(used, i * 2)
                    carry_wait(pool, net, pool_idle, carried, i * 2 + par)
                    for b in range(4):
                        for r in range(2):
                            pool.indirect_dma_start(
                                got[par][r][:, b, :], None, rows_dram[:, :],
                                bass.IndirectOffsetOnAxis(where[par][:, b, r:r + 1], 0),
                                bounds_check=n_rows - 1, oob_is_err=False).then_inc(gathered[par], 16)
                if final:
                    for par in range(2):
                        pool.wait_ge(var_ready, i * 2 + par + 1)
                        pool.tensor_tensor(rstd[:, :], rstd[:, :], net.minus_half[:, 0:4],
                                           ALU.pow).then_inc(rstd_ready, 1)

        @block.vector
        def _(dve):
            if final:
                dve.wait_ge(loaded, 32)
            with dve.Fori(0, NTURN // 2) as i:
                link = Link(dve, chain, i, 2 * LINKS)
                for par in range(2):
                    t = i * 2 + par
                    dve.wait_ge(gathered[par], (i + 1) * 8 * 16)
                    start = routed.xn if final else x
                    for b in range(4):
                        last = dve.scalar_tensor_tensor(acc[:, b, :], got[par][0][:, b, :],
                                                        routed.gate[:, 0, bass.ds(t * 4 + b, 1)],
                                                        start[:, t * 4 + b, :], ALU.mult, ALU.add)
                    link(last)
                    for b in range(4):
                        out = acc[:, b, :] if final else x[:, t * 4 + b, :]
                        last = dve.scalar_tensor_tensor(out, got[par][1][:, b, :],
                                                        routed.gate[:, 1, bass.ds(t * 4 + b, 1)],
                                                        acc[:, b, :], ALU.mult, ALU.add)
                    link(last)
                    dve.sem_inc(used, 1)
                    if final:
                        shape = [P, 4, P]
                        for b in range(4):
                            last = dve.bn_stats(stats[:, b, :], acc[:, b, :])
                        link(last)
                        dve.memset(idle[:, :], 0.0)
                        for b in range(4):
                            last = dve.bn_aggr(mean_var[:, b, :], stats[:, b, :])
                        link(last)
                        dve.tensor_scalar(rstd[:, :], mean_var[:, :, 1], 1e-6, None, ALU.add).then_inc(var_ready, 1)
                        dve.wait_ge(rstd_ready, t + 1)
                        for b in range(4):
                            last = dve.tensor_scalar(acc[:, b, :], acc[:, b, :], mean_var[:, b, 0:1],
                                                     rstd[:, b:b + 1], ALU.subtract, ALU.mult)
                        link(last)
                        link(dve.tensor_tensor(acc[:, :, :], acc[:, :, :],
                                               gain[:, :].unsqueeze(1).to_broadcast(shape), ALU.mult))
                        link(dve.tensor_tensor(acc[:, :, :], acc[:, :, :],
                                               offset[:, :].unsqueeze(1).to_broadcast(shape), ALU.add))
                        tokens = x[:, bass.ds(t * 4, 4), :]
                        dve.tensor_tensor(tokens, tokens, acc[:, :, :], ALU.add).then_inc(chain2, 1)
                        dve.wait_ge(chain2, t + 1)
                link.end()



def chunk_experts(nc, net, w1_dram, w2_dram, slots_dram, rows_dram):
    E, FC = 8, 4
    with ExitStack() as ctx:
        def sb(n, shape, dt=F32):
            return ctx.enter_context(nc.sbuf_tensor(f"L2e_{n}", shape, dt))

        def sem(n):
            return net.sem(f"L2e_{n}")

        w1 = [sb(f"w1{i}", [P, FC * P]) for i in range(2)]; w2 = [sb(f"w2{i}", [P, FC, P]) for i in range(2)]
        rows = [sb(f"rows{i}", [P, 4, P]) for i in range(2)]; xT = [sb(f"xT{i}", [P, 4 * P]) for i in range(2)]
        hT = [sb(f"hT{i}", [P, FC, 4 * P]) for i in range(2)]; y = [sb(f"y{i}", [P, 4, P]) for i in range(2)]
        hid_bank, y_bank, turn_bank = net.banks[0:4], net.banks[4:6], net.banks[6:8]
        w_loaded = [sem(f"w_loaded{i}") for i in range(2)]
        rows_loaded = [sem(f"rows_loaded{i}") for i in range(2)]
        stored = [sem(f"stored{i}") for i in range(2)]
        xT_ps, xT_ready, hid_ready, hid_out, y_ready, y_out = (
            sem(n) for n in ("xT_ps", "xT_ready", "hid_ready", "hid_out", "y_ready", "y_out"))
        slots = slots_dram.rearrange("(h q p) d -> h p q d", p=P, q=4)
        outs = rows_dram.rearrange("(h q p) d -> h p q d", p=P, q=4)
        NI = E // 2
        block = ctx.enter_context(nc.Block())

        @block.sync
        def _(sp):
            with sp.Fori(0, NI) as i:
                for n in range(4):
                    h, par = i * 4 + n, n % 2
                    if n % 2 == 0:
                        e = n // 2
                        sp.wait_ge(y_ready, i * 4)
                        sp.dma_start(w1[e][:, :], w1_dram[:, i * 2 + e, :]).then_inc(w_loaded[e], 16)
                        sp.dma_start(w2[e][:, :, :], w2_dram[:, i * 2 + e, :, :]).then_inc(w_loaded[e], 16)
                    if n >= 2:
                        sp.wait_ge(xT_ps, i * 4 + n - 1)
                    else:
                        sp.wait_ge(xT_ps, i * 4)
                    sp.dma_start(rows[par][:, :, :], slots[h, :, :, :]).then_inc(rows_loaded[par], 16)

        @block.gpsimd
        def _(pool):
            with pool.Fori(0, NI) as i:
                for n in range(4):
                    pool.wait_ge(y_out, i * 4 + n + 1)
                    pool.dma_start(outs[i * 4 + n, :, :, :], y[n % 2][:, :, :]).then_inc(stored[n % 2], 16)
            for par in range(2):
                pool.wait_ge(stored[par], NI * 2 * 16)

        @block.scalar
        def _(act):
            with act.Fori(0, NI) as i:
                for n in range(4):
                    h = i * 4 + n
                    for c in range(FC):
                        act.wait_ge(hid_ready, h * FC + c + 1)
                        if c == 0 and n >= 2:
                            act.wait_ge(y_ready, h - 1)
                        elif c == 0:
                            act.wait_ge(y_ready, i * 4)
                        act.activation(hT[n % 2][:, c, :], hid_bank[c][:, :], ACT.Gelu).then_inc(hid_out, 1)

        @block.vector
        def _(dve):
            with dve.Fori(0, NI) as i:
                for n in range(5):
                    if n < 4:
                        h = i * 4 + n
                        dve.wait_ge(xT_ps, h + 1)
                        dve.tensor_copy(xT[n % 2][:, :], turn_bank[n % 2][:, :]).then_inc(xT_ready, 1)
                    if n:
                        h, par = i * 4 + n - 1, (n - 1) % 2
                        dve.wait_ge(y_ready, h + 1)
                        dve.wait_ge(stored[par], 16 * (i * 2 + (n - 1) // 2))
                        dve.tensor_copy(y[par][:, :, :],
                                        y_bank[par][:, :].rearrange("p (q d) -> p q d", q=4)).then_inc(y_out, 1)

        @block.tensor
        def _(pe):
            def turn(i, n):
                h = i * 4 + n
                pe.wait_ge(rows_loaded[n % 2], 16 * (i * 2 + n // 2 + 1))
                for q in range(4):
                    last = pe.transpose(turn_bank[n % 2][:, q * P:(q + 1) * P], rows[n % 2][:, q, :], net.ident[:, :])
                last.then_inc(xT_ps, 1)

            def hidden(i, n):
                h, e = i * 4 + n, n // 2
                pe.wait_ge(xT_ready, h + 1)
                if n % 2 == 0:
                    pe.wait_ge(w_loaded[e], 32 * (i + 1))
                for c in range(FC):
                    pe.wait_ge(hid_out, i * 4 * FC + max(n * FC + c - 3, 0))
                    pe.matmul(hid_bank[c][:, :], w1[e][:, c * P:(c + 1) * P], xT[n % 2][:, :],
                              start=True, stop=True).then_inc(hid_ready, 1)

            def output(i, n):
                h, e = i * 4 + n, n // 2
                pe.wait_ge(hid_out, (h + 1) * FC)
                pe.wait_ge(y_out, i * 4 + max(n - 1, 0))
                for q in range(4):
                    for c in range(FC):
                        last = pe.matmul(y_bank[n % 2][:, q * P:(q + 1) * P], hT[n % 2][:, c, q * P:(q + 1) * P],
                                         w2[e][:, c, :], start=(c == 0), stop=(c == FC - 1))
                last.then_inc(y_ready, 1)

            with pe.Fori(0, NI) as i:
                turn(i, 0)
                hidden(i, 0)
                for n in range(4):
                    if n + 1 < 4:
                        turn(i, n + 1)
                        hidden(i, n + 1)
                    output(i, n)


def chunked_moe_stage(nc, net):
    with ExitStack() as ctx:
        routed = Routed(nc, ctx, "L2f")
        with ExitStack() as part:
            logits = part.enter_context(nc.sbuf_tensor("L2f_logits", [P, 8, NBATCH], F32))
            norm_and_logits(nc, net, "L2f", 8, net.t["L2f_wg"], routed, logits)
            route(nc, net, "L2f", 8, None, dict(lower=net.t["lower"], whole=net.t["ones"], reset=net.t["reset8"],
                                                base=net.t["base8"]), routed, logits)
        scatter_rows(nc, net, "L2f", routed, net.slots2, SLOTS_2)
        chunk_experts(nc, net, net.t["L2f_w1"], net.t["L2f_w2"], net.slots2, net.rows2)
        combine_rows(nc, net, "L2f", routed, net.rows2, SLOTS_2, None)


def hidden_experts(nc, net, w1_dram, b1_dram, slots_dram, rows_dram):
    E, FF, Q = 24, 512, 3
    with ExitStack() as ctx:
        def sb(n, shape, dt=F32):
            return ctx.enter_context(nc.sbuf_tensor(f"L1h_{n}", shape, dt))

        def sem(n):
            return net.sem(f"L1h_{n}")

        w1 = [sb(f"w1{i}", [P, FF]) for i in range(2)]; b1 = [sb(f"b1{i}", [P, FF]) for i in range(2)]
        rows = [sb(f"rows{i}", [P, Q, P]) for i in range(2)]; xT = [sb(f"xT{i}", [P, Q * P]) for i in range(2)]
        hid = [sb(f"hid{i}", [P, Q, FF]) for i in range(2)]
        hid_bank, turn_bank = net.banks[0:6], net.banks[6:8]
        loaded = [sem(f"loaded{i}") for i in range(2)]; stored = [sem(f"stored{i}") for i in range(2)]
        xT_ps, xT_ready, hid_ready, hid_out = (sem(n) for n in ("xT_ps", "xT_ready", "hid_ready", "hid_out"))
        slots = slots_dram.rearrange("(e q p) d -> e p q d", p=P, q=Q)
        outs = rows_dram[0:SLOTS_1, :].rearrange("(e q p) f -> e p q f", p=P, q=Q)
        block = ctx.enter_context(nc.Block())

        @block.sync
        def _(sp):
            with sp.Fori(0, E // 2) as i:
                for par in range(2):
                    e = i * 2 + par
                    sp.wait_ge(hid_out, i * 2 * Q)
                    sp.dma_start(rows[par][:, :, :], slots[e, :, :, :]).then_inc(loaded[par], 16)
                    sp.dma_start(w1[par][:, :], w1_dram[:, e, :]).then_inc(loaded[par], 16)
                    sp.dma_start(b1[par][:, :], b1_dram[bass.ds(e, 1), :].to_broadcast([P, FF])).then_inc(loaded[par], 16)

        @block.gpsimd
        def _(pool):
            with pool.Fori(0, E // 2) as i:
                for par in range(2):
                    e = i * 2 + par
                    pool.wait_ge(hid_out, (e + 1) * Q)
                    pool.dma_start(outs[e, :, :, :], hid[par][:, :, :]).then_inc(stored[par], 16)
            for par in range(2):
                pool.wait_ge(stored[par], E // 2 * 16)

        @block.scalar
        def _(act):
            with act.Fori(0, E // 2) as i:
                for par in range(2):
                    act.wait_ge(xT_ps, i * 2 + par + 1)
                    act.copy(xT[par][:, :], turn_bank[par][:, 0:Q * P]).then_inc(xT_ready, 1)

        @block.vector
        def _(dve):
            with dve.Fori(0, E // 2) as i:
                for par in range(2):
                    dve.wait_ge(stored[par], i * 16)
                    for q in range(Q):
                        dve.wait_ge(hid_ready, (i * 2 + par) * Q + q + 1)
                        dve.tensor_tensor(hid[par][:, q, :], hid_bank[par * Q + q][:, :], b1[par][:, :],
                                          ALU.add).then_inc(hid_out, 1)

        @block.tensor
        def _(pe):
            with pe.Fori(0, E // 2) as i:
                for par in range(2):
                    pe.wait_ge(loaded[par], 48 * (i + 1))
                    for q in range(Q):
                        last = pe.transpose(turn_bank[par][:, q * P:(q + 1) * P], rows[par][:, q, :], net.ident[:, :])
                    last.then_inc(xT_ps, 1)
                for par in range(2):
                    pe.wait_ge(xT_ready, i * 2 + par + 1)
                    pe.wait_ge(hid_out, i * 2 * Q)
                    for q in range(Q):
                        pe.matmul(hid_bank[par * Q + q][:, :], xT[par][:, q * P:(q + 1) * P], w1[par][:, :],
                                  start=True, stop=True).then_inc(hid_ready, 1)


def mix_hidden(nc, net, gain_dram, offset_dram, routed, rows_dram):
    FF = 512
    with ExitStack() as ctx:
        def sb(n, shape, dt=F32):
            return ctx.enter_context(nc.sbuf_tensor(f"L1m_{n}", shape, dt))

        def sem(n):
            return net.sem(f"L1m_{n}")

        gain = sb("gain", [P, FF]); offset = sb("offset", [P, FF])
        got = [[sb(f"got{b}{r}", [P, FF]) for r in range(2)] for b in range(4)]
        read = sb("read", [P, 4, 2], U32); write = sb("write", [P, 4, 2], U32)
        mixed = [sb(f"mixed{b}", [P, FF]) for b in range(4)]; out = [sb(f"out{b}", [P, FF]) for b in range(4)]
        stats = sb("stats", [P, 4, 6]); mean_var = sb("mean_var", [P, 4, 2]); rstd = sb("rstd", [P, 4])
        idle = sb("idle", [P, 1]); pool_idle = sb("pool_idle", [P, 1])
        loaded, read_staged, write_staged, chain = sem("loaded"), sem("read_staged"), sem("write_staged"), sem("chain")
        scaled, mixed_ready, var_ready, rstd_ready, normed = (
            sem(n) for n in ("scaled", "mixed_ready", "var_ready", "rstd_ready", "normed"))
        gained, affine, out_ready, carried = sem("gained"), sem("affine"), sem("out_ready"), sem("carried")
        gathered = [sem(f"gathered{b}") for b in range(4)]; written = [sem(f"written{b}") for b in range(4)]
        block = ctx.enter_context(nc.Block())

        @block.sync
        def _(sp):
            sp.dma_start(gain[:, :], gain_dram).then_inc(loaded, 16)
            sp.dma_start(offset[:, :], offset_dram).then_inc(loaded, 16)
            sp.wait_ge(loaded, 32)

        def gather(pool, b):
            for r in range(2):
                pool.indirect_dma_start(got[b][r][:, :], None, rows_dram[:, :],
                                        bass.IndirectOffsetOnAxis(read[:, b, r:r + 1], 0),
                                        bounds_check=SLOTS_1, oob_is_err=False).then_inc(gathered[b], 16)

        @block.gpsimd
        def _(pool):
            with pool.Fori(0, NTURN) as t:
                pool.wait_ge(read_staged, t + 1)
                carry_wait(pool, net, pool_idle, carried, t * 5)
                for b in range(4):
                    gather(pool, b)
                for b in range(4):
                    pool.wait_ge(var_ready, t * 4 + b + 1)
                    pool.tensor_tensor(rstd[:, b:b + 1], rstd[:, b:b + 1], net.minus_half[:, 0:1],
                                       ALU.pow).then_inc(rstd_ready, 1)
                pool.wait_ge(write_staged, t + 1)
                for b in range(4):
                    pool.wait_ge(out_ready, t * 4 + b + 1)
                    carry_wait(pool, net, pool_idle, carried, t * 5 + 1 + b)
                    for r in range(2):
                        pool.indirect_dma_start(rows_dram[0:SLOTS_1, :], bass.IndirectOffsetOnAxis(write[:, b, r:r + 1], 0),
                                                out[b][:, :], None, bounds_check=SLOTS_1 - 1,
                                                oob_is_err=False).then_inc(written[b], 16)
            for b in range(4):
                pool.wait_ge(written[b], NTURN * 32)

        @block.scalar
        def _(act):
            with act.Fori(0, NTURN) as t:
                now = bass.ds(t * 4, 4)
                for b in range(4):
                    act.wait_ge(gathered[b], t * 32)
                act.copy(read[:, :, :], routed.read[:, now, :]).then_inc(read_staged, 1)
                for b in range(4):
                    act.wait_ge(gathered[b], (t + 1) * 32)
                    act.wait_ge(normed, t * 4)
                    act.activation(mixed[b][:, :], got[b][0][:, :], ACT.Copy,
                                   scale=routed.gate[:, 0, bass.ds(t * 4 + b, 1)]).then_inc(scaled, 1)
                for b in range(4):
                    act.wait_ge(written[b], t * 32)
                act.copy(write[:, :, :], routed.write[:, now, :]).then_inc(write_staged, 1)
                for b in range(4):
                    act.wait_ge(affine, t * 4 + b + 1)
                    act.activation(out[b][:, :], mixed[b][:, :], ACT.Relu).then_inc(out_ready, 1)

        @block.vector
        def _(dve):
            dve.wait_ge(loaded, 32)
            with dve.Fori(0, NTURN) as t:
                link = Link(dve, chain, t, 2 * 4)
                for b in range(4):
                    dve.wait_ge(scaled, t * 4 + b + 1)
                    dve.scalar_tensor_tensor(mixed[b][:, :], got[b][1][:, :], routed.gate[:, 1, bass.ds(t * 4 + b, 1)],
                                             mixed[b][:, :], ALU.mult, ALU.add).then_inc(mixed_ready, 1)
                    dve.wait_ge(mixed_ready, t * 4 + b + 1)
                    link(dve.bn_stats(stats[:, b, :], mixed[b][:, :]))
                    dve.memset(idle[:, :], 0.0)
                    link(dve.bn_aggr(mean_var[:, b, :], stats[:, b, :]))
                    dve.tensor_scalar(rstd[:, b:b + 1], mean_var[:, b, 1:2], 1e-6, None, ALU.add).then_inc(var_ready, 1)
                link.end()
                for b in range(4):
                    dve.wait_ge(rstd_ready, t * 4 + b + 1)
                    dve.tensor_scalar(mixed[b][:, :], mixed[b][:, :], mean_var[:, b, 0:1], rstd[:, b:b + 1],
                                      ALU.subtract, ALU.mult).then_inc(normed, 1)
                    dve.wait_ge(normed, t * 4 + b + 1)
                    dve.tensor_tensor(mixed[b][:, :], mixed[b][:, :], gain[:, :], ALU.mult).then_inc(gained, 1)
                    dve.wait_ge(gained, t * 4 + b + 1)
                    dve.tensor_tensor(mixed[b][:, :], mixed[b][:, :], offset[:, :], ALU.add).then_inc(affine, 1)


def output_experts(nc, net, w2_dram, b2_dram, hidden_dram, rows_dram):
    E, FF, Q, FC = 24, 512, 3, 4
    with ExitStack() as ctx:
        def sb(n, shape, dt=F32):
            return ctx.enter_context(nc.sbuf_tensor(f"L1o_{n}", shape, dt))

        def sem(n):
            return net.sem(f"L1o_{n}")

        w2 = [sb(f"w2{i}", [P, FC, P]) for i in range(2)]; b2 = [sb(f"b2{i}", [P, P]) for i in range(2)]
        hid = [sb(f"hid{i}", [P, Q, FF]) for i in range(2)]
        hT = [sb(f"hT{i}", [P, Q, FC, P]) for i in range(2)]; y = [sb(f"y{i}", [P, Q, P]) for i in range(2)]
        turn_bank, y_bank = net.banks[0:6], net.banks[6:8]
        loaded = [sem(f"loaded{i}") for i in range(2)]; stored = [sem(f"stored{i}") for i in range(2)]
        hT_ps, hT_ready, y_ready, y_out = (sem(n) for n in ("hT_ps", "hT_ready", "y_ready", "y_out"))
        slots = hidden_dram[0:SLOTS_1, :].rearrange("(e q p) f -> e p q f", p=P, q=Q)
        outs = rows_dram[0:SLOTS_1, :].rearrange("(e q p) d -> e p q d", p=P, q=Q)
        block = ctx.enter_context(nc.Block())

        @block.sync
        def _(sp):
            with sp.Fori(0, E // 2) as i:
                for par in range(2):
                    e = i * 2 + par
                    sp.wait_ge(y_out, i * 2)
                    sp.dma_start(hid[par][:, :, :], slots[e, :, :, :]).then_inc(loaded[par], 16)
                    sp.dma_start(w2[par][:, :, :], w2_dram[:, e, :, :]).then_inc(loaded[par], 16)
                    sp.dma_start(b2[par][:, :], b2_dram[bass.ds(e, 1), :].to_broadcast([P, P])).then_inc(loaded[par], 16)

        @block.gpsimd
        def _(pool):
            with pool.Fori(0, E // 2) as i:
                for par in range(2):
                    e = i * 2 + par
                    pool.wait_ge(y_out, e + 1)
                    pool.dma_start(outs[e, :, :, :], y[par][:, :, :]).then_inc(stored[par], 16)
            for par in range(2):
                pool.wait_ge(stored[par], E // 2 * 16)

        @block.scalar
        def _(act):
            with act.Fori(0, E // 2) as i:
                for par in range(2):
                    for q in range(Q):
                        act.wait_ge(hT_ps, (i * 2 + par) * Q + q + 1)
                        act.copy(hT[par][:, q, :, :], turn_bank[par * Q + q][:, :].rearrange("p (c t) -> p c t", c=FC)
                                 ).then_inc(hT_ready, 1)

        @block.vector
        def _(dve):
            with dve.Fori(0, E // 2) as i:
                for par in range(2):
                    dve.wait_ge(stored[par], i * 16)
                    dve.wait_ge(y_ready, i * 2 + par + 1)
                    dve.tensor_tensor(y[par][:, :, :], y_bank[par][:, 0:Q * P].rearrange("p (q d) -> p q d", q=Q),
                                      b2[par][:, :].unsqueeze(1).to_broadcast([P, Q, P]), ALU.add).then_inc(y_out, 1)

        @block.tensor
        def _(pe):
            with pe.Fori(0, E // 2) as i:
                for par in range(2):
                    pe.wait_ge(loaded[par], 48 * (i + 1))
                    for q in range(Q):
                        for c in range(FC):
                            last = pe.transpose(turn_bank[par * Q + q][:, c * P:(c + 1) * P],
                                                hid[par][:, q, c * P:(c + 1) * P], net.ident[:, :])
                        last.then_inc(hT_ps, 1)
                for par in range(2):
                    pe.wait_ge(hT_ready, (i * 2 + par + 1) * Q)
                    pe.wait_ge(y_out, i * 2)
                    for q in range(Q):
                        for c in range(FC):
                            last = pe.matmul(y_bank[par][:, q * P:(q + 1) * P], hT[par][:, q, c, :], w2[par][:, c, :],
                                             start=(c == 0), stop=(c == FC - 1))
                    last.then_inc(y_ready, 1)


def capacity_moe_stage(nc, net):
    with ExitStack() as ctx:
        t = net.t
        routed = Routed(nc, ctx, "L1f")
        with ExitStack() as part:
            logits = part.enter_context(nc.sbuf_tensor("L1f_logits", [P, 24, NBATCH], F32))
            norm_and_logits(nc, net, "L1f", 24, t["L1f_wg"], routed, logits)
            route(nc, net, "L1f", 24, 86, dict(lower=t["lower32"], whole=t["ones32"], reset=t["reset24"],
                                               base=t["base24"]), routed, logits)
        scatter_rows(nc, net, "L1f", routed, net.slots1, SLOTS_1)
        hidden_experts(nc, net, t["L1f_w1"], t["L1f_b1"], net.slots1, net.hidden1)
        mix_hidden(nc, net, t["L1f_gain"], t["L1f_offset"], routed, net.hidden1)
        output_experts(nc, net, t["L1f_w2"], t["L1f_b2"], net.hidden1, net.rows1)
        combine_rows(nc, net, "L1f", routed, net.rows1, SLOTS_1 + 1, (t["L1f_out_w"], t["L1f_out_b"]))


def fill_zeros(nc, net):
    with ExitStack() as ctx:
        zeros = ctx.enter_context(nc.sbuf_tensor("zeros", [P, SLOTS_1 // 4], F32))
        zeroed, filled = net.sem("zeroed"), net.sem("zeros_filled")
        with nc.Block() as block:
            @block.vector
            def _(dve):
                dve.memset(zeros[:, :], 0.0).then_inc(zeroed, 1)

            @block.sync
            def _(sp):
                sp.wait_ge(zeroed, 1)
                slots = net.slots1.rearrange("(a p r) d -> a p (r d)", a=4, p=P)
                for a in range(4):
                    sp.dma_start(slots[a, :, :], zeros[:, :]).then_inc(filled, 16)
                sp.dma_start(net.hidden1[SLOTS_1:SLOTS_1 + 1, :], zeros[0:1, 0:512]).then_inc(filled, 16)
                sp.dma_start(net.rows1[SLOTS_1:SLOTS_1 + 1, :], zeros[0:1, 0:P]).then_inc(filled, 16)
                sp.wait_ge(filled, 96)


def build(nc, t, out, stages):
    with ExitStack() as ctx:
        net = Net(nc, ctx)
        net.x = net.sb("x", [P, NBATCH, P])
        net.ident = net.sb("ident", [P, P])
        net.index64 = net.sb("index64", [P, 24])
        net.ones_row = net.sb("ones_row", [1, P])
        net.minus_half = net.sb("minus_half", [P, NBATCH])
        net.plus_half = net.sb("plus_half", [P, NBATCH])
        banks = [ctx.enter_context(nc.psum_tensor(f"bank{i}", [P, 512], F32)) for i in range(8)]
        net.banks = banks
        net.t = t
        net.slots2 = nc.dram_tensor("slots2", (SLOTS_2, P), F32).ap()
        net.slots1 = nc.dram_tensor("slots1", (SLOTS_1, P), F32).ap()
        net.hidden1 = nc.dram_tensor("hidden1", (SLOTS_1 + 1, 512), F32).ap()
        net.rows1 = nc.dram_tensor("rows1", (SLOTS_1 + 1, P), F32).ap()
        net.rows2 = nc.dram_tensor("rows2", (SLOTS_2, P), F32).ap()
        loaded = net.sem("start_loaded")
        with nc.Block() as block:
            @block.sync
            def _(sp):
                sp.dma_start(net.x[:, :, :], t["x"]).then_inc(loaded, 16)
                sp.dma_start(net.ident[:, :], t["ident"]).then_inc(loaded, 16)
                sp.dma_start(net.index64[:, :], t["index64"]).then_inc(loaded, 16)
                sp.wait_ge(loaded, 48)

            @block.vector
            def _(dve):
                dve.memset(net.ones_row[:, :], 1.0)
                dve.memset(net.minus_half[:, :], -0.5)
                dve.memset(net.plus_half[:, :], 0.5)

        if "L1f" in stages:
            fill_zeros(nc, net)

        def attention(layer, kind, heads, hd, biased, names):
            with ExitStack() as part:
                if kind == "cross":
                    net.ctxT = part.enter_context(nc.sbuf_tensor(f"{layer}_ctxT", [CTX, NBATCH, NKEY], F32))
                    got = net.sem(f"{layer}_ctx_loaded")
                    with nc.Block() as block:
                        @block.sync
                        def _(sp):
                            sp.dma_start(net.ctxT[:, :, :], t["ctxT"]).then_inc(got, 16)
                            sp.wait_ge(got, 16)
                spec = dict(name=layer, kind=kind, heads=heads, hd=hd, biased=biased)
                w = {k: t[v] for k, v in names.items()}
                w["diag"] = t["diag"]
                attention_stage(nc, net, spec, w)

        if "L0x" in stages:
            attention("L0x", "cross", 16, 8, True,
                      dict(wq="L0_xattn_q_w", wk="L0k", wv="L0v", wo="L0o", bo="L0_xattn_proj_b",
                           bq="L0_xattn_q_b", bk="L0kb", bv="L0vb"))
        net.release_semaphores()
        if "L0f" in stages:
            dense_moe_stage(nc, net, dict(name="L0f", FF=512, kind="pre"), {k: t["L0f_" + k] for k in (
                "w1", "w2", "b1", "b2", "wg", "bg", "g_col", "b_col")})
        net.release_semaphores()
        if "L1x" in stages:
            attention("L1x", "cross", 16, 64, False,
                      dict(wq="L1_xattn_Wq", wk="L1_xattn_Wk", wv="L1_xattn_Wv", wo="L1o", bo="L1_xattn_bo"))
        net.release_semaphores()
        if "L1f" in stages:
            capacity_moe_stage(nc, net)
        net.release_semaphores()
        if "L2x" in stages:
            attention("L2x", "latent", 2, 64, False,
                      dict(wq="L2q", wlkv="L2lkv", wkv="L2kv", gamma="L2gamma", lat_g="L2lg", lat_b="L2lb",
                           ctx_g="L2xg", ctx_b="L2xb", ctx_tok="ctx_tok", mask="mask", wo="L2o", bo="L2_xattn_bo"))
        net.release_semaphores()
        if "L2f" in stages:
            chunked_moe_stage(nc, net)
        net.release_semaphores()
        if "L3x" in stages:
            attention("L3x", "cross", 8, 64, False,
                      dict(wq="L3_xattn_Wq", wk="L3_xattn_Wk", wv="L3_xattn_Wv", wo="L3o", bo="L3_xattn_bo"))
        net.release_semaphores()
        if "L3f" in stages:
            with ExitStack() as part:
                net.x1 = part.enter_context(nc.sbuf_tensor("x1", [P, NBATCH, P], F32))
                attention("L3s", "self", 16, 8, True,
                          {k: "L3s_" + k for k in ("wq", "wk", "wv", "wo", "bo", "bq", "bk", "bv")})
                dense_moe_stage(nc, net, dict(name="L3f", FF=256, kind="post"), {k: t["L3f_" + k] for k in (
                    "w1", "w2", "b1", "b2", "wg", "bg", "g_col", "b_col", "g1", "be1", "g2", "be2")})
        net.release_semaphores()
        stored = net.sem("stored")
        with nc.Block() as block:
            @block.sync
            def _(sp):
                sp.dma_start(out, net.x[:, :, :]).then_inc(stored, 16)
                sp.wait_ge(stored, 16)


def constants():
    p = np.arange(P)
    c = {"ident": np.eye(P, dtype=np.float32)}
    c["diag"] = (p[:, None] // 8 % 4 == np.arange(4)[None, :]).astype(np.float32)

    group = p // 32
    c["lower"] = (p[:, None] < p[None, :]).astype(np.float32)
    c["ones"] = np.ones((P, P), np.float32)
    c["lower32"] = c["lower"] * (group[:, None] == group[None, :])
    c["ones32"] = (group[:, None] == group[None, :]).astype(np.float32)
    for e in (8, 24):
        c[f"reset{e}"] = np.broadcast_to((np.arange(NBATCH) > 0).astype(np.float32), (P, e, NBATCH))
    c["base8"] = np.zeros((P, 8), np.float32)
    c["base24"] = (np.arange(24)[None, :] * 384 + group[:, None] * 86).astype(np.float32)
    c["index64"] = np.broadcast_to(np.arange(24, dtype=np.float32) - 64, (P, 24))
    return c


def layouts(i):
    a = {"x": i["x"].transpose(1, 0, 2), "ctxT": i["ctx_768"].transpose(2, 0, 1)}
    a["L0_xattn_q_w"] = i["L0_xattn_q_w"]
    a["L0k"], a["L0v"] = i["L0_xattn_kv_w"][:, :P], i["L0_xattn_kv_w"][:, P:]
    a["L0kb"], a["L0vb"] = i["L0_xattn_kv_b"][:P, None], i["L0_xattn_kv_b"][None, P:]
    a["L0_xattn_q_b"] = i["L0_xattn_q_b"][:, None]
    a["L0o"] = i["L0_xattn_proj_w"][:, None, :]
    a["L0_xattn_proj_b"] = i["L0_xattn_proj_b"][None, :]
    for n, key in (("L1", "L1o"), ("L3", "L3o")):
        for k in ("Wq", "Wk", "Wv"):
            a[f"{n}_xattn_{k}"] = i[f"{n}_xattn_{k}"]
        wo = i[f"{n}_xattn_Wo"]
        a[key] = wo.reshape(-1, P, P).transpose(1, 0, 2)
        a[f"{n}_xattn_bo"] = i[f"{n}_xattn_bo"][None, :]
    f = {k: i[f"L0_ffn_{k}"] for k in ("W1", "W2", "b1", "b2", "Wg", "bg", "gamma", "beta")}
    a["L0f_w1"] = f["W1"].transpose(2, 0, 1)
    a["L0f_w2"] = f["W2"].reshape(8, P, 4, P).transpose(3, 0, 2, 1)
    a["L0f_b1"] = f["b1"].reshape(8 * 4, P).T
    a["L0f_b2"], a["L0f_wg"], a["L0f_bg"] = f["b2"], f["Wg"].T, f["bg"][None, :]
    a["L0f_g_col"], a["L0f_b_col"] = f["gamma"][:, None], f["beta"][:, None]
    s = {k[7:]: v for k, v in i.items() if k.startswith("L3_ffn_")}
    for k in ("q", "k", "v"):
        a[f"L3s_w{k}"] = s[f"W{k}"]
        a[f"L3s_b{k}"] = s[f"b{k}"][None, :] if k == "v" else s[f"b{k}"][:, None]
    a["L3s_wo"], a["L3s_bo"] = s["Wo"][:, None, :], s["bo"][None, :]
    a["L3f_w1"] = s["W1"].transpose(1, 0, 2)
    a["L3f_w2"] = s["W2"].reshape(8, 2, P, P).transpose(2, 0, 1, 3)
    a["L3f_b1"] = s["b1"].reshape(8 * 2, P).T
    a["L3f_b2"], a["L3f_wg"], a["L3f_bg"] = s["b2"], s["gW"], s["gb"][None, :]
    a["L3f_g_col"], a["L3f_b_col"] = s["ln1_g"][:, None], s["ln1_b"][:, None]
    for k, n in (("g1", "ln1_g"), ("be1", "ln1_b"), ("g2", "ln2_g"), ("be2", "ln2_b")):
        a["L3f_" + k] = np.broadcast_to(s[n], (P, P))
    a["L2f_wg"] = i["L2_ffn_router_w"].T
    a["L2f_w1"] = i["L2_ffn_w1"].transpose(1, 0, 2)
    a["L2f_w2"] = i["L2_ffn_w2"].reshape(8, 4, P, P).transpose(2, 0, 1, 3)
    s = {k[7:]: v for k, v in i.items() if k.startswith("L1_ffn_")}
    a["L1f_wg"], a["L1f_w1"], a["L1f_b1"], a["L1f_b2"] = s["Wg"], s["W1"].transpose(1, 0, 2), s["b1"], s["b2"]
    a["L1f_w2"] = s["W2"].reshape(24, 4, P, P).transpose(2, 0, 1, 3)
    a["L1f_gain"], a["L1f_offset"] = (np.repeat(s[n], 32, axis=0) for n in ("ln_hid_w", "ln_hid_b"))
    a["L1f_out_w"], a["L1f_out_b"] = (np.broadcast_to(s[n], (P, P)) for n in ("ln_out_w", "ln_out_b"))
    a["ctx_tok"] = i["ctx_768"].transpose(1, 0, 2)
    a["mask"] = i["mask_BxS2_bk0"].reshape(1, -1)
    a["L2q"], a["L2kv"], a["L2lkv"] = i["L2_xattn_Wq"].T, i["L2_xattn_Wkv"].T, i["L2_xattn_Wlkv"].T
    a["L2o"] = i["L2_xattn_Wo"].T[:, None, :]
    a["L2_xattn_bo"] = i["L2_xattn_bo"][None, :]
    gq, gk = i["L2_xattn_qn_g"], i["L2_xattn_kn_g"]
    a["L2gamma"] = np.broadcast_to(np.stack([gq, gq, gk, gk]), (P, 4, 64))
    for key, n in (("L2lg", "ln_l_g"), ("L2lb", "ln_l_b"), ("L2xg", "ln_x_g"), ("L2xb", "ln_x_b")):
        a[key] = i[f"L2_xattn_{n}"][:, None]
    return a


STAGES = ("L0x", "L0f", "L1x", "L1f", "L2x", "L2f", "L3x", "L3f")


def program(nc, arrays, stages=STAGES):
    t = {n: nc.dram_tensor(f"in_{n}", a.shape, mybir.dt.from_np(a.dtype), kind="ExternalInput").ap()
         for n, a in arrays.items()}
    out = nc.dram_tensor("out_x", (P, NBATCH, P), F32, kind="ExternalOutput").ap()
    build(nc, t, out, stages)


def kernel(**inputs):
    import concourse.bacc as _bacc
    from concourse.bass_utils import run_bass_kernel_spmd as _run

    arrays = {n: np.ascontiguousarray(a) for n, a in {**layouts(inputs), **constants()}.items()}
    nc = _bacc.Bacc("TRN2", target_bir_lowering=False, num_devices=1)
    program(nc, arrays)
    r = _run(nc, [{f"in_{n}": a for n, a in arrays.items()}], core_ids=[0])
    return np.ascontiguousarray(r.results[0]["out_x"].transpose(1, 0, 2))
```

```python
from contextlib import ExitStack

import numpy as np

import concourse.bass as bass
from concourse import mybir

F32 = mybir.dt.float32
BF16 = mybir.dt.bfloat16
U8 = mybir.dt.uint8
U32 = mybir.dt.uint32
I32 = mybir.dt.int32
ALU = mybir.AluOpType
ACT = mybir.ActivationFunctionType
AX_X = mybir.AxisListType.X

P = 128
NBATCH = 32
NTURN = NBATCH // 4
NKEY = 77
CTX = 96
EPS = 1e-5


class Link:

    def __init__(self, eng, sem, turn, length):
        self.eng, self.sem, self.turn, self.length, self.count = eng, sem, turn, length, 0

    def __call__(self, instruction):
        self.count += 1
        instruction.then_inc(self.sem, 1)
        self.eng.wait_ge(self.sem, self.turn * self.length + self.count)

    def end(self):
        assert self.count == self.length, (self.count, self.length)


class Net:

    def __init__(self, nc, ctx):
        self.nc, self.ctx = nc, ctx
        self.semaphores = []

    def sb(self, name, shape, dt=F32):
        return self.ctx.enter_context(self.nc.sbuf_tensor(name, shape, dt))

    def sem(self, name):
        self.semaphores.append(self.nc.alloc_semaphore(name))
        return self.semaphores[-1]

    def release_semaphores(self):
        self.nc.all_engine_barrier()
        self.nc.clear_and_free_semaphores(self.semaphores)
        self.nc.all_engine_barrier()
        self.semaphores = []


def over_turns(eng, body):
    with eng.Fori(0, NTURN // 2 - 1) as i:
        for par in range(2):
            body(i * 2 + par, par, i, None)
    for par in range(2):
        body(NTURN - 2 + par, par, NTURN // 2 - 1, par)


def attention_stage(nc, net, spec, w):
    name, heads, hd, kind, biased = (spec[k] for k in ("name", "heads", "hd", "kind", "biased"))
    scale = float(hd) ** -0.5
    inner = heads * hd
    NC = inner // P
    NK = {"cross": NKEY, "self": P}[kind]
    U = 4
    NU = heads // U
    NP = (NC + 3) // 4

    with ExitStack() as ctx:
        def sb(n, shape, dt=F32):
            return ctx.enter_context(nc.sbuf_tensor(f"{name}_{n}", shape, dt))

        def sem(n):
            return net.sem(f"{name}_{n}")

        x = net.x
        dst = net.x1 if kind == "self" else net.x
        ident, ones_row = net.ident, net.ones_row
        score_bank, turn_bank, prep_bank = net.banks[0:2], net.banks[2:4], net.banks[4:6]
        out_bank = net.banks[6:6 + NP]
        proj_bank = net.banks[6 if NP == 2 else 7]

        KD = P if kind == "self" else CTX
        wq = sb("wq", [P, inner]); wk = sb("wk", [KD, inner]); wv = sb("wv", [KD, inner])
        wo = sb("wo", [P, NC, P]); bo = sb("bo", [1, P])
        loads = [(wk[:, :], w["wk"]), (wq[:, :], w["wq"]), (wv[:, :], w["wv"]), (wo[:, :, :], w["wo"]),
                 (bo[:, :], w["bo"])]
        if biased:
            bq = sb("bq", [P, 1]); bk = sb("bk", [P, 1]); bv = sb("bv", [1, P])
            loads += [(bq[:, :], w["bq"]), (bk[:, :], w["bk"]), (bv[:, :], w["bv"])]
        if hd == 8:
            diag = sb("diag", [P, 4]); loads.append((diag[:, :], w["diag"]))

        stats = sb("stats", [P, 4, 6]); mean_var = sb("mean_var", [P, 4, 2]); rstd = sb("rstd", [P, 4])
        idle = sb("idle", [P, 1])
        xn = [sb(f"xn{i}", [P, 4, P]) for i in range(2)]; xT = sb("xT", [P, 4 * P])
        qT = [sb(f"qT{i}", [P, NC, 4 * P]) for i in range(2)]
        if kind == "cross":
            ctxg = [sb(f"ctxg{i}", [CTX, 4, NKEY]) for i in range(2)]
        if hd == 8:
            kbd = [sb(f"kbd{i}", [P, 4, 4, NK]) for i in range(2)]
            vals = [sb(f"vals{i}", [NK, 4, heads, 32]) for i in range(2)]
        else:
            kbd = [sb(f"kbd{i}", [P, NC, 4, 2, NK]) for i in range(2)]
            vals = [sb(f"vals{i}", [NK, 4, inner]) for i in range(2)]
        soft = [sb(f"soft{i}", [P, heads, NK]) for i in range(4)]
        mx = [sb(f"mx{i}", [P, U]) for i in range(2)]
        rsum = [sb(f"rsum{i}", [P, heads]) for i in range(2)]
        rinv = [sb(f"rinv{i}", [P, heads]) for i in range(2)]
        probsT = [sb(f"probsT{i}", [NK, 4, P]) for i in range(2)]
        attnT = sb("attnT", [P, NC, P])

        loaded, constants, chain = sem("loaded"), sem("constants"), sem("chain")
        var_ready, rstd_ready, normed = sem("var_ready"), sem("rstd_ready"), sem("normed")
        ctx_loaded = [sem(f"ctx_loaded{i}") for i in range(2)]
        job_ready, job_out = sem("job_ready"), [sem(f"job_out{i}") for i in range(2)]
        scores_ready, max_ready, shifted = sem("scores_ready"), sem("max_ready"), sem("shifted")
        exp_done, sum_ready, inv_ready, probs_ready = sem("exp_done"), sem("sum_ready"), sem("inv_ready"), sem("probs_ready")
        turned, turned_out, values_done = sem("turned"), sem("turned_out"), sem("values_done")
        attnT_ready, proj_done, added = sem("attnT_ready"), sem("proj_done"), sem("added")

        if inner == P:
            vjobs = [([0, 1, 2, 3], 0, P)]
        else:
            vjobs = [([b], c, 512) for b in range(4) for c in range(0, inner, 512)]
        first = [("x", 0)] + [(k, c) for c in range(NC) for k in ("k", "q")]
        jobs = [(j, *job) for j, job in enumerate(first + [("v", v) for v in range(len(vjobs))])]
        J, JF = len(jobs), len(first)

        def taken(turn, count):
            return [turn * ((J + 1 - i) // 2) + (count + 1 - i) // 2 for i in range(2)]

        def between(b, final):
            if final == 1:
                return [[] for _ in range(2 * NU)]
            some, at = (jobs[:JF], b) if b < 2 else (jobs[JF:], b - 2)
            cut = [len(some) * i // (4 * NU) for i in range(4 * NU + 1)]
            return [some[cut[i]:cut[i + 1]] for i in range(2 * NU * at, 2 * NU * (at + 1))]

        def steps(final):
            return [(b, final != 1 or b < 2, final != 1 or b < 3) for b in range(4)]

        def shift(dve, g, unit, tile, later):
            n = g * NU + unit
            ps = score_bank[unit % 2][:, 0:U * NK].rearrange("p (h k) -> p h k", h=U)
            dve.wait_ge(scores_ready, n + 1)
            if unit >= 2 or later:
                dve.wait_ge(shifted, n - 1)
            dve.tensor_reduce(mx[unit % 2][:, :], ps, AX_X, ALU.max).then_inc(max_ready, 1)
            dve.wait_ge(max_ready, n + 1)
            dve.tensor_tensor(tile[:, unit * U:(unit + 1) * U, :], ps,
                              mx[unit % 2][:, :].unsqueeze(2).to_broadcast([P, U, NK]),
                              ALU.subtract).then_inc(shifted, 1)

        def row_sums(dve, g, tile, two, reused):
            dve.wait_ge(exp_done, g + 1)
            if reused:
                dve.wait_ge(probs_ready, g - 1)
            dve.tensor_reduce(rsum[two][:, :], tile[:, :, :], AX_X, ALU.add).then_inc(sum_ready, 1)
            dve.wait_ge(sum_ready, g + 1)
            dve.reciprocal(rinv[two][:, :], rsum[two][:, :]).then_inc(inv_ready, 1)

        def variances(dve, turn):
            link = Link(dve, chain, turn, 2)
            for b in range(4):
                last = dve.bn_stats(stats[:, b, :], x[:, turn * 4 + b, :])
            link(last)
            dve.memset(idle[:, :], 0.0)
            for b in range(4):
                last = dve.bn_aggr(mean_var[:, b, :], stats[:, b, :])
            link(last)
            dve.tensor_scalar(rstd[:, :], mean_var[:, :, 1], EPS, None, ALU.add).then_inc(var_ready, 1)

        def normalize(dve, turn, par):
            dve.wait_ge(rstd_ready, turn + 1)
            for b in range(4):
                last = dve.tensor_scalar(xn[par][:, b, :], x[:, turn * 4 + b, :], mean_var[:, b, 0:1],
                                         rstd[:, b:b + 1], ALU.subtract, ALU.mult)
            last.then_inc(normed, 1)

        def take_keys(dve, turn, par, job):
            j, what, c = job
            if what != "k":
                return
            kps = prep_bank[j % 2][:, 0:4 * NK].rearrange("p (b k) -> p b k", b=4)
            dve.wait_ge(job_ready, turn * J + j + 1)
            if hd == 8:
                for b in range(4):
                    last = dve.scalar_tensor_tensor(
                        kbd[par][:, b, :, :], kps[:, b:b + 1, :].to_broadcast([P, 4, NK]), bk[:, 0:1],
                        diag[:, :].unsqueeze(2).to_broadcast([P, 4, NK]), ALU.add, ALU.mult)
            else:
                dve.tensor_copy(kbd[par][0:64, c, :, 0, :], kps[0:64, :, :])
                last = dve.tensor_copy(kbd[par][64:P, c, :, 1, :], kps[64:P, :, :])
            last.then_inc(job_out[j % 2], 1)

        def take_others(act, turn, par, job):
            j, what, c = job
            bank = prep_bank[j % 2]
            if what == "k":
                return
            act.wait_ge(job_ready, turn * J + j + 1)
            if what == "x":
                last = act.copy(xT[:, :], bank[:, :])
            elif what == "q" and biased:
                last = act.activation(qT[par][:, c, :], bank[:, :], ACT.Identity, bias=bq[:, 0:1])
            elif what == "q":
                last = act.copy(qT[par][:, c, :], bank[:, :])
            elif hd == 8:
                ps = bank[0:NK, :].rearrange("p (b r j d) -> p b r j d", b=4, r=4, j=4)
                out = vals[par][:, :, :, :].rearrange("p b (r j) d -> p b r j d", j=4)
                for i in range(4):
                    for b in range(4):
                        last = act.copy(out[:, b, :, i, 8 * i:8 * i + 8], ps[:, b, :, i, :])
            else:
                bs, c0, cols = vjobs[c]
                last = act.copy(vals[par][:, bs[0], c0:c0 + cols], bank[0:NK, :])
            last.then_inc(job_out[j % 2], 1)

        def do_job(pe, turn, par, half, job):
            j, what, c = job
            pe.wait_ge(job_out[j % 2], taken(turn, j)[j % 2])
            bank = prep_bank[j % 2]
            src = [xT[:, b * P:(b + 1) * P] if kind == "self" else ctxg[par][:, b, :] for b in range(4)]
            if what == "x":
                pe.wait_ge(normed, turn + 1)
                for b in range(4):
                    last = pe.transpose(bank[:, b * P:(b + 1) * P], xn[par][:, b, :], ident[:, :])
            elif what == "k":
                if kind == "self" and c == 0:
                    pe.wait_ge(job_out[0], taken(turn, 1)[0])
                if kind == "cross" and c == 0:
                    pe.wait_ge(ctx_loaded[par], (half + 1) * 16)
                last = pe.matmul(bank[:, 0:4 * NK], wk[:, c * P:(c + 1) * P],
                                 xT[:, :] if kind == "self" else ctxg[par][:, :, :], start=True, stop=True)
            elif what == "q":
                if c == 0:
                    pe.wait_ge(job_out[0], taken(turn, 1)[0])
                last = pe.matmul(bank[:, :], wq[:, c * P:(c + 1) * P], xT[:, :], start=True, stop=True)
            else:
                bs, c0, cols = vjobs[c]
                for i, b in enumerate(bs):
                    out = bank[0:NK, i * cols:(i + 1) * cols]
                    last = pe.matmul(out, src[b], wv[:, c0:c0 + cols], start=True, stop=not biased)
                    if biased:
                        last = pe.matmul(out, ones_row[:, 0:NK], bv[:, :], start=False, stop=True)
            last.then_inc(job_ready, 1)

        def scores(pe, g, b, par, u, later):
            bank = score_bank[u % 2]
            if u >= 2 or later:
                pe.wait_ge(shifted, g * NU + u - 1)
            if hd == 8:
                last = pe.matmul(bank[:, 0:U * NK], qT[par][32 * u:32 * u + 32, 0, b * P:(b + 1) * P],
                                 kbd[par][32 * u:32 * u + 32, b, :, :], start=True, stop=True)
            else:
                for c in range(u * 2, u * 2 + 2):
                    at = (c - u * 2) * 2 * NK
                    last = pe.matmul(bank[:, at:at + 2 * NK], qT[par][:, c, b * P:(b + 1) * P],
                                     kbd[par][:, c, b, :, :], start=True, stop=True)
            last.then_inc(scores_ready, 1)

        def turn_unit(pe, g, b, u):
            if u == 0:
                pe.wait_ge(probs_ready, g + 1)
            for i in range(U):
                last = pe.transpose(turn_bank[u % 2][0:NK, i * P:(i + 1) * P], soft[b][:, u * U + i, :], ident[:, :])
            last.then_inc(turned, 1)

        def values(pe, g, b, par, u):
            pe.wait_ge(turned_out, g * NU + u + 1)
            if NP == 2 and u == 0:
                pe.wait_ge(added, g)
            for i in range(U):
                h = u * U + i
                if hd == 8:
                    last = pe.matmul(out_bank[0][32 * u:32 * u + 32, 0:P], vals[par][:, b, h, :],
                                     probsT[u % 2][:, i, :], start=(i == 0), stop=(i == U - 1))
                else:
                    c = h // 2
                    out = out_bank[c // 4][64 * (h % 2):64 * (h % 2) + 64, c % 4 * P:(c % 4 + 1) * P]
                    last = pe.matmul(out, vals[par][:, b, h * 64:(h + 1) * 64], probsT[u % 2][:, i, :],
                                     start=True, stop=True)
            last.then_inc(values_done, 1)

        def project(pe, g):
            pe.wait_ge(attnT_ready, (g + 1) * NP)
            pe.wait_ge(added, g)
            pe.matmul(proj_bank[:, 0:P], ones_row[:, :], bo[:, :], start=True, stop=False)
            for c in range(NC):
                last = pe.matmul(proj_bank[:, 0:P], attnT[:, c, :], wo[:, c, :], start=False, stop=(c == NC - 1))
            last.then_inc(proj_done, 1)

        def take_attention(act, g, b, p):
            nch = min(4, NC - 4 * p)
            act.wait_ge(values_done, g * NU + (p + 1) * (NU // NP))
            act.copy(attnT[:, 4 * p:4 * p + nch, :],
                     out_bank[p][:, 0:nch * P].rearrange("p (c t) -> p c t", c=nch)
                     ).then_inc(attnT_ready, 1)

        def exponents(act, g, tile):
            flat = tile[:, :, :].rearrange("p h k -> p (h k)")
            act.wait_ge(shifted, (g + 1) * NU)
            act.activation(flat, flat, ACT.Exp, scale=scale).then_inc(exp_done, 1)

        def weigh(pool, g, tile, two):
            pool.wait_ge(inv_ready, g + 1)
            pool.tensor_tensor(tile[:, :, :], tile[:, :, :], rinv[two][:, :].unsqueeze(2).to_broadcast([P, heads, NK]),
                               ALU.mult).then_inc(probs_ready, 1)

        block = ctx.enter_context(nc.Block())

        @block.sync
        def _(sp):
            def load_context(turn, par):
                sp.dma_start(ctxg[par][:, :, :], w["ctxT"][:, bass.ds(turn * 4, 4), :]).then_inc(ctx_loaded[par], 16)

            if kind == "cross":
                load_context(0, 0)
            for dst_ap, src in loads:
                sp.dma_start(dst_ap, src).then_inc(loaded, 16)
            if kind == "cross":
                load_context(1, 1)
                with sp.Fori(1, NTURN // 2) as i:
                    for par in range(2):
                        sp.wait_ge(job_ready, (i * 2 + par - 1) * J)
                        load_context(i * 2 + par, par)

        @block.gpsimd
        def _(pool):
            def invert_root(turn):
                pool.wait_ge(var_ready, turn + 1)
                pool.tensor_tensor(rstd[:, :], rstd[:, :], net.minus_half[:, 0:4], ALU.pow).then_inc(rstd_ready, 1)

            if hd == 8:
                pool.memset(vals[0][:, :, :, :], 0.0)
                pool.memset(vals[1][:, :, :, :], 0.0).then_inc(constants, 1)
            else:
                for tile in kbd:
                    pool.memset(tile[0:64, :, :, 1, :], 0.0)
                    last = pool.memset(tile[64:P, :, :, 0, :], 0.0)
                last.then_inc(constants, 1)
            pool.wait_ge(constants, 1)
            for t in range(2):
                invert_root(t)
            weigh(pool, 0, soft[0], 0)

            def body(turn, par, pair, final):
                for b, _, one_more in steps(final):
                    if one_more:
                        weigh(pool, turn * 4 + b + 1, soft[(b + 1) % 4], (b + 1) % 2)
                    if b == 1 and final is None:
                        invert_root(turn + 2)

            over_turns(pool, body)

        @block.vector
        def _(dve):
            variances(dve, 0)
            normalize(dve, 0, 0)
            dve.wait_ge(normed, 1)
            variances(dve, 1)
            normalize(dve, 1, 1)
            dve.wait_ge(loaded, 16 * len(loads))
            dve.wait_ge(constants, 1)
            for job in jobs:
                take_keys(dve, 0, 0, job)
            for g in range(2):
                for u in range(NU):
                    shift(dve, g, u, soft[g], g > 0)
            row_sums(dve, 0, soft[0], 0, False)

            def body(turn, par, pair, final):
                for b, two_more, one_more in steps(final):
                    g = turn * 4 + b
                    slots = between(b, final)
                    for u in range(NU):
                        if two_more and u:
                            shift(dve, g + 2, u - 1, soft[(b + 2) % 4], True)
                        for job in slots[2 * u]:
                            take_keys(dve, turn + 1, 1 - par, job)
                        if u == 0 and one_more:
                            row_sums(dve, g + 1, soft[(b + 1) % 4], (b + 1) % 2, True)
                        if u < NU - 1:
                            for job in slots[2 * u + 1]:
                                take_keys(dve, turn + 1, 1 - par, job)
                    if two_more:
                        shift(dve, g + 2, NU - 1, soft[(b + 2) % 4], True)
                    for job in slots[-1]:
                        take_keys(dve, turn + 1, 1 - par, job)
                    dve.wait_ge(proj_done, g + 1)
                    inp = xn[par][:, b, :] if kind == "self" else x[:, g, :]
                    dve.tensor_tensor(dst[:, g, :], inp, proj_bank[:, 0:P], ALU.add).then_inc(added, 1)
                    if b == 1 and final is None:
                        dve.wait_ge(normed, turn + 2)
                        variances(dve, turn + 2)
                if final is None:
                    dve.wait_ge(added, (turn + 1) * 4)
                    normalize(dve, turn + 2, par)

            over_turns(dve, body)

        @block.scalar
        def _(act):
            act.wait_ge(loaded, 16 * len(loads))
            act.wait_ge(constants, 1)
            for job in jobs:
                take_others(act, 0, 0, job)
            for g in range(2):
                exponents(act, g, soft[g])

            def body(turn, par, pair, final):
                for b, two_more, _ in steps(final):
                    g = turn * 4 + b
                    slots = between(b, final)
                    for u in range(NU):
                        n = g * NU + u
                        act.wait_ge(turned, n + 1)
                        if u >= 2:
                            act.wait_ge(values_done, n - 1)
                        act.copy(probsT[u % 2][:, :, :], turn_bank[u % 2][0:NK, :].rearrange("p (m t) -> p m t", m=4)
                                 ).then_inc(turned_out, 1)
                        for job in slots[2 * u]:
                            take_others(act, turn + 1, 1 - par, job)
                        if NP == 2 and u == NU // 2:
                            take_attention(act, g, b, 0)
                        if u < NU - 1:
                            for job in slots[2 * u + 1]:
                                take_others(act, turn + 1, 1 - par, job)
                    take_attention(act, g, b, NP - 1)
                    for job in slots[-1]:
                        take_others(act, turn + 1, 1 - par, job)
                    if two_more:
                        exponents(act, g + 2, soft[(b + 2) % 4])

            over_turns(act, body)

        @block.tensor
        def _(pe):
            pe.wait_ge(loaded, 16 * len(loads))
            pe.wait_ge(constants, 1)
            for job in jobs:
                do_job(pe, 0, 0, 0, job)
            for i in range(2):
                pe.wait_ge(job_out[i], taken(0, J)[i])
            for g in range(2):
                for u in range(NU):
                    scores(pe, g, g, 0, u, g > 0)

            def body(turn, par, pair, final):
                for b, two_more, _ in steps(final):
                    g = turn * 4 + b
                    slots = between(b, final)

                    def fill(slot):
                        for job in slots[slot]:
                            do_job(pe, turn + 1, 1 - par, pair + par, job)

                    if b == 2 and final != 1:
                        for i in range(2):
                            pe.wait_ge(job_out[i], taken(turn + 1, JF)[i])
                    if b == 0:
                        for i in range(2):
                            pe.wait_ge(job_out[i], taken(turn, J)[i])

                    def scores_ahead(u):
                        if two_more:
                            scores(pe, g + 2, (b + 2) % 4, par if b < 2 else 1 - par, u, True)

                    for u in range(NU):
                        turn_unit(pe, g, b, u)
                        if u:
                            scores_ahead(u - 1)
                        fill(2 * u)
                        if u:
                            values(pe, g, b, par, u - 1)
                        if u < NU - 1:
                            fill(2 * u + 1)
                    values(pe, g, b, par, NU - 1)
                    scores_ahead(NU - 1)
                    fill(2 * NU - 1)
                    project(pe, g)

            over_turns(pe, body)


def latent_stage(nc, net, spec, w):
    name, heads, hd, kind, biased = (spec[k] for k in ("name", "heads", "hd", "kind", "biased"))
    scale = float(hd) ** -0.5
    inner = heads * hd
    NC = inner // P
    KEYS = {"cross": [NKEY], "self": [P], "latent": [NKEY, P]}[kind]
    NK = sum(KEYS)
    OFF = [0, NKEY][: len(KEYS)]
    U = min(4, heads)
    NU = heads // U
    NP = (NC + 3) // 4
    SLOTS = [(i, e) for i in range(U) for e in range(len(KEYS))]

    with ExitStack() as ctx:
        def sb(n, shape, dt=F32):
            return ctx.enter_context(nc.sbuf_tensor(f"{name}_{n}", shape, dt))

        def sem(n):
            return net.sem(f"{name}_{n}")

        x = net.x
        dst = net.x1 if kind == "self" else net.x
        ident, ones_row = net.ident, net.ones_row
        score_bank, turn_bank, out_bank, proj_bank = net.banks[0:3], net.banks[3:5], net.banks[5:7], net.banks[7]

        KD = P if kind == "self" else CTX
        wo = sb("wo", [P, NC, P]); bo = sb("bo", [1, P])
        loads = [(wo[:, :, :], w["wo"]), (bo[:, :], w["bo"])]
        if kind != "latent":
            wq = sb("wq", [P, inner]); wk = sb("wk", [KD, inner]); wv = sb("wv", [KD, inner])
            loads = [(wq[:, :], w["wq"]), (wk[:, :], w["wk"]), (wv[:, :], w["wv"])] + loads
        if biased:
            bq = sb("bq", [P, 1]); bk = sb("bk", [P, 1]); bv = sb("bv", [1, P])
            loads += [(bq[:, :], w["bq"]), (bk[:, :], w["bk"]), (bv[:, :], w["bv"])]
        if hd == 8:
            diag = sb("diag", [P, 4]); loads.append((diag[:, :], w["diag"]))

        if kind == "latent":
            wqkv_lat = sb("wqkv_lat", [P, 3 * P]); wkv_ctx = sb("wkv_ctx", [CTX, 2 * P])
            gamma = sb("gamma", [P, 4, 64]); lat_g = sb("lat_g", [P, 1]); lat_b = sb("lat_b", [P, 1])
            ctx_g = sb("ctx_g", [CTX, 1]); ctx_b = sb("ctx_b", [CTX, 1])
            ctx_tok = sb("ctx_tok", [NKEY, NBATCH, CTX])
            mask8 = sb("mask8", [1, NBATCH * NKEY], U8); mask_row = sb("mask_row", [1, NBATCH, 2, NK])
            loads += [(wqkv_lat[:, 0:P], w["wq"]), (wqkv_lat[:, P:3 * P], w["wlkv"]),
                      (wkv_ctx[:, :], w["wkv"]), (gamma[:, :, :], w["gamma"]), (lat_g[:, :], w["lat_g"]),
                      (lat_b[:, :], w["lat_b"]), (ctx_g[:, :], w["ctx_g"]), (ctx_b[:, :], w["ctx_b"]),
                      (ctx_tok[:, :, :], w["ctx_tok"]), (mask8[:, :], w["mask"])]

        stats = sb("stats", [P, 4, 6]); mean_var = sb("mean_var", [P, 4, 2]); rstd = sb("rstd", [P, 4])
        idle = sb("idle", [P, 1])
        xn = sb("xn", [P, 4, P]); xT = sb("xT", [P, 4 * P])
        qT = sb("qT", [P, NC, 4 * P])
        ctxg = sb("ctxg", [CTX, 4, NKEY])
        if hd == 8:
            kbd = sb("kbd", [P, 4, 4, NK])
            vals = [sb("vals", [KEYS[0], 4, heads, 32])]
        else:
            kbd = sb("kbd", [P, NC, 4, 2, NK])
            if kind == "latent":
                raw_lat = sb("raw_lat", [P, 4, 3 * P]); raw_ctx = sb("raw_ctx", [NKEY, 4, 2 * P])
                vals = [raw_ctx[:, :, P:2 * P], raw_lat[:, :, 2 * P:3 * P]]
                sq_lat = sb("sq_lat", [P, 4, 2 * P]); sq_ctx = sb("sq_ctx", [NKEY, 4, P])
                xn2 = sb("xn2", [P, 4, P]); cn = sb("cn", [NKEY, 4, CTX]); cT = sb("cT", [CTX, 4, NKEY])
                stats_ctx = sb("stats_ctx", [NKEY, 4, 6]); mv_ctx = sb("mv_ctx", [NKEY, 4, 2])
                rstd_ctx = sb("rstd_ctx", [NKEY, 4])
                rms_lat = sb("rms_lat", [P, 16]); rms_ctx = sb("rms_ctx", [NKEY, 8])
                qk_tok = sb("qk_tok", [P, 4, 4, 64]); kc_tok = sb("kc_tok", [NKEY, 4, 2, 64])
            else:
                vals = [sb("vals", [KEYS[0], 4, inner])]
        NB = 3
        soft = [sb(f"soft{i}", [P, heads, NK]) for i in range(NB)]
        mx = [sb(f"mx{i}", [P, U]) for i in range(2)]
        rsum = [sb(f"rsum{i}", [P, heads]) for i in range(2)]
        rinv = [sb(f"rinv{i}", [P, heads]) for i in range(2)]
        probsT = [sb(f"probsT{i}", [P, 4, P]) for i in range(2)]
        attnT = sb("attnT", [P, NC, P])

        loaded, constants, dve_chain = sem("loaded"), sem("constants"), sem("dve_chain")
        var_ready, rstd_ready, normed = sem("var_ready"), sem("rstd_ready"), sem("normed")
        xT_ps, xT_ready, ctx_ready = sem("xT_ps"), sem("xT_ready"), sem("ctx_ready")
        a_ps, a_done = sem("a_ps"), sem("a_done")
        d_ps, d_done = sem("d_ps"), sem("d_done")
        scores_ready, max_ready, shifted = sem("scores_ready"), sem("max_ready"), sem("shifted")
        exp_done, sum_ready, inv_ready, probs_ready = sem("exp_done"), sem("sum_ready"), sem("inv_ready"), sem("probs_ready")
        turned, turned_out, values_done = sem("turned"), sem("turned_out"), sem("values_done")
        attnT_ready, proj_done, added = sem("attnT_ready"), sem("proj_done"), sem("added")
        var2_ready, rstd2_ready = sem("var2_ready"), sem("rstd2_ready")
        mask_zero = sem("mask_zero")
        qkv_ps, qkv_out, squared = sem("qkv_ps"), sem("qkv_out"), sem("squared")
        ss_ready, rms_ready, qk_ready, qkT_ps = sem("ss_ready"), sem("rms_ready"), sem("qk_ready"), sem("qkT_ps")

        if inner == P:
            vjobs = [([0, 1, 2, 3], 0, P)]
        else:
            vjobs = [([b], c, 512) for b in range(4) for c in range(0, inner, 512)]
        NA, ND = NC + len(vjobs), NC
        TU = 4 * NU

        def shift(dve, it, b):
            for u in range(NU):
                n = b * NU + u
                ps = score_bank[n % 3][:, 0:U * NK].rearrange("p (h k) -> p h k", h=U)
                dve.wait_ge(scores_ready, it * TU + n + 1)
                if n >= 2:
                    dve.wait_ge(shifted, it * TU + n - 1)
                dve.tensor_reduce(mx[n % 2][:, :], ps, AX_X, ALU.max).then_inc(max_ready, 1)
                dve.wait_ge(max_ready, it * TU + n + 1)
                if u == 0 and b >= NB:
                    dve.wait_ge(turned, it * TU + (b - NB + 1) * NU)
                dve.tensor_tensor(soft[b % NB][:, u * U:(u + 1) * U, :], ps,
                                  mx[n % 2][:, :].unsqueeze(2).to_broadcast([P, U, NK]),
                                  ALU.subtract).then_inc(shifted, 1)

        def row_sums(dve, it, b):
            g = it * 4 + b
            dve.wait_ge(exp_done, g + 1)
            if b >= 2:
                dve.wait_ge(probs_ready, g - 1)
            dve.tensor_reduce(rsum[b % 2][:, :], soft[b % NB][:, :, :], AX_X, ALU.add).then_inc(sum_ready, 1)
            dve.wait_ge(sum_ready, g + 1)
            dve.reciprocal(rinv[b % 2][:, :], rsum[b % 2][:, :]).then_inc(inv_ready, 1)

        def latent_dve(dve, it):
            link = Link(dve, dve_chain, it, 8)
            for b in range(4):
                dve.bn_stats(stats[:, b, :], x[:, it * 4 + b, :])
                last = dve.bn_stats(stats_ctx[:, b, :], ctx_tok[:, it * 4 + b, :])
            link(last)
            dve.memset(idle[:, :], 0.0)
            for b in range(4):
                dve.bn_aggr(mean_var[:, b, :], stats[:, b, :])
                last = dve.bn_aggr(mv_ctx[:, b, :], stats_ctx[:, b, :])
            link(last)
            dve.tensor_scalar(rstd[:, :], mean_var[:, :, 1], EPS, None, ALU.add)
            dve.tensor_scalar(rstd_ctx[:, :], mv_ctx[:, :, 1], EPS, None, ALU.add).then_inc(var_ready, 1)
            dve.wait_ge(rstd_ready, it + 1)
            for b in range(4):
                dve.tensor_scalar(cn[:, b, :], ctx_tok[:, it * 4 + b, :], mv_ctx[:, b, 0:1],
                                  rstd_ctx[:, b:b + 1], ALU.subtract, ALU.mult)
            for b in range(4):
                last = dve.tensor_scalar(xn[:, b, :], x[:, it * 4 + b, :], mean_var[:, b, 0:1],
                                         rstd[:, b:b + 1], ALU.subtract, ALU.mult)
            link(last)
            for b in range(4):
                last = dve.bn_stats(stats[:, b, :], xn[:, b, :])
            link(last)
            dve.memset(idle[:, :], 0.0)
            for b in range(4):
                last = dve.bn_aggr(mean_var[:, b, :], stats[:, b, :])
            link(last)
            dve.tensor_scalar(rstd[:, :], mean_var[:, :, 1], EPS, None, ALU.add).then_inc(var2_ready, 1)
            dve.wait_ge(rstd2_ready, it + 1)
            for b in range(4):
                last = dve.tensor_scalar(xn2[:, b, :], xn[:, b, :], mean_var[:, b, 0:1],
                                         rstd[:, b:b + 1], ALU.subtract, ALU.mult)
            last.then_inc(normed, 1)
            dve.wait_ge(squared, it + 1)
            dve.tensor_reduce(rms_lat[:, :], sq_lat[:, :, :].rearrange("p b (g d) -> p (b g) d", d=64), AX_X, ALU.add)
            dve.tensor_reduce(rms_ctx[:, :], sq_ctx[:, :, :].rearrange("p b (g d) -> p (b g) d", d=64),
                              AX_X, ALU.add).then_inc(ss_ready, 1)
            dve.wait_ge(rms_ready, it + 1)
            dve.tensor_scalar(rms_lat[:, :], rms_lat[:, :], 0.125, 1e-8, ALU.mult, ALU.max)
            link(dve.tensor_scalar(rms_ctx[:, :], rms_ctx[:, :], 0.125, 1e-8, ALU.mult, ALU.max))
            dve.reciprocal(rms_lat[:, :], rms_lat[:, :])
            link(dve.reciprocal(rms_ctx[:, :], rms_ctx[:, :]))
            dve.tensor_tensor(qk_tok[:, :, :, :], raw_lat[:, :, 0:2 * P].rearrange("p b (g d) -> p b g d", d=64),
                              rms_lat[:, :].rearrange("p (b g) -> p b g", b=4).unsqueeze(3).to_broadcast([P, 4, 4, 64]),
                              ALU.mult)
            link(dve.tensor_tensor(kc_tok[:, :, :, :], raw_ctx[:, :, 0:P].rearrange("p b (g d) -> p b g d", d=64),
                                   rms_ctx[:, :].rearrange("p (b g) -> p b g", b=4).unsqueeze(3).to_broadcast([NKEY, 4, 2, 64]),
                                   ALU.mult))
            dve.tensor_tensor(qk_tok[:, :, :, :], qk_tok[:, :, :, :],
                              gamma[:, :, :].unsqueeze(1).to_broadcast([P, 4, 4, 64]), ALU.mult)
            dve.tensor_tensor(kc_tok[:, :, :, :], kc_tok[:, :, :, :],
                              gamma[0:NKEY, 2:4, :].unsqueeze(1).to_broadcast([NKEY, 4, 2, 64]),
                              ALU.mult).then_inc(qk_ready, 1)
            link.end()
            dve.wait_ge(qkT_ps, it + 1)
            lat = score_bank[0][:, :].rearrange("p (b t) -> p b t", b=4)
            con = score_bank[1][:, 0:4 * NKEY].rearrange("p (b t) -> p b t", b=4)
            for i in range(2):
                dve.tensor_copy(kbd[64 * i:64 * i + 64, 0, :, i, NKEY:NK], lat[64 * i:64 * i + 64, :, :])
                last = dve.tensor_copy(kbd[64 * i:64 * i + 64, 0, :, i, 0:NKEY], con[64 * i:64 * i + 64, :, :])
            last.then_inc(d_done, 1)

        def latent_act(act, it):
            act.wait_ge(xT_ps, it + 1)
            act.activation(xT[:, :], out_bank[0][:, :], ACT.Identity, scale=lat_g[:, 0:1], bias=lat_b[:, 0:1])
            act.activation(cT[:, :, :], out_bank[1][0:CTX, 0:4 * NKEY].rearrange("p (b t) -> p b t", b=4),
                           ACT.Identity, scale=ctx_g[:, 0:1], bias=ctx_b[:, 0:1]).then_inc(xT_ready, 1)
            for b in range(4):
                act.wait_ge(qkv_ps, it * 6 + b + 1)
                last = act.copy(raw_lat[:, b, :], [*score_bank, turn_bank[0]][b][:, 0:3 * P])
            for i in range(2):
                act.wait_ge(qkv_ps, it * 6 + 5 + i)
                last = act.copy(raw_ctx[:, 2 * i:2 * i + 2, :],
                                [turn_bank[1], proj_bank][i][0:NKEY, :].rearrange("p (b f) -> p b f", b=2))
            last.then_inc(qkv_out, 1)
            act.wait_ge(qkv_out, it + 1)
            act.activation(sq_lat[:, :, :], raw_lat[:, :, 0:2 * P], ACT.Square)
            act.activation(sq_ctx[:, :, :], raw_ctx[:, :, 0:P], ACT.Square).then_inc(squared, 1)
            act.wait_ge(qkT_ps, it + 1)
            act.copy(qT[:, 0, :], turn_bank[0][:, :]).then_inc(a_done, 1)

        def latent_pe(pe, it):
            pe.wait_ge(normed, it + 1)
            for b in range(4):
                pe.transpose(out_bank[1][0:CTX, b * NKEY:(b + 1) * NKEY], cn[:, b, :], ident[0:NKEY, 0:NKEY])
            for b in range(4):
                last = pe.transpose(out_bank[0][:, b * P:(b + 1) * P], xn2[:, b, :], ident[:, :])
            last.then_inc(xT_ps, 1)
            pe.wait_ge(xT_ready, it + 1)
            pe.wait_ge(added, it * 4)
            for b in range(4):
                pe.matmul([*score_bank, turn_bank[0]][b][:, 0:3 * P], xT[:, b * P:(b + 1) * P], wqkv_lat[:, :],
                          start=True, stop=True).then_inc(qkv_ps, 1)
            for b in range(4):
                last = pe.matmul([turn_bank[1], proj_bank][b // 2][0:NKEY, b % 2 * 2 * P:(b % 2 + 1) * 2 * P],
                                 cT[:, b, :], wkv_ctx[:, :], start=True, stop=True)
                if b % 2:
                    last.then_inc(qkv_ps, 1)
            pe.wait_ge(qk_ready, it + 1)
            for b in range(4):
                pe.transpose(turn_bank[0][:, b * P:(b + 1) * P],
                             qk_tok[:, b, 0:2, :].rearrange("p g d -> p (g d)"), ident[:, :])
                pe.transpose(score_bank[0][:, b * P:(b + 1) * P],
                             qk_tok[:, b, 2:4, :].rearrange("p g d -> p (g d)"), ident[:, :])
                last = pe.transpose(score_bank[1][:, b * NKEY:(b + 1) * NKEY],
                                    kc_tok[:, b, :, :].rearrange("p g d -> p (g d)"), ident[0:NKEY, 0:NKEY])
            last.then_inc(qkT_ps, 1)
            pe.wait_ge(a_done, it + 1)
            pe.wait_ge(d_done, it + 1)

        block = ctx.enter_context(nc.Block())

        @block.sync
        def _(sp):
            for dst_ap, src in loads:
                sp.dma_start(dst_ap, src).then_inc(loaded, 16)

        @block.gpsimd
        def _(pool):
            with pool.Fori(0, NTURN) as it:
                if kind == "cross":
                    pool.wait_ge(a_done, it * NA)
                    pool.tensor_copy(ctxg[:, :, :], net.ctxT[:, bass.ds(it * 4, 4), :]).then_inc(ctx_ready, 1)
                if kind != "latent":
                    pool.wait_ge(var_ready, it + 1)
                    pool.tensor_tensor(rstd[:, :], rstd[:, :], net.minus_half[:, 0:4], ALU.pow).then_inc(rstd_ready, 1)
                if kind == "latent":
                    half = net.minus_half
                    pool.wait_ge(var_ready, it + 1)
                    pool.tensor_tensor(rstd[:, :], rstd[:, :], half[:, 0:4], ALU.pow)
                    pool.tensor_tensor(rstd_ctx[:, :], rstd_ctx[:, :], half[0:NKEY, 0:4], ALU.pow).then_inc(rstd_ready, 1)
                    pool.wait_ge(var2_ready, it + 1)
                    pool.tensor_tensor(rstd[:, :], rstd[:, :], half[:, 0:4], ALU.pow).then_inc(rstd2_ready, 1)
                    pool.wait_ge(ss_ready, it + 1)
                    pool.tensor_tensor(rms_lat[:, :], rms_lat[:, :], net.plus_half[:, 0:16], ALU.pow)
                    pool.tensor_tensor(rms_ctx[:, :], rms_ctx[:, :], net.plus_half[0:NKEY, 0:8], ALU.pow).then_inc(rms_ready, 1)
                for b in range(4):
                    tile = soft[b % NB][:, :, :]
                    pool.wait_ge(inv_ready, it * 4 + b + 1)
                    pool.tensor_tensor(tile, tile, rinv[b % 2][:, :].unsqueeze(2).to_broadcast([P, heads, NK]),
                                       ALU.mult).then_inc(probs_ready, 1)

        @block.vector
        def _(dve):
            dve.wait_ge(loaded, 16 * len(loads))
            if kind == "latent":
                dve.memset(mask_row[:, :, :, :], 0.0).then_inc(mask_zero, 1)
                dve.wait_ge(mask_zero, 1)
                for i in range(2):
                    dve.tensor_scalar(mask_row[:, :, i, 0:NKEY], mask8[:, :].rearrange("p (b t) -> p b t", t=NKEY),
                                      1.0, 1e30, ALU.subtract, ALU.mult)
            if hd == 8:
                dve.memset(vals[0][:, :, :, :], 0.0).then_inc(constants, 1)
            else:
                dve.memset(kbd[0:64, :, :, 1, :], 0.0)
                dve.memset(kbd[64:P, :, :, 0, :], 0.0).then_inc(constants, 1)
            with dve.Fori(0, NTURN) as it:
                if kind != "latent":
                    for b in range(4):
                        last = dve.bn_stats(stats[:, b, :], x[:, it * 4 + b, :])
                    last.then_inc(dve_chain, 1)
                    dve.wait_ge(dve_chain, it * 2 + 1)
                    dve.memset(idle[:, :], 0.0)
                    for b in range(4):
                        last = dve.bn_aggr(mean_var[:, b, :], stats[:, b, :])
                    last.then_inc(dve_chain, 1)
                    dve.wait_ge(dve_chain, it * 2 + 2)
                    dve.tensor_scalar(rstd[:, :], mean_var[:, :, 1], EPS, None, ALU.add).then_inc(var_ready, 1)
                    dve.wait_ge(rstd_ready, it + 1)
                    dve.wait_ge(added, it * 4)
                    for b in range(4):
                        last = dve.tensor_scalar(xn[:, b, :], x[:, it * 4 + b, :], mean_var[:, b, 0:1],
                                                 rstd[:, b:b + 1], ALU.subtract, ALU.mult)
                    last.then_inc(normed, 1)
                if kind == "latent":
                    latent_dve(dve, it)
                else:
                    for c in range(NC):
                        kps = score_bank[c % 2][:, 0:4 * NK].rearrange("p (b k) -> p b k", b=4)
                        dve.wait_ge(d_ps, it * ND + c + 1)
                        if hd == 8:
                            for b in range(4):
                                last = dve.scalar_tensor_tensor(
                                    kbd[:, b, :, :], kps[:, b:b + 1, :].to_broadcast([P, 4, NK]), bk[:, 0:1],
                                    diag[:, :].unsqueeze(2).to_broadcast([P, 4, NK]), ALU.add, ALU.mult)
                        else:
                            dve.tensor_copy(kbd[0:64, c, :, 0, :], kps[0:64, :, :])
                            last = dve.tensor_copy(kbd[64:P, c, :, 1, :], kps[64:P, :, :])
                        last.then_inc(d_done, 1)
                for s in range(7):
                    if s < 4:
                        shift(dve, it, s)
                    if 1 <= s <= 4:
                        row_sums(dve, it, s - 1)
                    if s >= 3:
                        g = it * 4 + s - 3
                        dve.wait_ge(proj_done, g + 1)
                        inp = xn[:, s - 3, :] if kind == "self" else x[:, g, :]
                        dve.tensor_tensor(dst[:, g, :], inp, proj_bank[:, 0:P], ALU.add).then_inc(added, 1)

        @block.scalar
        def _(act):
            act.wait_ge(loaded, 16 * len(loads))
            act.wait_ge(constants, 1)
            with act.Fori(0, NTURN) as it:
                if kind == "latent":
                    latent_act(act, it)
                else:
                    act.wait_ge(xT_ps, it + 1)
                    act.copy(xT[:, :], out_bank[0][:, :]).then_inc(xT_ready, 1)
                    for c in range(NC):
                        act.wait_ge(a_ps, it * NA + c + 1)
                        if biased:
                            act.activation(qT[:, c, :], turn_bank[c % 2][:, :], ACT.Identity,
                                           bias=bq[:, 0:1]).then_inc(a_done, 1)
                        else:
                            act.copy(qT[:, c, :], turn_bank[c % 2][:, :]).then_inc(a_done, 1)
                    for v, (bs, c0, cols) in enumerate(vjobs):
                        bank = turn_bank[(NC + v) % 2][0:KEYS[0], 0:len(bs) * cols]
                        act.wait_ge(a_ps, it * NA + NC + v + 1)
                        if hd == 8:
                            ps = bank.rearrange("p (b r j d) -> p b r j d", b=4, r=4, j=4)
                            out = vals[0][:, :, :, :].rearrange("p b (r j) d -> p b r j d", j=4)
                            for j in range(4):
                                for b in range(4):
                                    last = act.copy(out[:, b, :, j, 8 * j:8 * j + 8], ps[:, b, :, j, :])
                        else:
                            last = act.copy(vals[0][:, bs[0], c0:c0 + cols], bank)
                        last.then_inc(a_done, 1)
                for s in range(1, 6):
                    if s <= 4:
                        tile = soft[(s - 1) % NB][:, :, :].rearrange("p h k -> p (h k)")
                        act.wait_ge(shifted, it * TU + s * NU)
                        act.activation(tile, tile, ACT.Exp, scale=scale).then_inc(exp_done, 1)
                    if s >= 2:
                        b = s - 2
                        for u in range(NU):
                            n = b * NU + u
                            act.wait_ge(turned, it * TU + n + 1)
                            if n >= 2:
                                act.wait_ge(values_done, it * TU + n - 1)
                            ps = turn_bank[n % 2][:, :].rearrange("p (m t) -> p m t", m=4)
                            for e, nk in enumerate(KEYS):
                                last = act.copy(probsT[n % 2][0:nk, e:len(SLOTS):len(KEYS), :],
                                                ps[0:nk, e:len(SLOTS):len(KEYS), :])
                            last.then_inc(turned_out, 1)
                        for p in range(NP):
                            nch = min(4, NC - 4 * p)
                            act.wait_ge(values_done, it * TU + b * NU + (p + 1) * (NU // NP))
                            act.copy(attnT[:, 4 * p:4 * p + nch, :],
                                     out_bank[(b * NP + p) % 2][:, 0:nch * P].rearrange("p (c t) -> p c t", c=nch)
                                     ).then_inc(attnT_ready, 1)

        @block.tensor
        def _(pe):
            pe.wait_ge(loaded, 16 * len(loads))
            pe.wait_ge(constants, 1)

            def prep(it):
                pe.wait_ge(normed, it + 1)
                for b in range(4):
                    last = pe.transpose(out_bank[0][:, b * P:(b + 1) * P], xn[:, b, :], ident[:, :])
                last.then_inc(xT_ps, 1)
                if kind == "self":
                    pe.wait_ge(xT_ready, it + 1)
                for c in range(NC):
                    if c >= 2:
                        pe.wait_ge(d_done, it * ND + c - 1)
                    src = xT[:, :] if kind == "self" else net.ctxT[:, bass.ds(it * 4, 4), :]
                    pe.matmul(score_bank[c % 2][:, 0:4 * NK], wk[:, c * P:(c + 1) * P], src,
                              start=True, stop=True).then_inc(d_ps, 1)
                    if c == 0 and kind == "cross":
                        pe.wait_ge(xT_ready, it + 1)
                    if c >= 2:
                        pe.wait_ge(a_done, it * NA + c - 1)
                    pe.matmul(turn_bank[c % 2][:, :], wq[:, c * P:(c + 1) * P], xT[:, :],
                              start=True, stop=True).then_inc(a_ps, 1)
                if kind == "cross":
                    pe.wait_ge(ctx_ready, it + 1)
                for v, (bs, c0, cols) in enumerate(vjobs):
                    n = NC + v
                    if n >= 2:
                        pe.wait_ge(a_done, it * NA + n - 1)
                    for i, b in enumerate(bs):
                        src = xT[:, b * P:(b + 1) * P] if kind == "self" else ctxg[:, b, :]
                        out = turn_bank[n % 2][0:KEYS[0], i * cols:(i + 1) * cols]
                        last = pe.matmul(out, src, wv[:, c0:c0 + cols], start=True, stop=not biased)
                        if biased:
                            last = pe.matmul(out, ones_row[:, 0:KEYS[0]], bv[:, :], start=False, stop=True)
                    last.then_inc(a_ps, 1)
                pe.wait_ge(d_done, (it + 1) * ND)
                pe.wait_ge(a_done, (it + 1) * NA)

            def scores(it, b):
                for u in range(NU):
                    n = b * NU + u
                    bank = score_bank[n % 3]
                    if n >= 3:
                        pe.wait_ge(shifted, it * TU + n - 2)
                    if hd == 8:
                        last = pe.matmul(bank[:, 0:U * NK], qT[32 * u:32 * u + 32, 0, b * P:(b + 1) * P],
                                         kbd[32 * u:32 * u + 32, b, :, :], start=True, stop=True)
                    else:
                        for c in range(u * U // 2, (u + 1) * U // 2):
                            at = (2 * c - u * U) * NK
                            last = pe.matmul(bank[:, at:at + 2 * NK], qT[:, c, b * P:(b + 1) * P],
                                             kbd[:, c, b, :, :], start=True, stop=kind != "latent")
                            if kind == "latent":
                                last = pe.matmul(bank[:, at:at + 2 * NK], ones_row[:, :],
                                                 mask_row[:, it * 4 + b, :, :], start=False, stop=True)
                    last.then_inc(scores_ready, 1)

            def turn(it, b, u):
                n = b * NU + u
                if u == 0:
                    pe.wait_ge(probs_ready, it * 4 + b + 1)
                if n >= 2:
                    pe.wait_ge(turned_out, it * TU + n - 1)
                for m, (i, e) in enumerate(SLOTS):
                    last = pe.transpose(turn_bank[n % 2][0:KEYS[e], m * P:(m + 1) * P],
                                        soft[b % NB][:, u * U + i, OFF[e]:OFF[e] + KEYS[e]], ident[:, :])
                last.then_inc(turned, 1)

            def values(it, b, u):
                n = b * NU + u
                pe.wait_ge(turned_out, it * TU + n + 1)
                if u % (NU // NP) == 0:
                    pe.wait_ge(attnT_ready, max(b * NP + u // (NU // NP) - 1, 0) + it * 4 * NP)
                for m, (i, e) in enumerate(SLOTS):
                    h, nk = u * U + i, KEYS[e]
                    if hd == 8:
                        last = pe.matmul(out_bank[b % 2][32 * u:32 * u + 32, 0:P], vals[0][:, b, h, :],
                                         probsT[n % 2][0:nk, m, :], start=(i == 0), stop=(i == U - 1))
                    else:
                        c = h // 2
                        out = out_bank[(b * NP + c // 4) % 2][64 * (h % 2):64 * (h % 2) + 64, c % 4 * P:(c % 4 + 1) * P]
                        last = pe.matmul(out, vals[e][:, b, h * 64:(h + 1) * 64], probsT[n % 2][0:nk, m, :],
                                         start=(e == 0), stop=(e == len(KEYS) - 1))
                last.then_inc(values_done, 1)

            def project(it, b):
                g = it * 4 + b
                pe.wait_ge(attnT_ready, (g + 1) * NP)
                pe.wait_ge(added, g)
                pe.matmul(proj_bank[:, 0:P], ones_row[:, :], bo[:, :], start=True, stop=False)
                for c in range(NC):
                    last = pe.matmul(proj_bank[:, 0:P], attnT[:, c, :], wo[:, c, :], start=False, stop=(c == NC - 1))
                last.then_inc(proj_done, 1)

            with pe.Fori(0, NTURN) as it:
                if kind == "latent":
                    latent_pe(pe, it)
                else:
                    prep(it)
                for s in range(7):
                    if s < 4:
                        scores(it, s)
                    if s >= 3:
                        project(it, s - 3)
                    if 2 <= s <= 5:
                        for u in range(NU):
                            turn(it, s - 2, u)
                            if u:
                                values(it, s - 2, u - 1)
                        values(it, s - 2, NU - 1)


def top_two(dve, link, net, logits, n, experts, tiles):
    shape = [P, n, experts]
    index = net.index64[:, 0:experts].unsqueeze(1).to_broadcast(shape)
    left = logits
    for rank in range(2):
        top, hot, least = tiles["top"][rank], tiles["hot"][rank], tiles["least"]
        link(dve.tensor_reduce(top, left, AX_X, ALU.max))
        link(dve.tensor_tensor(hot, left, top.unsqueeze(2).to_broadcast(shape), ALU.is_equal))
        link(dve.tensor_tensor(hot, hot, index, ALU.mult))
        link(dve.tensor_reduce(least, hot, AX_X, ALU.min))
        link(dve.tensor_tensor(hot, index, least.unsqueeze(2).to_broadcast(shape), ALU.is_equal))
        if rank == 0:
            left = tiles["left"]
            link(dve.scalar_tensor_tensor(left, hot, -3e38, logits, ALU.mult, ALU.add))


TOP_TWO_LINKS = 11


def dense_moe_stage(nc, net, spec, w):
    name, FF, kind = spec["name"], spec["FF"], spec["kind"]
    E, FC = 8, FF // P
    func = ACT.Gelu if kind == "pre" else ACT.Relu
    post = kind == "post"
    with ExitStack() as ctx:
        def sb(n, shape, dt=F32):
            return ctx.enter_context(nc.sbuf_tensor(f"{name}_{n}", shape, dt))

        def sem(n):
            return net.sem(f"{name}_{n}")

        x, ident, ones_row = net.x, net.ident, net.ones_row
        src = net.x1 if post else net.x
        hid_bank, y_bank, turn_bank, gate_bank = net.banks[0:4], net.banks[4:6], net.banks[6], net.banks[7]
        w1 = sb("w1", [P, E, FF]); w2 = sb("w2", [P, E, FC, P]); b1 = sb("b1", [P, E * FC]); b2 = sb("b2", [E, P])
        wg = sb("wg", [P, E]); bg = sb("bg", [1, E]); g_col = sb("g_col", [P, 1]); b_col = sb("b_col", [P, 1])
        loads = [(wg[:, :], w["wg"]), (bg[:, :], w["bg"]), (g_col[:, :], w["g_col"]), (b_col[:, :], w["b_col"]),
                 (b1[:, :], w["b1"]), (b2[:, :], w["b2"]), (w1[:, :, :], w["w1"]), (w2[:, :, :, :], w["w2"])]
        if post:
            g1, be1, g2, be2 = (sb(n, [P, P]) for n in ("g1", "be1", "g2", "be2"))
            loads += [(g1[:, :], w["g1"]), (be1[:, :], w["be1"]), (g2[:, :], w["g2"]), (be2[:, :], w["be2"])]
            stats2 = sb("stats2", [P, 4, 6]); mv2 = sb("mv2", [P, 4, 2]); rstd2 = sb("rstd2", [P, 4])
            out_n = sb("out_n", [P, 4, P])
        stats = sb("stats", [P, 4, 6]); mean_var = sb("mean_var", [P, 4, 2]); rstd = sb("rstd", [P, 4])
        idle = sb("idle", [P, 1])
        xn = sb("xn", [P, 4, P]); xn2 = sb("xn2", [P, 4, P]); base = sb("base", [P, 4, P])
        xT = [sb(f"xT{i}", [P, 4 * P]) for i in range(2)]
        gates = [sb(f"gates{i}", [P, 4, E]) for i in range(2)]
        acc = [sb(f"acc{i}", [P, 4, P]) for i in range(2)]
        logits = sb("logits", [P, 4, E]); expd = sb("expd", [P, 4, E]); both = sb("both", [P, 4, E])
        small = {n: sb(n, [P, 4]) for n in ("top0", "top1", "least", "total", "gate0", "gate1", "gap")}
        tiles = dict(top=[small["top0"][:, :], small["top1"][:, :]], least=small["least"][:, :],
                     hot=[sb(f"hot{i}", [P, 4, E])[:, :, :] for i in range(2)], left=sb("left", [P, 4, E])[:, :, :])
        gatesT = sb("gatesT", [E, 4 * P]); hT = [sb(f"hT{i}", [P, FC, 4 * P]) for i in range(2)]

        loaded, chain = sem("loaded"), sem("chain")
        var_ready, rstd_ready, normed = sem("var_ready"), sem("rstd_ready"), sem("normed")
        affine_done = sem("affine_done")
        xT_ps, xT_ready, logits_ps = sem("xT_ps"), sem("xT_ready"), sem("logits_ps")
        less_top, exp_done, gates_ready = sem("less_top"), sem("exp_done"), sem("gates_ready")
        gatesT_ps, gatesT_ready, bias_ps, acc_ready = sem("gatesT_ps"), sem("gatesT_ready"), sem("bias_ps"), sem("acc_ready")
        hid_ready, hid_out, y_ready, y_added = sem("hid_ready"), sem("hid_out"), sem("y_ready"), sem("y_added")
        var2_ready, rstd2_ready, finished = sem("var2_ready"), sem("rstd2_ready"), sem("finished")
        NORMS = 1 if post else 2
        LINKS = 1 + TOP_TWO_LINKS + (2 + 4 if post else 6 + 8)
        post_chain = sem("post_chain")

        def norm_dve(dve, t, link, out, inp, i):
            for b in range(4):
                last = dve.bn_stats(stats[:, b, :], inp(b))
            link(last)
            dve.memset(idle[:, :], 0.0)
            for b in range(4):
                last = dve.bn_aggr(mean_var[:, b, :], stats[:, b, :])
            link(last)
            dve.tensor_scalar(rstd[:, :], mean_var[:, :, 1], EPS, None, ALU.add).then_inc(var_ready, 1)
            dve.wait_ge(rstd_ready, t * NORMS + i + 1)
            for b in range(4):
                last = dve.tensor_scalar(out[:, b, :], inp(b), mean_var[:, b, 0:1], rstd[:, b:b + 1],
                                         ALU.subtract, ALU.mult)
            return last

        def prep_dve(dve, t, par, part, link):
            if part == "norm":
                norm_part(dve, t, link)
            elif part == "gates":
                gates_part(dve, t, par, link)
            else:
                start_part(dve, t, par, link)

        def norm_part(dve, t, link):
            last = norm_dve(dve, t, link, xn, lambda b: src[:, t * 4 + b, :], 0)
            if post:
                last.then_inc(normed, 1)
            else:
                link(last)
                norm_dve(dve, t, link, xn2, lambda b: xn[:, b, :], 1).then_inc(normed, 1)
                link(dve.tensor_tensor(base[:, :, :], x[:, bass.ds(t * 4, 4), :], xn[:, :, :], ALU.add))

        def gates_part(dve, t, par, link):
            dve.wait_ge(logits_ps, t + 1)
            link(dve.tensor_copy(logits[:, :, :], gate_bank[:, 0:4 * E].rearrange("p (b e) -> p b e", b=4)))
            top_two(dve, link, net, logits[:, :, :], 4, E, tiles)
            shape = [P, 4, E]
            dve.tensor_tensor(expd[:, :, :], logits[:, :, :], tiles["top"][0].unsqueeze(2).to_broadcast(shape),
                              ALU.subtract).then_inc(less_top, 1)
            dve.wait_ge(exp_done, t + 1)
            link(dve.tensor_reduce(small["total"][:, :], expd[:, :, :], AX_X, ALU.add))
            link(dve.reciprocal(small["gate0"][:, :], small["total"][:, :]))
            link(dve.tensor_tensor(expd[:, :, :], expd[:, :, :],
                                   small["gate0"][:, :].unsqueeze(2).to_broadcast(shape), ALU.mult))
            link(dve.tensor_tensor(both[:, :, :], tiles["hot"][0], tiles["hot"][1], ALU.add))
            gate = gates[par][:, :, :]
            if post:
                dve.tensor_tensor(gate, expd[:, :, :], both[:, :, :], ALU.mult).then_inc(gates_ready, 1)
            else:
                link(dve.tensor_tensor(gate, expd[:, :, :], both[:, :, :], ALU.mult))
                link(dve.tensor_reduce(small["total"][:, :], gate, AX_X, ALU.add))
                link(dve.tensor_scalar(small["total"][:, :], small["total"][:, :], 1e-8, None, ALU.add))
                link(dve.reciprocal(small["gap"][:, :], small["total"][:, :]))
                dve.tensor_tensor(gate, gate, small["gap"][:, :].unsqueeze(2).to_broadcast(shape),
                                  ALU.mult).then_inc(gates_ready, 1)

        def start_part(dve, t, par, link):
            link.end()
            dve.wait_ge(bias_ps, t + 1)
            if post:
                dve.wait_ge(affine_done, t + 1)
            dve.tensor_tensor(acc[par][:, :, :], turn_bank[:, :].rearrange("p (b f) -> p b f", b=4),
                              (xn2 if post else base)[:, :, :], ALU.add).then_inc(acc_ready, 1)

        def prep_pool(pool, t):
            for i in range(NORMS):
                pool.wait_ge(var_ready, t * NORMS + i + 1)
                pool.tensor_tensor(rstd[:, :], rstd[:, :], net.minus_half[:, 0:4], ALU.pow).then_inc(rstd_ready, 1)
            if post:
                pool.wait_ge(normed, t + 1)
                shape = [P, 4, P]
                pool.wait_ge(acc_ready, t)
                pool.tensor_tensor(xn2[:, :, :], xn[:, :, :], g1[:, :].unsqueeze(1).to_broadcast(shape),
                                   ALU.mult).then_inc(affine_half, 1)
                pool.wait_ge(affine_half, t + 1)
                pool.tensor_tensor(xn2[:, :, :], xn2[:, :, :], be1[:, :].unsqueeze(1).to_broadcast(shape),
                                   ALU.add).then_inc(affine_done, 1)

        affine_half, out_half = sem("affine_half"), sem("out_half")

        def prep_act(act, t, par, part):
            if part == "tokens":
                act.wait_ge(xT_ps, t + 1)
                act.activation(xT[par][:, :], turn_bank[:, :], ACT.Identity, scale=g_col[:, 0:1],
                               bias=b_col[:, 0:1]).then_inc(xT_ready, 1)
            elif part == "exp":
                act.wait_ge(less_top, t + 1)
                act.activation(expd[:, :, :], expd[:, :, :], ACT.Exp).then_inc(exp_done, 1)
            else:
                act.wait_ge(gatesT_ps, t + 1)
                act.copy(gatesT[:, :], gate_bank[0:E, :]).then_inc(gatesT_ready, 1)

        def prep_pe(pe, t, par, part):
            if part == 0:
                pe.wait_ge(normed, t + 1)
                for b in range(4):
                    last = pe.transpose(turn_bank[:, b * P:(b + 1) * P], (xn if post else xn2)[:, b, :], ident[:, :])
                last.then_inc(xT_ps, 1)
            if part == 1:
                pe.wait_ge(xT_ready, t + 1)
                for b in range(4):
                    out = gate_bank[:, b * E:(b + 1) * E]
                    pe.matmul(out, xT[par][:, b * P:(b + 1) * P], wg[:, :], start=True, stop=False)
                    last = pe.matmul(out, ones_row[:, :], bg[:, :], start=False, stop=True)
                last.then_inc(logits_ps, 1)
            if part == 2:
                pe.wait_ge(gates_ready, t + 1)
                for b in range(4):
                    last = pe.transpose(gate_bank[0:E, b * P:(b + 1) * P], gates[par][:, b, :], ident[:, :])
                last.then_inc(gatesT_ps, 1)
            if part == 3:
                pe.wait_ge(gatesT_ready, t + 1)
                for b in range(4):
                    last = pe.matmul(turn_bank[:, b * P:(b + 1) * P], gatesT[:, b * P:(b + 1) * P], b2[:, :],
                                     start=True, stop=True)
                last.then_inc(bias_ps, 1)

        def hidden_pe(pe, t, par, e):
            for c in range(FC):
                n = e * FC + c
                if n >= 4:
                    pe.wait_ge(hid_out, t * E * FC + n - 3)
                pe.matmul(hid_bank[n % 4][:, :], w1[:, e, c * P:(c + 1) * P], xT[par][:, :],
                          start=True, stop=True).then_inc(hid_ready, 1)

        def output_pe(pe, t, e):
            pe.wait_ge(hid_out, (t * E + e + 1) * FC)
            pe.wait_ge(y_added, t * E + max(e - 1, 0))
            for b in range(4):
                for c in range(FC):
                    last = pe.matmul(y_bank[e % 2][:, b * P:(b + 1) * P], hT[e % 2][:, c, b * P:(b + 1) * P],
                                     w2[:, e, c, :], start=(c == 0), stop=(c == FC - 1))
            last.then_inc(y_ready, 1)

        def experts_act(act, t, e):
            for c in range(FC):
                n = e * FC + c
                act.wait_ge(hid_ready, t * E * FC + n + 1)
                if c == 0 and e >= 2:
                    act.wait_ge(y_ready, t * E + e - 1)
                act.activation(hT[e % 2][:, c, :], hid_bank[n % 4][:, :], func,
                               bias=b1[:, n:n + 1]).then_inc(hid_out, 1)

        def add_dve(dve, t, par, e):
            dve.wait_ge(y_ready, t * E + e + 1)
            if e == 0:
                dve.wait_ge(acc_ready, t + 1)
            else:
                dve.wait_ge(y_added, t * E + e)
            for b in range(4):
                out = x[:, t * 4 + b, :] if e == E - 1 and not post else acc[par][:, b, :]
                last = dve.scalar_tensor_tensor(out, y_bank[e % 2][:, b * P:(b + 1) * P], gates[par][:, b, e:e + 1],
                                                acc[par][:, b, :], ALU.mult, ALU.add)
            last.then_inc(y_added, 1)

        def finish_dve(dve, t, par):
            link = Link(dve, post_chain, t, 2)
            dve.wait_ge(y_added, (t + 1) * E)
            for b in range(4):
                last = dve.bn_stats(stats2[:, b, :], acc[par][:, b, :])
            link(last)
            dve.memset(idle[:, :], 0.0)
            for b in range(4):
                last = dve.bn_aggr(mv2[:, b, :], stats2[:, b, :])
            link(last)
            dve.tensor_scalar(rstd2[:, :], mv2[:, :, 1], EPS, None, ALU.add).then_inc(var2_ready, 1)
            dve.wait_ge(rstd2_ready, t + 1)
            dve.wait_ge(finished, t)
            for b in range(4):
                last = dve.tensor_scalar(out_n[:, b, :], acc[par][:, b, :], mv2[:, b, 0:1], rstd2[:, b:b + 1],
                                         ALU.subtract, ALU.mult)
            last.then_inc(out_normed, 1)
            link.end()

        out_normed = sem("out_normed")

        def finish_pool(pool, t):
            shape = [P, 4, P]
            pool.wait_ge(var2_ready, t + 1)
            pool.tensor_tensor(rstd2[:, :], rstd2[:, :], net.minus_half[:, 0:4], ALU.pow).then_inc(rstd2_ready, 1)
            pool.wait_ge(out_normed, t + 1)
            pool.tensor_tensor(out_n[:, :, :], out_n[:, :, :], g2[:, :].unsqueeze(1).to_broadcast(shape),
                               ALU.mult).then_inc(out_half, 1)
            pool.wait_ge(out_half, t * 2 + 1)
            pool.tensor_tensor(out_n[:, :, :], out_n[:, :, :], be2[:, :].unsqueeze(1).to_broadcast(shape),
                               ALU.add).then_inc(out_half, 1)
            pool.wait_ge(out_half, t * 2 + 2)
            tokens = x[:, bass.ds(t * 4, 4), :]
            pool.tensor_tensor(tokens, tokens, out_n[:, :, :], ALU.add).then_inc(finished, 1)

        def turns(eng, body, prep):
            prep(0, 0)
            with eng.Fori(0, NTURN // 2 - 1) as i:
                body(i * 2, 0, True)
                body(i * 2 + 1, 1, True)
            body(NTURN - 2, 0, True)
            body(NTURN - 1, 1, False)

        block = ctx.enter_context(nc.Block())

        @block.sync
        def _(sp):
            for dst_ap, s in loads:
                sp.dma_start(dst_ap, s).then_inc(loaded, 16)

        @block.gpsimd
        def _(pool):
            pool.wait_ge(loaded, 16 * len(loads))

            def body(t, par, more):
                if more:
                    prep_pool(pool, t + 1)
                if post:
                    finish_pool(pool, t)

            turns(pool, body, lambda t, par: prep_pool(pool, t))

        @block.vector
        def _(dve):
            dve.wait_ge(loaded, 16 * len(loads))

            def body(t, par, more):
                link = Link(dve, chain, t + 1, LINKS)
                for e in range(E):
                    add_dve(dve, t, par, e)
                    if more and e in (0, 3, 6):
                        prep_dve(dve, t + 1, 1 - par, {0: "norm", 3: "gates", 6: "start"}[e], link)
                if post:
                    finish_dve(dve, t, par)

            def first(t, par):
                link = Link(dve, chain, t, LINKS)
                for part in ("norm", "gates", "start"):
                    prep_dve(dve, t, par, part, link)

            turns(dve, body, first)

        @block.scalar
        def _(act):
            act.wait_ge(loaded, 16 * len(loads))

            def body(t, par, more):
                for e in range(E):
                    experts_act(act, t, e)
                    if more and e in (3, 4, 6):
                        prep_act(act, t + 1, 1 - par, {3: "tokens", 4: "exp", 6: "gates"}[e])

            def first(t, par):
                for part in ("tokens", "exp", "gates"):
                    prep_act(act, t, par, part)

            turns(act, body, first)

        @block.tensor
        def _(pe):
            pe.wait_ge(loaded, 16 * len(loads))

            def body(t, par, more):
                hidden_pe(pe, t, par, 0)
                for e in range(E):
                    if e + 1 < E:
                        hidden_pe(pe, t, par, e + 1)
                    output_pe(pe, t, e)
                    if more and e in (2, 3, 5, 6):
                        prep_pe(pe, t + 1, 1 - par, (2, 3, 5, 6).index(e))

            def first(t, par):
                for part in range(4):
                    prep_pe(pe, t, par, part)

            turns(pe, body, first)


SLOTS_1 = 24 * 384
SLOTS_2 = 2 * NBATCH * P


class Routed:

    def __init__(self, nc, ctx, name):
        def sb(n, shape, dt=F32):
            return ctx.enter_context(nc.sbuf_tensor(f"{name}_{n}", shape, dt))

        self.xn = sb("xn_all", [P, NBATCH, P])
        self.gate = sb("gate", [P, 2, NBATCH])
        self.write = sb("slot_write", [P, NBATCH, 2], U32)
        self.read = sb("slot_read", [P, NBATCH, 2], U32)


def norm_and_logits(nc, net, name, E, wg_dram, routed, logits):
    with ExitStack() as ctx:
        def sb(n, shape, dt=F32):
            return ctx.enter_context(nc.sbuf_tensor(f"{name}n_{n}", shape, dt))

        def sem(n):
            return net.sem(f"{name}n_{n}")

        x, xn_all = net.x, routed.xn
        wg = sb("wg", [P, E]); idle = sb("idle", [P, 1])
        stats = sb("stats", [P, 4, 6]); mean_var = sb("mean_var", [P, 4, 2]); rstd = sb("rstd", [P, 4])
        xn = [sb(f"xn{i}", [P, 4, P]) for i in range(2)]
        xT = [sb(f"xT{i}", [P, 4 * P]) for i in range(2)]
        turn_bank, logit_bank = net.banks[0:2], net.banks[2:4]
        loaded, chain = sem("loaded"), sem("chain")
        var_ready, rstd_ready, normed = sem("var_ready"), sem("rstd_ready"), sem("normed")
        xT_ps, xT_ready, logits_ps, logits_out, kept = (
            sem("xT_ps"), sem("xT_ready"), sem("logits_ps"), sem("logits_out"), sem("kept"))

        block = ctx.enter_context(nc.Block())

        @block.sync
        def _(sp):
            sp.dma_start(wg[:, :], wg_dram).then_inc(loaded, 16)
            sp.wait_ge(loaded, 16)

        @block.gpsimd
        def _(pool):
            with pool.Fori(0, NTURN // 2) as i:
                for par in range(2):
                    t = i * 2 + par
                    pool.wait_ge(var_ready, t + 1)
                    pool.tensor_tensor(rstd[:, :], rstd[:, :], net.minus_half[:, 0:4], ALU.pow).then_inc(rstd_ready, 1)
                    pool.wait_ge(normed, t + 1)
                    pool.tensor_copy(xn[par][:, :, :], xn_all[:, bass.ds(t * 4, 4), :]).then_inc(kept, 1)

        @block.vector
        def _(dve):
            with dve.Fori(0, NTURN // 2) as i:
                link = Link(dve, chain, i, 4)
                for par in range(2):
                    t = i * 2 + par
                    for b in range(4):
                        last = dve.bn_stats(stats[:, b, :], x[:, t * 4 + b, :])
                    link(last)
                    dve.memset(idle[:, :], 0.0)
                    for b in range(4):
                        last = dve.bn_aggr(mean_var[:, b, :], stats[:, b, :])
                    link(last)
                    dve.tensor_scalar(rstd[:, :], mean_var[:, :, 1], EPS, None, ALU.add).then_inc(var_ready, 1)
                    dve.wait_ge(rstd_ready, t + 1)
                    for b in range(4):
                        last = dve.tensor_scalar(xn_all[:, t * 4 + b, :], x[:, t * 4 + b, :], mean_var[:, b, 0:1],
                                                 rstd[:, b:b + 1], ALU.subtract, ALU.mult)
                    last.then_inc(normed, 1)
                for par in range(2):
                    t = i * 2 + par
                    dve.wait_ge(logits_ps, t + 1)
                    dve.tensor_copy(logits[:, :, bass.ds(t * 4, 4)],
                                    logit_bank[par][:, 0:4 * E].rearrange("p (b e) -> p e b", b=4)
                                    ).then_inc(logits_out, 1)
                link.end()

        @block.scalar
        def _(act):
            with act.Fori(0, NTURN // 2) as i:
                for par in range(2):
                    act.wait_ge(xT_ps, i * 2 + par + 1)
                    act.copy(xT[par][:, :], turn_bank[par][:, :]).then_inc(xT_ready, 1)

        @block.tensor
        def _(pe):
            pe.wait_ge(loaded, 16)
            with pe.Fori(0, NTURN // 2) as i:
                for par in range(2):
                    pe.wait_ge(kept, i * 2 + par + 1)
                    for b in range(4):
                        last = pe.transpose(turn_bank[par][:, b * P:(b + 1) * P], xn[par][:, b, :], net.ident[:, :])
                    last.then_inc(xT_ps, 1)
                pe.wait_ge(logits_out, i * 2)
                for par in range(2):
                    pe.wait_ge(xT_ready, i * 2 + par + 1)
                    for b in range(4):
                        last = pe.matmul(logit_bank[par][:, b * E:(b + 1) * E], xT[par][:, b * P:(b + 1) * P],
                                         wg[:, :], start=True, stop=True)
                    last.then_inc(logits_ps, 1)


def route(nc, net, name, E, capacity, consts, routed, logits):
    grouped = capacity is not None
    with ExitStack() as ctx:
        def sb(n, shape, dt=F32):
            return ctx.enter_context(nc.sbuf_tensor(f"{name}r_{n}", shape, dt))

        def sem(n):
            return net.sem(f"{name}r_{n}")

        B, W = NBATCH, E * NBATCH
        lower = sb("lower", [P, P]); whole = sb("whole", [P, P]); reset = sb("reset", [P, E, B])
        base = sb("base", [P, E]); one = sb("one", [P, E])
        hot = [sb(f"hot{i}", [P, E, B]) for i in range(2)]
        left = sb("left", [P, E, B]); count = [sb(f"count{i}", [P, E, B]) for i in range(2)]
        top = [sb(f"top{i}", [P, B]) for i in range(2)]
        least = sb("least", [P, B]); gap = sb("gap", [P, 2, B]); total = sb("total", [P, B])
        rank = sb("rank", [P, 2, B]); start = sb("start", [P, 2, B]); keep = sb("keep", [P, 2, B])
        slot = sb("slot", [P, 2, B]); sizes = sb("sizes", [P, E])
        loaded, chain = sem("loaded"), sem("chain")
        less_top, exp_done, counts_ready, ranks_ps = (
            sem("less_top"), sem("exp_done"), sem("counts_ready"), sem("ranks_ps"))
        shape = [P, B, E]

        def by_token(tile):
            return tile[:, :, :].rearrange("p e b -> p b e")

        def flat(tile):
            return tile[:, :, :].rearrange("p e b -> p (e b)")

        sets = hot if grouped else [left]
        half = W // 2 if grouped else W
        banks = [net.banks[2 * r:2 * r + 2] if grouped else [net.banks[0]] for r in range(len(sets))]

        block = ctx.enter_context(nc.Block())

        @block.sync
        def _(sp):
            for dst_ap, s in ((lower[:, :], consts["lower"]), (whole[:, :], consts["whole"]),
                              (reset[:, :, :], consts["reset"]), (base[:, :], consts["base"])):
                sp.dma_start(dst_ap, s).then_inc(loaded, 16)
            sp.wait_ge(loaded, 64)

        @block.scalar
        def _(act):
            act.wait_ge(less_top, 1)
            if grouped:
                act.activation(flat(left), flat(left), ACT.Exp)
            act.activation(gap[:, 0, :], gap[:, 0, :], ACT.Exp).then_inc(exp_done, 1)

        @block.vector
        def _(dve):
            link = Link(dve, chain, 0, 0)
            dve.wait_ge(loaded, 64)
            top_two(dve, link, net, by_token(logits), B, E,
                    dict(top=[top[0][:, :], top[1][:, :]], hot=[by_token(hot[0]), by_token(hot[1])],
                         least=least[:, :], left=by_token(left)))
            if grouped:
                link(dve.tensor_tensor(by_token(left), by_token(logits),
                                       top[0][:, :].unsqueeze(2).to_broadcast(shape), ALU.subtract))
            dve.tensor_tensor(gap[:, 0, :], top[1][:, :], top[0][:, :], ALU.subtract).then_inc(less_top, 1)
            dve.wait_ge(exp_done, 1)
            if grouped:
                link(dve.tensor_reduce(total[:, :], by_token(left), AX_X, ALU.add))
            else:
                link(dve.tensor_scalar(total[:, :], gap[:, 0, :], 1.0, None, ALU.add))
            link(dve.reciprocal(routed.gate[:, 0, :], total[:, :]))
            link(dve.tensor_tensor(routed.gate[:, 1, :], gap[:, 0, :], routed.gate[:, 0, :], ALU.mult))
            if not grouped:
                link(dve.tensor_tensor(flat(left), flat(hot[0]), flat(hot[1]), ALU.add))
                link(dve.memset(one[:, :], 1.0))
            for r, s in enumerate(sets):
                link(dve.tensor_tensor_scan(flat(count[r]), flat(reset), flat(s), 0.0, ALU.mult, ALU.add))
            link(dve.tensor_copy(sizes[:, :], count[0][:, :, B - 1]))
            for r, s in enumerate(sets):
                link(dve.tensor_tensor(flat(count[r]), flat(count[r]), flat(s), ALU.subtract))
            if grouped:
                link(dve.tensor_tensor(count[1][:, :, :], count[1][:, :, :],
                                       sizes[:, :].unsqueeze(2).to_broadcast([P, E, B]), ALU.add))
            dve.sem_inc(counts_ready, 1)
            dve.wait_ge(ranks_ps, 1)
            if not grouped:
                link(dve.tensor_copy(sizes[:, :], net.banks[1][:, 0:E]))
                link(dve.tensor_tensor_scan(base[:, :], one[:, :], sizes[:, :], 0.0, ALU.mult, ALU.add))
                link(dve.tensor_tensor(base[:, :], base[:, :], sizes[:, :], ALU.subtract))
            for r in range(2):
                n = r if grouped else 0
                step = half // B
                for i, bank in enumerate(banks[n]):
                    link(dve.tensor_tensor(left[:, i * step:(i + 1) * step, :], hot[r][:, i * step:(i + 1) * step, :],
                                           bank[:, 0:half].rearrange("p (e b) -> p e b", b=B), ALU.mult))
                link(dve.tensor_reduce(rank[:, r, :], by_token(left), AX_X, ALU.add))
                link(dve.tensor_tensor(left[:, :, :], hot[r][:, :, :],
                                       base[:, :].unsqueeze(2).to_broadcast([P, E, B]), ALU.mult))
                link(dve.tensor_reduce(start[:, r, :], by_token(left), AX_X, ALU.add))
            link(dve.tensor_tensor(slot[:, :, :], rank[:, :, :], start[:, :, :], ALU.add))
            if grouped:
                link(dve.tensor_scalar(keep[:, :, :], rank[:, :, :], float(capacity), None, ALU.is_lt))
                link(dve.tensor_tensor(routed.gate[:, :, :], routed.gate[:, :, :], keep[:, :, :], ALU.mult))
                link(dve.tensor_tensor(total[:, :], routed.gate[:, 0, :], routed.gate[:, 1, :], ALU.add))
                link(dve.tensor_scalar(total[:, :], total[:, :], 1e-9, None, ALU.max))
                link(dve.reciprocal(least[:, :], total[:, :]))
                link(dve.tensor_tensor(routed.gate[:, :, :], routed.gate[:, :, :],
                                       least[:, :].unsqueeze(1).to_broadcast([P, 2, B]), ALU.mult))
                for out, other in ((routed.write, SLOTS_1 + 1), (routed.read, SLOTS_1)):
                    link(dve.tensor_scalar(start[:, :, :], slot[:, :, :], -float(other), None, ALU.add))
                    link(dve.tensor_tensor(start[:, :, :], start[:, :, :], keep[:, :, :], ALU.mult))
                    link(dve.tensor_scalar(out[:, :, :].rearrange("p b r -> p r b"), start[:, :, :],
                                           float(other), None, ALU.add))
            else:
                link(dve.tensor_copy(routed.write[:, :, :].rearrange("p b r -> p r b"), slot[:, :, :]))
                link(dve.tensor_copy(routed.read[:, :, :].rearrange("p b r -> p r b"), slot[:, :, :]))

        @block.tensor
        def _(pe):
            pe.wait_ge(counts_ready, 1)
            for r, s in enumerate(sets):
                for i, bank in enumerate(banks[r]):
                    at = slice(i * half, (i + 1) * half)
                    pe.matmul(bank[:, 0:half], lower[:, :], flat(s)[:, at], start=True, stop=False)
                    last = pe.matmul(bank[:, 0:half], whole[:, :], flat(count[r])[:, at], start=False, stop=True)
            if not grouped:
                last = pe.matmul(net.banks[1][:, 0:E], whole[:, :], sizes[:, :], start=True, stop=True)
            last.then_inc(ranks_ps, 1)


def carry_wait(pool, net, idle, carried, before):
    pool.wait_ge(carried, before)
    pool.tensor_tensor(idle[:, :], net.plus_half[:, 0:1], net.plus_half[:, 0:1], ALU.mult).then_inc(carried, 1)


def scatter_rows(nc, net, name, routed, slots_dram, n_slots):
    with ExitStack() as ctx:
        def sb(n, shape, dt=F32):
            return ctx.enter_context(nc.sbuf_tensor(f"{name}s_{n}", shape, dt))

        rows = [sb(f"rows{i}", [P, 4, P]) for i in range(2)]
        where = [sb(f"where{i}", [P, 4, 2], U32) for i in range(2)]
        idle = sb("idle", [P, 1])
        staged, carried = net.sem(f"{name}s_staged"), net.sem(f"{name}s_carried")
        written = [net.sem(f"{name}s_written{i}") for i in range(2)]
        block = ctx.enter_context(nc.Block())

        @block.vector
        def _(dve):
            with dve.Fori(0, NTURN // 2) as i:
                for par in range(2):
                    t = i * 2 + par
                    dve.wait_ge(written[par], i * 8 * 16)
                    dve.tensor_copy(rows[par][:, :, :], routed.xn[:, bass.ds(t * 4, 4), :])
                    dve.tensor_copy(where[par][:, :, :], routed.write[:, bass.ds(t * 4, 4), :]).then_inc(staged, 1)

        @block.gpsimd
        def _(pool):
            with pool.Fori(0, NTURN // 2) as i:
                for par in range(2):
                    pool.wait_ge(staged, i * 2 + par + 1)
                    carry_wait(pool, net, idle, carried, i * 2 + par)
                    for b in range(4):
                        for r in range(2):
                            pool.indirect_dma_start(
                                slots_dram[:, :], bass.IndirectOffsetOnAxis(where[par][:, b, r:r + 1], 0),
                                rows[par][:, b, :], None, bounds_check=n_slots - 1,
                                oob_is_err=False).then_inc(written[par], 16)
            for par in range(2):
                pool.wait_ge(written[par], NTURN // 2 * 8 * 16)


def combine_rows(nc, net, name, routed, rows_dram, n_rows, final):
    with ExitStack() as ctx:
        def sb(n, shape, dt=F32):
            return ctx.enter_context(nc.sbuf_tensor(f"{name}c_{n}", shape, dt))

        def sem(n):
            return net.sem(f"{name}c_{n}")

        x = net.x
        got = [[sb(f"got{i}{r}", [P, 4, P]) for r in range(2)] for i in range(2)]
        where = [sb(f"where{i}", [P, 4, 2], U32) for i in range(2)]
        acc = sb("acc", [P, 4, P]); stats = sb("stats", [P, 4, 6]); mean_var = sb("mean_var", [P, 4, 2])
        rstd = sb("rstd", [P, 4]); idle = sb("idle", [P, 1]); pool_idle = sb("pool_idle", [P, 1])
        gain = sb("gain", [P, P]); offset = sb("offset", [P, P])
        loaded, staged, chain, used = sem("loaded"), sem("staged"), sem("chain"), sem("used")
        var_ready, rstd_ready = sem("var_ready"), sem("rstd_ready")
        chain2, carried = sem("chain2"), sem("carried")
        gathered = [sem(f"gathered{i}") for i in range(2)]
        LINKS = 7 if final else 2
        block = ctx.enter_context(nc.Block())

        if final:
            @block.sync
            def _(sp):
                sp.dma_start(gain[:, :], final[0]).then_inc(loaded, 16)
                sp.dma_start(offset[:, :], final[1]).then_inc(loaded, 16)
                sp.wait_ge(loaded, 32)

        @block.scalar
        def _(act):
            with act.Fori(0, NTURN // 2) as i:
                for par in range(2):
                    t = i * 2 + par
                    act.wait_ge(gathered[par], i * 8 * 16)
                    act.copy(where[par][:, :, :],
                             routed.read[:, bass.ds(t * 4, 4), :]).then_inc(staged, 1)

        @block.gpsimd
        def _(pool):
            with pool.Fori(0, NTURN // 2) as i:
                for par in range(2):
                    t = i * 2 + par
                    pool.wait_ge(staged, t + 1)
                    pool.wait_ge(used, i * 2)
                    carry_wait(pool, net, pool_idle, carried, i * 2 + par)
                    for b in range(4):
                        for r in range(2):
                            pool.indirect_dma_start(
                                got[par][r][:, b, :], None, rows_dram[:, :],
                                bass.IndirectOffsetOnAxis(where[par][:, b, r:r + 1], 0),
                                bounds_check=n_rows - 1, oob_is_err=False).then_inc(gathered[par], 16)
                if final:
                    for par in range(2):
                        pool.wait_ge(var_ready, i * 2 + par + 1)
                        pool.tensor_tensor(rstd[:, :], rstd[:, :], net.minus_half[:, 0:4],
                                           ALU.pow).then_inc(rstd_ready, 1)

        @block.vector
        def _(dve):
            if final:
                dve.wait_ge(loaded, 32)
            with dve.Fori(0, NTURN // 2) as i:
                link = Link(dve, chain, i, 2 * LINKS)
                for par in range(2):
                    t = i * 2 + par
                    dve.wait_ge(gathered[par], (i + 1) * 8 * 16)
                    start = routed.xn if final else x
                    for b in range(4):
                        last = dve.scalar_tensor_tensor(acc[:, b, :], got[par][0][:, b, :],
                                                        routed.gate[:, 0, bass.ds(t * 4 + b, 1)],
                                                        start[:, t * 4 + b, :], ALU.mult, ALU.add)
                    link(last)
                    for b in range(4):
                        out = acc[:, b, :] if final else x[:, t * 4 + b, :]
                        last = dve.scalar_tensor_tensor(out, got[par][1][:, b, :],
                                                        routed.gate[:, 1, bass.ds(t * 4 + b, 1)],
                                                        acc[:, b, :], ALU.mult, ALU.add)
                    link(last)
                    dve.sem_inc(used, 1)
                    if final:
                        shape = [P, 4, P]
                        for b in range(4):
                            last = dve.bn_stats(stats[:, b, :], acc[:, b, :])
                        link(last)
                        dve.memset(idle[:, :], 0.0)
                        for b in range(4):
                            last = dve.bn_aggr(mean_var[:, b, :], stats[:, b, :])
                        link(last)
                        dve.tensor_scalar(rstd[:, :], mean_var[:, :, 1], 1e-6, None, ALU.add).then_inc(var_ready, 1)
                        dve.wait_ge(rstd_ready, t + 1)
                        for b in range(4):
                            last = dve.tensor_scalar(acc[:, b, :], acc[:, b, :], mean_var[:, b, 0:1],
                                                     rstd[:, b:b + 1], ALU.subtract, ALU.mult)
                        link(last)
                        link(dve.tensor_tensor(acc[:, :, :], acc[:, :, :],
                                               gain[:, :].unsqueeze(1).to_broadcast(shape), ALU.mult))
                        link(dve.tensor_tensor(acc[:, :, :], acc[:, :, :],
                                               offset[:, :].unsqueeze(1).to_broadcast(shape), ALU.add))
                        tokens = x[:, bass.ds(t * 4, 4), :]
                        dve.tensor_tensor(tokens, tokens, acc[:, :, :], ALU.add).then_inc(chain2, 1)
                        dve.wait_ge(chain2, t + 1)
                link.end()



def chunk_experts(nc, net, w1_dram, w2_dram, slots_dram, rows_dram):
    E, FC = 8, 4
    with ExitStack() as ctx:
        def sb(n, shape, dt=F32):
            return ctx.enter_context(nc.sbuf_tensor(f"L2e_{n}", shape, dt))

        def sem(n):
            return net.sem(f"L2e_{n}")

        w1 = [sb(f"w1{i}", [P, FC * P]) for i in range(2)]; w2 = [sb(f"w2{i}", [P, FC, P]) for i in range(2)]
        rows = [sb(f"rows{i}", [P, 4, P]) for i in range(2)]; xT = [sb(f"xT{i}", [P, 4 * P]) for i in range(2)]
        hT = [sb(f"hT{i}", [P, FC, 4 * P]) for i in range(2)]; y = [sb(f"y{i}", [P, 4, P]) for i in range(2)]
        hid_bank, y_bank, turn_bank = net.banks[0:4], net.banks[4:6], net.banks[6:8]
        w_loaded = [sem(f"w_loaded{i}") for i in range(2)]
        rows_loaded = [sem(f"rows_loaded{i}") for i in range(2)]
        stored = [sem(f"stored{i}") for i in range(2)]
        xT_ps, xT_ready, hid_ready, hid_out, y_ready, y_out = (
            sem(n) for n in ("xT_ps", "xT_ready", "hid_ready", "hid_out", "y_ready", "y_out"))
        slots = slots_dram.rearrange("(h q p) d -> h p q d", p=P, q=4)
        outs = rows_dram.rearrange("(h q p) d -> h p q d", p=P, q=4)
        NI = E // 2
        block = ctx.enter_context(nc.Block())

        @block.sync
        def _(sp):
            with sp.Fori(0, NI) as i:
                for n in range(4):
                    h, par = i * 4 + n, n % 2
                    if n % 2 == 0:
                        e = n // 2
                        sp.wait_ge(y_ready, i * 4)
                        sp.dma_start(w1[e][:, :], w1_dram[:, i * 2 + e, :]).then_inc(w_loaded[e], 16)
                        sp.dma_start(w2[e][:, :, :], w2_dram[:, i * 2 + e, :, :]).then_inc(w_loaded[e], 16)
                    if n >= 2:
                        sp.wait_ge(xT_ps, i * 4 + n - 1)
                    else:
                        sp.wait_ge(xT_ps, i * 4)
                    sp.dma_start(rows[par][:, :, :], slots[h, :, :, :]).then_inc(rows_loaded[par], 16)

        @block.gpsimd
        def _(pool):
            with pool.Fori(0, NI) as i:
                for n in range(4):
                    pool.wait_ge(y_out, i * 4 + n + 1)
                    pool.dma_start(outs[i * 4 + n, :, :, :], y[n % 2][:, :, :]).then_inc(stored[n % 2], 16)
            for par in range(2):
                pool.wait_ge(stored[par], NI * 2 * 16)

        @block.scalar
        def _(act):
            with act.Fori(0, NI) as i:
                for n in range(4):
                    h = i * 4 + n
                    for c in range(FC):
                        act.wait_ge(hid_ready, h * FC + c + 1)
                        if c == 0 and n >= 2:
                            act.wait_ge(y_ready, h - 1)
                        elif c == 0:
                            act.wait_ge(y_ready, i * 4)
                        act.activation(hT[n % 2][:, c, :], hid_bank[c][:, :], ACT.Gelu).then_inc(hid_out, 1)

        @block.vector
        def _(dve):
            with dve.Fori(0, NI) as i:
                for n in range(5):
                    if n < 4:
                        h = i * 4 + n
                        dve.wait_ge(xT_ps, h + 1)
                        dve.tensor_copy(xT[n % 2][:, :], turn_bank[n % 2][:, :]).then_inc(xT_ready, 1)
                    if n:
                        h, par = i * 4 + n - 1, (n - 1) % 2
                        dve.wait_ge(y_ready, h + 1)
                        dve.wait_ge(stored[par], 16 * (i * 2 + (n - 1) // 2))
                        dve.tensor_copy(y[par][:, :, :],
                                        y_bank[par][:, :].rearrange("p (q d) -> p q d", q=4)).then_inc(y_out, 1)

        @block.tensor
        def _(pe):
            def turn(i, n):
                h = i * 4 + n
                pe.wait_ge(rows_loaded[n % 2], 16 * (i * 2 + n // 2 + 1))
                for q in range(4):
                    last = pe.transpose(turn_bank[n % 2][:, q * P:(q + 1) * P], rows[n % 2][:, q, :], net.ident[:, :])
                last.then_inc(xT_ps, 1)

            def hidden(i, n):
                h, e = i * 4 + n, n // 2
                pe.wait_ge(xT_ready, h + 1)
                if n % 2 == 0:
                    pe.wait_ge(w_loaded[e], 32 * (i + 1))
                for c in range(FC):
                    pe.wait_ge(hid_out, i * 4 * FC + max(n * FC + c - 3, 0))
                    pe.matmul(hid_bank[c][:, :], w1[e][:, c * P:(c + 1) * P], xT[n % 2][:, :],
                              start=True, stop=True).then_inc(hid_ready, 1)

            def output(i, n):
                h, e = i * 4 + n, n // 2
                pe.wait_ge(hid_out, (h + 1) * FC)
                pe.wait_ge(y_out, i * 4 + max(n - 1, 0))
                for q in range(4):
                    for c in range(FC):
                        last = pe.matmul(y_bank[n % 2][:, q * P:(q + 1) * P], hT[n % 2][:, c, q * P:(q + 1) * P],
                                         w2[e][:, c, :], start=(c == 0), stop=(c == FC - 1))
                last.then_inc(y_ready, 1)

            with pe.Fori(0, NI) as i:
                turn(i, 0)
                hidden(i, 0)
                for n in range(4):
                    if n + 1 < 4:
                        turn(i, n + 1)
                        hidden(i, n + 1)
                    output(i, n)


def chunked_moe_stage(nc, net):
    with ExitStack() as ctx:
        routed = Routed(nc, ctx, "L2f")
        with ExitStack() as part:
            logits = part.enter_context(nc.sbuf_tensor("L2f_logits", [P, 8, NBATCH], F32))
            norm_and_logits(nc, net, "L2f", 8, net.t["L2f_wg"], routed, logits)
            route(nc, net, "L2f", 8, None, dict(lower=net.t["lower"], whole=net.t["ones"], reset=net.t["reset8"],
                                                base=net.t["base8"]), routed, logits)
        scatter_rows(nc, net, "L2f", routed, net.slots2, SLOTS_2)
        chunk_experts(nc, net, net.t["L2f_w1"], net.t["L2f_w2"], net.slots2, net.rows2)
        combine_rows(nc, net, "L2f", routed, net.rows2, SLOTS_2, None)


def hidden_experts(nc, net, w1_dram, b1_dram, slots_dram, rows_dram):
    E, FF, Q = 24, 512, 3
    with ExitStack() as ctx:
        def sb(n, shape, dt=F32):
            return ctx.enter_context(nc.sbuf_tensor(f"L1h_{n}", shape, dt))

        def sem(n):
            return net.sem(f"L1h_{n}")

        w1 = [sb(f"w1{i}", [P, FF]) for i in range(2)]; b1 = [sb(f"b1{i}", [P, FF]) for i in range(2)]
        rows = [sb(f"rows{i}", [P, Q, P]) for i in range(2)]; xT = [sb(f"xT{i}", [P, Q * P]) for i in range(2)]
        hid = [sb(f"hid{i}", [P, Q, FF]) for i in range(2)]
        hid_bank, turn_bank = net.banks[0:6], net.banks[6:8]
        loaded = [sem(f"loaded{i}") for i in range(2)]; stored = [sem(f"stored{i}") for i in range(2)]
        xT_ps, xT_ready, hid_ready, hid_out = (sem(n) for n in ("xT_ps", "xT_ready", "hid_ready", "hid_out"))
        slots = slots_dram.rearrange("(e q p) d -> e p q d", p=P, q=Q)
        outs = rows_dram[0:SLOTS_1, :].rearrange("(e q p) f -> e p q f", p=P, q=Q)
        block = ctx.enter_context(nc.Block())

        @block.sync
        def _(sp):
            with sp.Fori(0, E // 2) as i:
                for par in range(2):
                    e = i * 2 + par
                    sp.wait_ge(hid_out, i * 2 * Q)
                    sp.dma_start(rows[par][:, :, :], slots[e, :, :, :]).then_inc(loaded[par], 16)
                    sp.dma_start(w1[par][:, :], w1_dram[:, e, :]).then_inc(loaded[par], 16)
                    sp.dma_start(b1[par][:, :], b1_dram[bass.ds(e, 1), :].to_broadcast([P, FF])).then_inc(loaded[par], 16)

        @block.gpsimd
        def _(pool):
            with pool.Fori(0, E // 2) as i:
                for par in range(2):
                    e = i * 2 + par
                    pool.wait_ge(hid_out, (e + 1) * Q)
                    pool.dma_start(outs[e, :, :, :], hid[par][:, :, :]).then_inc(stored[par], 16)
            for par in range(2):
                pool.wait_ge(stored[par], E // 2 * 16)

        @block.scalar
        def _(act):
            with act.Fori(0, E // 2) as i:
                for par in range(2):
                    act.wait_ge(xT_ps, i * 2 + par + 1)
                    act.copy(xT[par][:, :], turn_bank[par][:, 0:Q * P]).then_inc(xT_ready, 1)

        @block.vector
        def _(dve):
            with dve.Fori(0, E // 2) as i:
                for par in range(2):
                    dve.wait_ge(stored[par], i * 16)
                    for q in range(Q):
                        dve.wait_ge(hid_ready, (i * 2 + par) * Q + q + 1)
                        dve.tensor_tensor(hid[par][:, q, :], hid_bank[par * Q + q][:, :], b1[par][:, :],
                                          ALU.add).then_inc(hid_out, 1)

        @block.tensor
        def _(pe):
            with pe.Fori(0, E // 2) as i:
                for par in range(2):
                    pe.wait_ge(loaded[par], 48 * (i + 1))
                    for q in range(Q):
                        last = pe.transpose(turn_bank[par][:, q * P:(q + 1) * P], rows[par][:, q, :], net.ident[:, :])
                    last.then_inc(xT_ps, 1)
                for par in range(2):
                    pe.wait_ge(xT_ready, i * 2 + par + 1)
                    pe.wait_ge(hid_out, i * 2 * Q)
                    for q in range(Q):
                        pe.matmul(hid_bank[par * Q + q][:, :], xT[par][:, q * P:(q + 1) * P], w1[par][:, :],
                                  start=True, stop=True).then_inc(hid_ready, 1)


def mix_hidden(nc, net, gain_dram, offset_dram, routed, rows_dram):
    FF = 512
    with ExitStack() as ctx:
        def sb(n, shape, dt=F32):
            return ctx.enter_context(nc.sbuf_tensor(f"L1m_{n}", shape, dt))

        def sem(n):
            return net.sem(f"L1m_{n}")

        gain = sb("gain", [P, FF]); offset = sb("offset", [P, FF])
        got = [[sb(f"got{b}{r}", [P, FF]) for r in range(2)] for b in range(4)]
        read = sb("read", [P, 4, 2], U32); write = sb("write", [P, 4, 2], U32)
        mixed = [sb(f"mixed{b}", [P, FF]) for b in range(4)]; out = [sb(f"out{b}", [P, FF]) for b in range(4)]
        stats = sb("stats", [P, 4, 6]); mean_var = sb("mean_var", [P, 4, 2]); rstd = sb("rstd", [P, 4])
        idle = sb("idle", [P, 1]); pool_idle = sb("pool_idle", [P, 1])
        loaded, read_staged, write_staged, chain = sem("loaded"), sem("read_staged"), sem("write_staged"), sem("chain")
        scaled, mixed_ready, var_ready, rstd_ready, normed = (
            sem(n) for n in ("scaled", "mixed_ready", "var_ready", "rstd_ready", "normed"))
        gained, affine, out_ready, carried = sem("gained"), sem("affine"), sem("out_ready"), sem("carried")
        gathered = [sem(f"gathered{b}") for b in range(4)]; written = [sem(f"written{b}") for b in range(4)]
        block = ctx.enter_context(nc.Block())

        @block.sync
        def _(sp):
            sp.dma_start(gain[:, :], gain_dram).then_inc(loaded, 16)
            sp.dma_start(offset[:, :], offset_dram).then_inc(loaded, 16)
            sp.wait_ge(loaded, 32)

        def gather(pool, b):
            for r in range(2):
                pool.indirect_dma_start(got[b][r][:, :], None, rows_dram[:, :],
                                        bass.IndirectOffsetOnAxis(read[:, b, r:r + 1], 0),
                                        bounds_check=SLOTS_1, oob_is_err=False).then_inc(gathered[b], 16)

        @block.gpsimd
        def _(pool):
            with pool.Fori(0, NTURN) as t:
                pool.wait_ge(read_staged, t + 1)
                carry_wait(pool, net, pool_idle, carried, t * 5)
                for b in range(4):
                    gather(pool, b)
                for b in range(4):
                    pool.wait_ge(var_ready, t * 4 + b + 1)
                    pool.tensor_tensor(rstd[:, b:b + 1], rstd[:, b:b + 1], net.minus_half[:, 0:1],
                                       ALU.pow).then_inc(rstd_ready, 1)
                pool.wait_ge(write_staged, t + 1)
                for b in range(4):
                    pool.wait_ge(out_ready, t * 4 + b + 1)
                    carry_wait(pool, net, pool_idle, carried, t * 5 + 1 + b)
                    for r in range(2):
                        pool.indirect_dma_start(rows_dram[0:SLOTS_1, :], bass.IndirectOffsetOnAxis(write[:, b, r:r + 1], 0),
                                                out[b][:, :], None, bounds_check=SLOTS_1 - 1,
                                                oob_is_err=False).then_inc(written[b], 16)
            for b in range(4):
                pool.wait_ge(written[b], NTURN * 32)

        @block.scalar
        def _(act):
            with act.Fori(0, NTURN) as t:
                now = bass.ds(t * 4, 4)
                for b in range(4):
                    act.wait_ge(gathered[b], t * 32)
                act.copy(read[:, :, :], routed.read[:, now, :]).then_inc(read_staged, 1)
                for b in range(4):
                    act.wait_ge(gathered[b], (t + 1) * 32)
                    act.wait_ge(normed, t * 4)
                    act.activation(mixed[b][:, :], got[b][0][:, :], ACT.Copy,
                                   scale=routed.gate[:, 0, bass.ds(t * 4 + b, 1)]).then_inc(scaled, 1)
                for b in range(4):
                    act.wait_ge(written[b], t * 32)
                act.copy(write[:, :, :], routed.write[:, now, :]).then_inc(write_staged, 1)
                for b in range(4):
                    act.wait_ge(affine, t * 4 + b + 1)
                    act.activation(out[b][:, :], mixed[b][:, :], ACT.Relu).then_inc(out_ready, 1)

        @block.vector
        def _(dve):
            dve.wait_ge(loaded, 32)
            with dve.Fori(0, NTURN) as t:
                link = Link(dve, chain, t, 2 * 4)
                for b in range(4):
                    dve.wait_ge(scaled, t * 4 + b + 1)
                    dve.scalar_tensor_tensor(mixed[b][:, :], got[b][1][:, :], routed.gate[:, 1, bass.ds(t * 4 + b, 1)],
                                             mixed[b][:, :], ALU.mult, ALU.add).then_inc(mixed_ready, 1)
                    dve.wait_ge(mixed_ready, t * 4 + b + 1)
                    link(dve.bn_stats(stats[:, b, :], mixed[b][:, :]))
                    dve.memset(idle[:, :], 0.0)
                    link(dve.bn_aggr(mean_var[:, b, :], stats[:, b, :]))
                    dve.tensor_scalar(rstd[:, b:b + 1], mean_var[:, b, 1:2], 1e-6, None, ALU.add).then_inc(var_ready, 1)
                link.end()
                for b in range(4):
                    dve.wait_ge(rstd_ready, t * 4 + b + 1)
                    dve.tensor_scalar(mixed[b][:, :], mixed[b][:, :], mean_var[:, b, 0:1], rstd[:, b:b + 1],
                                      ALU.subtract, ALU.mult).then_inc(normed, 1)
                    dve.wait_ge(normed, t * 4 + b + 1)
                    dve.tensor_tensor(mixed[b][:, :], mixed[b][:, :], gain[:, :], ALU.mult).then_inc(gained, 1)
                    dve.wait_ge(gained, t * 4 + b + 1)
                    dve.tensor_tensor(mixed[b][:, :], mixed[b][:, :], offset[:, :], ALU.add).then_inc(affine, 1)


def output_experts(nc, net, w2_dram, b2_dram, hidden_dram, rows_dram):
    E, FF, Q, FC = 24, 512, 3, 4
    with ExitStack() as ctx:
        def sb(n, shape, dt=F32):
            return ctx.enter_context(nc.sbuf_tensor(f"L1o_{n}", shape, dt))

        def sem(n):
            return net.sem(f"L1o_{n}")

        w2 = [sb(f"w2{i}", [P, FC, P]) for i in range(2)]; b2 = [sb(f"b2{i}", [P, P]) for i in range(2)]
        hid = [sb(f"hid{i}", [P, Q, FF]) for i in range(2)]
        hT = [sb(f"hT{i}", [P, Q, FC, P]) for i in range(2)]; y = [sb(f"y{i}", [P, Q, P]) for i in range(2)]
        turn_bank, y_bank = net.banks[0:6], net.banks[6:8]
        loaded = [sem(f"loaded{i}") for i in range(2)]; stored = [sem(f"stored{i}") for i in range(2)]
        hT_ps, hT_ready, y_ready, y_out = (sem(n) for n in ("hT_ps", "hT_ready", "y_ready", "y_out"))
        slots = hidden_dram[0:SLOTS_1, :].rearrange("(e q p) f -> e p q f", p=P, q=Q)
        outs = rows_dram[0:SLOTS_1, :].rearrange("(e q p) d -> e p q d", p=P, q=Q)
        block = ctx.enter_context(nc.Block())

        @block.sync
        def _(sp):
            with sp.Fori(0, E // 2) as i:
                for par in range(2):
                    e = i * 2 + par
                    sp.wait_ge(y_out, i * 2)
                    sp.dma_start(hid[par][:, :, :], slots[e, :, :, :]).then_inc(loaded[par], 16)
                    sp.dma_start(w2[par][:, :, :], w2_dram[:, e, :, :]).then_inc(loaded[par], 16)
                    sp.dma_start(b2[par][:, :], b2_dram[bass.ds(e, 1), :].to_broadcast([P, P])).then_inc(loaded[par], 16)

        @block.gpsimd
        def _(pool):
            with pool.Fori(0, E // 2) as i:
                for par in range(2):
                    e = i * 2 + par
                    pool.wait_ge(y_out, e + 1)
                    pool.dma_start(outs[e, :, :, :], y[par][:, :, :]).then_inc(stored[par], 16)
            for par in range(2):
                pool.wait_ge(stored[par], E // 2 * 16)

        @block.scalar
        def _(act):
            with act.Fori(0, E // 2) as i:
                for par in range(2):
                    for q in range(Q):
                        act.wait_ge(hT_ps, (i * 2 + par) * Q + q + 1)
                        act.copy(hT[par][:, q, :, :], turn_bank[par * Q + q][:, :].rearrange("p (c t) -> p c t", c=FC)
                                 ).then_inc(hT_ready, 1)

        @block.vector
        def _(dve):
            with dve.Fori(0, E // 2) as i:
                for par in range(2):
                    dve.wait_ge(stored[par], i * 16)
                    dve.wait_ge(y_ready, i * 2 + par + 1)
                    dve.tensor_tensor(y[par][:, :, :], y_bank[par][:, 0:Q * P].rearrange("p (q d) -> p q d", q=Q),
                                      b2[par][:, :].unsqueeze(1).to_broadcast([P, Q, P]), ALU.add).then_inc(y_out, 1)

        @block.tensor
        def _(pe):
            with pe.Fori(0, E // 2) as i:
                for par in range(2):
                    pe.wait_ge(loaded[par], 48 * (i + 1))
                    for q in range(Q):
                        for c in range(FC):
                            last = pe.transpose(turn_bank[par * Q + q][:, c * P:(c + 1) * P],
                                                hid[par][:, q, c * P:(c + 1) * P], net.ident[:, :])
                        last.then_inc(hT_ps, 1)
                for par in range(2):
                    pe.wait_ge(hT_ready, (i * 2 + par + 1) * Q)
                    pe.wait_ge(y_out, i * 2)
                    for q in range(Q):
                        for c in range(FC):
                            last = pe.matmul(y_bank[par][:, q * P:(q + 1) * P], hT[par][:, q, c, :], w2[par][:, c, :],
                                             start=(c == 0), stop=(c == FC - 1))
                    last.then_inc(y_ready, 1)


def capacity_moe_stage(nc, net):
    with ExitStack() as ctx:
        t = net.t
        routed = Routed(nc, ctx, "L1f")
        with ExitStack() as part:
            logits = part.enter_context(nc.sbuf_tensor("L1f_logits", [P, 24, NBATCH], F32))
            norm_and_logits(nc, net, "L1f", 24, t["L1f_wg"], routed, logits)
            route(nc, net, "L1f", 24, 86, dict(lower=t["lower32"], whole=t["ones32"], reset=t["reset24"],
                                               base=t["base24"]), routed, logits)
        scatter_rows(nc, net, "L1f", routed, net.slots1, SLOTS_1)
        hidden_experts(nc, net, t["L1f_w1"], t["L1f_b1"], net.slots1, net.hidden1)
        mix_hidden(nc, net, t["L1f_gain"], t["L1f_offset"], routed, net.hidden1)
        output_experts(nc, net, t["L1f_w2"], t["L1f_b2"], net.hidden1, net.rows1)
        combine_rows(nc, net, "L1f", routed, net.rows1, SLOTS_1 + 1, (t["L1f_out_w"], t["L1f_out_b"]))


def fill_zeros(nc, net):
    with ExitStack() as ctx:
        zeros = ctx.enter_context(nc.sbuf_tensor("zeros", [P, SLOTS_1 // 4], F32))
        zeroed, filled = net.sem("zeroed"), net.sem("zeros_filled")
        with nc.Block() as block:
            @block.vector
            def _(dve):
                dve.memset(zeros[:, :], 0.0).then_inc(zeroed, 1)

            @block.sync
            def _(sp):
                sp.wait_ge(zeroed, 1)
                slots = net.slots1.rearrange("(a p r) d -> a p (r d)", a=4, p=P)
                for a in range(4):
                    sp.dma_start(slots[a, :, :], zeros[:, :]).then_inc(filled, 16)
                sp.dma_start(net.hidden1[SLOTS_1:SLOTS_1 + 1, :], zeros[0:1, 0:512]).then_inc(filled, 16)
                sp.dma_start(net.rows1[SLOTS_1:SLOTS_1 + 1, :], zeros[0:1, 0:P]).then_inc(filled, 16)
                sp.wait_ge(filled, 96)


def build(nc, t, out, stages):
    with ExitStack() as ctx:
        net = Net(nc, ctx)
        net.x = net.sb("x", [P, NBATCH, P])
        net.ident = net.sb("ident", [P, P])
        net.index64 = net.sb("index64", [P, 24])
        net.ones_row = net.sb("ones_row", [1, P])
        net.minus_half = net.sb("minus_half", [P, NBATCH])
        net.plus_half = net.sb("plus_half", [P, NBATCH])
        banks = [ctx.enter_context(nc.psum_tensor(f"bank{i}", [P, 512], F32)) for i in range(8)]
        net.banks = banks
        net.t = t
        net.slots2 = nc.dram_tensor("slots2", (SLOTS_2, P), F32).ap()
        net.slots1 = nc.dram_tensor("slots1", (SLOTS_1, P), F32).ap()
        net.hidden1 = nc.dram_tensor("hidden1", (SLOTS_1 + 1, 512), F32).ap()
        net.rows1 = nc.dram_tensor("rows1", (SLOTS_1 + 1, P), F32).ap()
        net.rows2 = nc.dram_tensor("rows2", (SLOTS_2, P), F32).ap()
        loaded = net.sem("start_loaded")
        with nc.Block() as block:
            @block.sync
            def _(sp):
                sp.dma_start(net.x[:, :, :], t["x"]).then_inc(loaded, 16)
                sp.dma_start(net.ident[:, :], t["ident"]).then_inc(loaded, 16)
                sp.dma_start(net.index64[:, :], t["index64"]).then_inc(loaded, 16)
                sp.wait_ge(loaded, 48)

            @block.vector
            def _(dve):
                dve.memset(net.ones_row[:, :], 1.0)
                dve.memset(net.minus_half[:, :], -0.5)
                dve.memset(net.plus_half[:, :], 0.5)

        if "L1f" in stages:
            fill_zeros(nc, net)

        def attention(layer, kind, heads, hd, biased, names):
            with ExitStack() as part:
                spec = dict(name=layer, kind=kind, heads=heads, hd=hd, biased=biased)
                w = {k: t[v] for k, v in names.items()}
                w["diag"], w["ctxT"] = t["diag"], t["ctxT"]
                (latent_stage if kind == "latent" else attention_stage)(nc, net, spec, w)

        if "L0x" in stages:
            attention("L0x", "cross", 16, 8, True,
                      dict(wq="L0_xattn_q_w", wk="L0k", wv="L0v", wo="L0o", bo="L0_xattn_proj_b",
                           bq="L0_xattn_q_b", bk="L0kb", bv="L0vb"))
        net.release_semaphores()
        if "L0f" in stages:
            dense_moe_stage(nc, net, dict(name="L0f", FF=512, kind="pre"), {k: t["L0f_" + k] for k in (
                "w1", "w2", "b1", "b2", "wg", "bg", "g_col", "b_col")})
        net.release_semaphores()
        if "L1x" in stages:
            attention("L1x", "cross", 16, 64, False,
                      dict(wq="L1_xattn_Wq", wk="L1_xattn_Wk", wv="L1_xattn_Wv", wo="L1o", bo="L1_xattn_bo"))
        net.release_semaphores()
        if "L1f" in stages:
            capacity_moe_stage(nc, net)
        net.release_semaphores()
        if "L2x" in stages:
            attention("L2x", "latent", 2, 64, False,
                      dict(wq="L2q", wlkv="L2lkv", wkv="L2kv", gamma="L2gamma", lat_g="L2lg", lat_b="L2lb",
                           ctx_g="L2xg", ctx_b="L2xb", ctx_tok="ctx_tok", mask="mask", wo="L2o", bo="L2_xattn_bo"))
        net.release_semaphores()
        if "L2f" in stages:
            chunked_moe_stage(nc, net)
        net.release_semaphores()
        if "L3x" in stages:
            attention("L3x", "cross", 8, 64, False,
                      dict(wq="L3_xattn_Wq", wk="L3_xattn_Wk", wv="L3_xattn_Wv", wo="L3o", bo="L3_xattn_bo"))
        net.release_semaphores()
        if "L3f" in stages:
            with ExitStack() as part:
                net.x1 = part.enter_context(nc.sbuf_tensor("x1", [P, NBATCH, P], F32))
                attention("L3s", "self", 16, 8, True,
                          {k: "L3s_" + k for k in ("wq", "wk", "wv", "wo", "bo", "bq", "bk", "bv")})
                dense_moe_stage(nc, net, dict(name="L3f", FF=256, kind="post"), {k: t["L3f_" + k] for k in (
                    "w1", "w2", "b1", "b2", "wg", "bg", "g_col", "b_col", "g1", "be1", "g2", "be2")})
        net.release_semaphores()
        stored = net.sem("stored")
        with nc.Block() as block:
            @block.sync
            def _(sp):
                sp.dma_start(out, net.x[:, :, :]).then_inc(stored, 16)
                sp.wait_ge(stored, 16)


def constants():
    p = np.arange(P)
    c = {"ident": np.eye(P, dtype=np.float32)}
    c["diag"] = (p[:, None] // 8 % 4 == np.arange(4)[None, :]).astype(np.float32)

    group = p // 32
    c["lower"] = (p[:, None] < p[None, :]).astype(np.float32)
    c["ones"] = np.ones((P, P), np.float32)
    c["lower32"] = c["lower"] * (group[:, None] == group[None, :])
    c["ones32"] = (group[:, None] == group[None, :]).astype(np.float32)
    for e in (8, 24):
        c[f"reset{e}"] = np.broadcast_to((np.arange(NBATCH) > 0).astype(np.float32), (P, e, NBATCH))
    c["base8"] = np.zeros((P, 8), np.float32)
    c["base24"] = (np.arange(24)[None, :] * 384 + group[:, None] * 86).astype(np.float32)
    c["index64"] = np.broadcast_to(np.arange(24, dtype=np.float32) - 64, (P, 24))
    return c


def layouts(i):
    a = {"x": i["x"].transpose(1, 0, 2), "ctxT": i["ctx_768"].transpose(2, 0, 1)}
    a["L0_xattn_q_w"] = i["L0_xattn_q_w"]
    a["L0k"], a["L0v"] = i["L0_xattn_kv_w"][:, :P], i["L0_xattn_kv_w"][:, P:]
    a["L0kb"], a["L0vb"] = i["L0_xattn_kv_b"][:P, None], i["L0_xattn_kv_b"][None, P:]
    a["L0_xattn_q_b"] = i["L0_xattn_q_b"][:, None]
    a["L0o"] = i["L0_xattn_proj_w"][:, None, :]
    a["L0_xattn_proj_b"] = i["L0_xattn_proj_b"][None, :]
    for n, key in (("L1", "L1o"), ("L3", "L3o")):
        for k in ("Wq", "Wk", "Wv"):
            a[f"{n}_xattn_{k}"] = i[f"{n}_xattn_{k}"]
        wo = i[f"{n}_xattn_Wo"]
        a[key] = wo.reshape(-1, P, P).transpose(1, 0, 2)
        a[f"{n}_xattn_bo"] = i[f"{n}_xattn_bo"][None, :]
    f = {k: i[f"L0_ffn_{k}"] for k in ("W1", "W2", "b1", "b2", "Wg", "bg", "gamma", "beta")}
    a["L0f_w1"] = f["W1"].transpose(2, 0, 1)
    a["L0f_w2"] = f["W2"].reshape(8, P, 4, P).transpose(3, 0, 2, 1)
    a["L0f_b1"] = f["b1"].reshape(8 * 4, P).T
    a["L0f_b2"], a["L0f_wg"], a["L0f_bg"] = f["b2"], f["Wg"].T, f["bg"][None, :]
    a["L0f_g_col"], a["L0f_b_col"] = f["gamma"][:, None], f["beta"][:, None]
    s = {k[7:]: v for k, v in i.items() if k.startswith("L3_ffn_")}
    for k in ("q", "k", "v"):
        a[f"L3s_w{k}"] = s[f"W{k}"]
        a[f"L3s_b{k}"] = s[f"b{k}"][None, :] if k == "v" else s[f"b{k}"][:, None]
    a["L3s_wo"], a["L3s_bo"] = s["Wo"][:, None, :], s["bo"][None, :]
    a["L3f_w1"] = s["W1"].transpose(1, 0, 2)
    a["L3f_w2"] = s["W2"].reshape(8, 2, P, P).transpose(2, 0, 1, 3)
    a["L3f_b1"] = s["b1"].reshape(8 * 2, P).T
    a["L3f_b2"], a["L3f_wg"], a["L3f_bg"] = s["b2"], s["gW"], s["gb"][None, :]
    a["L3f_g_col"], a["L3f_b_col"] = s["ln1_g"][:, None], s["ln1_b"][:, None]
    for k, n in (("g1", "ln1_g"), ("be1", "ln1_b"), ("g2", "ln2_g"), ("be2", "ln2_b")):
        a["L3f_" + k] = np.broadcast_to(s[n], (P, P))
    a["L2f_wg"] = i["L2_ffn_router_w"].T
    a["L2f_w1"] = i["L2_ffn_w1"].transpose(1, 0, 2)
    a["L2f_w2"] = i["L2_ffn_w2"].reshape(8, 4, P, P).transpose(2, 0, 1, 3)
    s = {k[7:]: v for k, v in i.items() if k.startswith("L1_ffn_")}
    a["L1f_wg"], a["L1f_w1"], a["L1f_b1"], a["L1f_b2"] = s["Wg"], s["W1"].transpose(1, 0, 2), s["b1"], s["b2"]
    a["L1f_w2"] = s["W2"].reshape(24, 4, P, P).transpose(2, 0, 1, 3)
    a["L1f_gain"], a["L1f_offset"] = (np.repeat(s[n], 32, axis=0) for n in ("ln_hid_w", "ln_hid_b"))
    a["L1f_out_w"], a["L1f_out_b"] = (np.broadcast_to(s[n], (P, P)) for n in ("ln_out_w", "ln_out_b"))
    a["ctx_tok"] = i["ctx_768"].transpose(1, 0, 2)
    a["mask"] = i["mask_BxS2_bk0"].reshape(1, -1)
    a["L2q"], a["L2kv"], a["L2lkv"] = i["L2_xattn_Wq"].T, i["L2_xattn_Wkv"].T, i["L2_xattn_Wlkv"].T
    a["L2o"] = i["L2_xattn_Wo"].T[:, None, :]
    a["L2_xattn_bo"] = i["L2_xattn_bo"][None, :]
    gq, gk = i["L2_xattn_qn_g"], i["L2_xattn_kn_g"]
    a["L2gamma"] = np.broadcast_to(np.stack([gq, gq, gk, gk]), (P, 4, 64))
    for key, n in (("L2lg", "ln_l_g"), ("L2lb", "ln_l_b"), ("L2xg", "ln_x_g"), ("L2xb", "ln_x_b")):
        a[key] = i[f"L2_xattn_{n}"][:, None]
    return a


STAGES = ("L0x", "L0f", "L1x", "L1f", "L2x", "L2f", "L3x", "L3f")


def program(nc, arrays, stages=STAGES):
    t = {n: nc.dram_tensor(f"in_{n}", a.shape, mybir.dt.from_np(a.dtype), kind="ExternalInput").ap()
         for n, a in arrays.items()}
    out = nc.dram_tensor("out_x", (P, NBATCH, P), F32, kind="ExternalOutput").ap()
    build(nc, t, out, stages)


def kernel(**inputs):
    import concourse.bacc as _bacc
    from concourse.bass_utils import run_bass_kernel_spmd as _run

    arrays = {n: np.ascontiguousarray(a) for n, a in {**layouts(inputs), **constants()}.items()}
    nc = _bacc.Bacc("TRN2", target_bir_lowering=False, num_devices=1)
    program(nc, arrays)
    r = _run(nc, [{f"in_{n}": a for n, a in arrays.items()}], core_ids=[0])
    return np.ascontiguousarray(r.results[0]["out_x"].transpose(1, 0, 2))
```

```python
from contextlib import ExitStack

import numpy as np

import concourse.bass as bass
from concourse import mybir

F32 = mybir.dt.float32
U8 = mybir.dt.uint8
U32 = mybir.dt.uint32
ALU = mybir.AluOpType
ACT = mybir.ActivationFunctionType
AX_X = mybir.AxisListType.X

P = 128
NBATCH = 32
NTURN = NBATCH // 4
NKEY = 77
CTX = 96
EPS = 1e-5


class Link:

    def __init__(self, eng, sem, turn, length):
        self.eng, self.sem, self.turn, self.length, self.count = eng, sem, turn, length, 0

    def __call__(self, instruction):
        self.count += 1
        instruction.then_inc(self.sem, 1)
        self.eng.wait_ge(self.sem, self.turn * self.length + self.count)

    def end(self):
        assert self.count == self.length, (self.count, self.length)


class Net:

    def __init__(self, nc, ctx):
        self.nc, self.ctx = nc, ctx
        self.semaphores = []

    def sb(self, name, shape, dt=F32):
        return self.ctx.enter_context(self.nc.sbuf_tensor(name, shape, dt))

    def sem(self, name):
        self.semaphores.append(self.nc.alloc_semaphore(name))
        return self.semaphores[-1]

    def release_semaphores(self):
        self.nc.all_engine_barrier()
        self.nc.clear_and_free_semaphores(self.semaphores)
        self.nc.all_engine_barrier()
        self.semaphores = []


def over_turns(eng, body):
    with eng.Fori(0, NTURN // 2 - 1) as i:
        for par in range(2):
            body(i * 2 + par, par, i, None)
    for par in range(2):
        body(NTURN - 2 + par, par, NTURN // 2 - 1, par)


def attention_stage(nc, net, spec, w):
    name, heads, hd, kind, biased = (spec[k] for k in ("name", "heads", "hd", "kind", "biased"))
    scale = float(hd) ** -0.5
    inner = heads * hd
    NC = inner // P
    NK = {"cross": NKEY, "self": P}[kind]
    U = 4
    NU = heads // U
    NP = (NC + 3) // 4

    with ExitStack() as ctx:
        def sb(n, shape, dt=F32):
            return ctx.enter_context(nc.sbuf_tensor(f"{name}_{n}", shape, dt))

        def sem(n):
            return net.sem(f"{name}_{n}")

        x = net.x
        dst = net.x1 if kind == "self" else net.x
        ident, ones_row = net.ident, net.ones_row
        score_bank, turn_bank, prep_bank = net.banks[0:2], net.banks[2:4], net.banks[4:6]
        out_bank = net.banks[6:6 + NP]
        proj_bank = net.banks[6 if NP == 2 else 7]

        KD = P if kind == "self" else CTX
        wq = sb("wq", [P, inner]); wk = sb("wk", [KD, inner]); wv = sb("wv", [KD, inner])
        wo = sb("wo", [P, NC, P]); bo = sb("bo", [1, P])
        loads = [(wk[:, :], w["wk"]), (wq[:, :], w["wq"]), (wv[:, :], w["wv"]), (wo[:, :, :], w["wo"]),
                 (bo[:, :], w["bo"])]
        if biased:
            bq = sb("bq", [P, 1]); bk = sb("bk", [P, 1]); bv = sb("bv", [1, P])
            loads += [(bq[:, :], w["bq"]), (bk[:, :], w["bk"]), (bv[:, :], w["bv"])]
        if hd == 8:
            diag = sb("diag", [P, 4]); loads.append((diag[:, :], w["diag"]))

        stats = sb("stats", [P, 4, 6]); mean_var = sb("mean_var", [P, 4, 2]); rstd = sb("rstd", [P, 4])
        idle = sb("idle", [P, 1])
        xn = [sb(f"xn{i}", [P, 4, P]) for i in range(2)]; xT = sb("xT", [P, 4 * P])
        qT = [sb(f"qT{i}", [P, NC, 4 * P]) for i in range(2)]
        if kind == "cross":
            ctxg = [sb(f"ctxg{i}", [CTX, 4, NKEY]) for i in range(2)]
        if hd == 8:
            kbd = [sb(f"kbd{i}", [P, 4, heads, NK]) for i in range(2)]
            vals = [sb(f"vals{i}", [NK, 4, heads, 32]) for i in range(2)]
        else:
            kbd = [sb(f"kbd{i}", [P, NC, 4, 2, NK]) for i in range(2)]
            vals = [sb(f"vals{i}", [NK, 4, inner]) for i in range(2)]
        soft = [sb(f"soft{i}", [P, heads, NK]) for i in range(4)]
        mx = [sb(f"mx{i}", [P, U]) for i in range(2)]
        rsum = [sb(f"rsum{i}", [P, heads]) for i in range(2)]
        rinv = [sb(f"rinv{i}", [P, heads]) for i in range(2)]
        probsT = [sb(f"probsT{i}", [NK, 4, P]) for i in range(2)]
        attnT = sb("attnT", [P, NC, P])

        loaded, constants, cleared, chain = (sem(n) for n in ("loaded", "constants", "cleared", "chain"))
        var_ready, rstd_ready, normed = sem("var_ready"), sem("rstd_ready"), sem("normed")
        ctx_loaded = [sem(f"ctx_loaded{i}") for i in range(2)]
        job_ready, job_out = sem("job_ready"), [sem(f"job_out{i}") for i in range(2)]
        scores_ready, max_ready, shifted = sem("scores_ready"), sem("max_ready"), sem("shifted")
        exp_done, sum_ready, inv_ready, probs_ready = sem("exp_done"), sem("sum_ready"), sem("inv_ready"), sem("probs_ready")
        turned, turned_out, values_done = sem("turned"), sem("turned_out"), sem("values_done")
        attnT_ready, proj_done, added = sem("attnT_ready"), sem("proj_done"), sem("added")

        if inner == P:
            vjobs = [([0, 1, 2, 3], 0, P)]
        else:
            vjobs = [([b], c, 512) for b in range(4) for c in range(0, inner, 512)]
        first = [("x", 0)] + [(k, c) for c in range(NC) for k in ("k", "q")]
        jobs = [(j, *job) for j, job in enumerate(first + [("v", v) for v in range(len(vjobs))])]
        J, JF = len(jobs), len(first)

        def taken(turn, count):
            return [turn * ((J + 1 - i) // 2) + (count + 1 - i) // 2 for i in range(2)]

        def between(b, final):
            if final == 1:
                return [[] for _ in range(2 * NU)]
            some, at = (jobs[:JF], b) if b < 2 else (jobs[JF:], b - 2)
            if hd == 8:
                return [some[i // 2:i // 2 + 1] if i % 2 == 0 else [] for i in range(2 * NU * at, 2 * NU * (at + 1))]
            cut = [len(some) * i // (4 * NU) for i in range(4 * NU + 1)]
            return [some[cut[i]:cut[i + 1]] for i in range(2 * NU * at, 2 * NU * (at + 1))]

        KEYS_FROM = [len(c) and c[-1][1] == "k" for b in range(2) for c in between(b, None)].index(True) if hd == 8 else 0

        def steps(final):
            return [(b, final != 1 or b < 2, final != 1 or b < 3) for b in range(4)]

        def shift(dve, g, unit, tile, later):
            n = g * NU + unit
            ps = score_bank[unit % 2][:, 0:U * NK].rearrange("p (h k) -> p h k", h=U)
            dve.wait_ge(scores_ready, n + 1)
            if unit >= 2 or later:
                dve.wait_ge(shifted, n - 1)
            dve.tensor_reduce(mx[unit % 2][:, :], ps, AX_X, ALU.max).then_inc(max_ready, 1)
            dve.wait_ge(max_ready, n + 1)
            dve.tensor_tensor(tile[:, unit * U:(unit + 1) * U, :], ps,
                              mx[unit % 2][:, :].unsqueeze(2).to_broadcast([P, U, NK]),
                              ALU.subtract).then_inc(shifted, 1)

        def row_sums(dve, g, tile, two, reused):
            dve.wait_ge(exp_done, g + 1)
            if reused:
                dve.wait_ge(probs_ready, g - 1)
            dve.tensor_reduce(rsum[two][:, :], tile[:, :, :], AX_X, ALU.add).then_inc(sum_ready, 1)
            dve.wait_ge(sum_ready, g + 1)
            dve.reciprocal(rinv[two][:, :], rsum[two][:, :]).then_inc(inv_ready, 1)

        def variances(dve, turn):
            link = Link(dve, chain, turn, 2)
            for b in range(4):
                last = dve.bn_stats(stats[:, b, :], x[:, turn * 4 + b, :])
            link(last)
            dve.memset(idle[:, :], 0.0)
            for b in range(4):
                last = dve.bn_aggr(mean_var[:, b, :], stats[:, b, :])
            link(last)
            dve.tensor_scalar(rstd[:, :], mean_var[:, :, 1], EPS, None, ALU.add).then_inc(var_ready, 1)

        def normalize(dve, turn, par):
            dve.wait_ge(rstd_ready, turn + 1)
            for b in range(4):
                last = dve.tensor_scalar(xn[par][:, b, :], x[:, turn * 4 + b, :], mean_var[:, b, 0:1],
                                         rstd[:, b:b + 1], ALU.subtract, ALU.mult)
            last.then_inc(normed, 1)

        def take_keys(dve, turn, par, job, pieces=range(4)):
            j, what, c = job
            if what != "k":
                return
            kps = prep_bank[j % 2][:, 0:4 * NK].rearrange("p (b k) -> p b k", b=4)
            dve.wait_ge(job_ready, turn * J + j + 1)
            if hd == 8:
                for r in pieces:
                    rows = slice(32 * r, 32 * r + 32)
                    for b in range(4):
                        last = dve.scalar_tensor_tensor(
                            kbd[par][rows, b, 4 * r:4 * r + 4, :], kps[rows, b:b + 1, :].to_broadcast([32, 4, NK]),
                            bk[rows, 0:1], diag[rows, :].unsqueeze(2).to_broadcast([32, 4, NK]), ALU.add, ALU.mult)
                if 3 not in pieces:
                    return
            else:
                dve.tensor_copy(kbd[par][0:64, c, :, 0, :], kps[0:64, :, :])
                last = dve.tensor_copy(kbd[par][64:P, c, :, 1, :], kps[64:P, :, :])
            last.then_inc(job_out[j % 2], 1)

        def take_others(act, turn, par, job):
            j, what, c = job
            bank = prep_bank[j % 2]
            if what == "k":
                return
            act.wait_ge(job_ready, turn * J + j + 1)
            if what == "x":
                last = act.copy(xT[:, :], bank[:, :])
            elif what == "q" and biased:
                last = act.activation(qT[par][:, c, :], bank[:, :], ACT.Identity, bias=bq[:, 0:1])
            elif what == "q":
                last = act.copy(qT[par][:, c, :], bank[:, :])
            elif hd == 8:
                ps = bank[0:NK, :].rearrange("p (b r j d) -> p b r j d", b=4, r=4, j=4)
                out = vals[par][:, :, :, :].rearrange("p b (r j) d -> p b r j d", j=4)
                for i in range(4):
                    last = act.copy(out[:, :, :, i, 8 * i:8 * i + 8], ps[:, :, :, i, :])
            else:
                bs, c0, cols = vjobs[c]
                last = act.copy(vals[par][:, bs[0], c0:c0 + cols], bank[0:NK, :])
            last.then_inc(job_out[j % 2], 1)

        def do_job(pe, turn, par, half, job):
            j, what, c = job
            pe.wait_ge(job_out[j % 2], taken(turn, j)[j % 2])
            bank = prep_bank[j % 2]
            src = [xT[:, b * P:(b + 1) * P] if kind == "self" else ctxg[par][:, b, :] for b in range(4)]
            if what == "x":
                pe.wait_ge(normed, turn + 1)
                for b in range(4):
                    last = pe.transpose(bank[:, b * P:(b + 1) * P], xn[par][:, b, :], ident[:, :])
            elif what == "k":
                if kind == "self" and c == 0:
                    pe.wait_ge(job_out[0], taken(turn, 1)[0])
                if kind == "cross" and c == 0:
                    pe.wait_ge(ctx_loaded[par], (half + 1) * 16)
                last = pe.matmul(bank[:, 0:4 * NK], wk[:, c * P:(c + 1) * P],
                                 xT[:, :] if kind == "self" else ctxg[par][:, :, :], start=True, stop=True)
            elif what == "q":
                if c == 0:
                    pe.wait_ge(job_out[0], taken(turn, 1)[0])
                last = pe.matmul(bank[:, :], wq[:, c * P:(c + 1) * P], xT[:, :], start=True, stop=True)
            else:
                bs, c0, cols = vjobs[c]
                for i, b in enumerate(bs):
                    out = bank[0:NK, i * cols:(i + 1) * cols]
                    last = pe.matmul(out, src[b], wv[:, c0:c0 + cols], start=True, stop=not biased)
                    if biased:
                        last = pe.matmul(out, ones_row[:, 0:NK], bv[:, :], start=False, stop=True)
            last.then_inc(job_ready, 1)

        def scores(pe, g, b, par, u, later):
            bank = score_bank[u % 2]
            if u >= 2 or later:
                pe.wait_ge(shifted, g * NU + u - 1)
            if hd == 8:
                last = pe.matmul(bank[:, 0:U * NK], qT[par][:, 0, b * P:(b + 1) * P],
                                 kbd[par][:, b, u * U:(u + 1) * U, :], start=True, stop=True)
            else:
                for c in range(u * 2, u * 2 + 2):
                    at = (c - u * 2) * 2 * NK
                    last = pe.matmul(bank[:, at:at + 2 * NK], qT[par][:, c, b * P:(b + 1) * P],
                                     kbd[par][:, c, b, :, :], start=True, stop=True)
            last.then_inc(scores_ready, 1)

        def turn_unit(pe, g, b, u):
            if u == 0:
                pe.wait_ge(probs_ready, g + 1)
            for i in range(U):
                last = pe.transpose(turn_bank[u % 2][0:NK, i * P:(i + 1) * P], soft[b][:, u * U + i, :], ident[:, :])
            last.then_inc(turned, 1)

        def values(pe, g, b, par, u):
            pe.wait_ge(turned_out, g * NU + u + 1)
            if NP == 2 and u == 0:
                pe.wait_ge(added, g)
            for i in range(U):
                h = u * U + i
                if hd == 8:
                    last = pe.matmul(out_bank[0][32 * u:32 * u + 32, 0:P], vals[par][:, b, h, :],
                                     probsT[u % 2][:, i, :], start=(i == 0), stop=(i == U - 1))
                else:
                    c = h // 2
                    out = out_bank[c // 4][64 * (h % 2):64 * (h % 2) + 64, c % 4 * P:(c % 4 + 1) * P]
                    last = pe.matmul(out, vals[par][:, b, h * 64:(h + 1) * 64], probsT[u % 2][:, i, :],
                                     start=True, stop=True)
            last.then_inc(values_done, 1)

        def project(pe, g):
            pe.wait_ge(attnT_ready, (g + 1) * NP)
            pe.wait_ge(added, g)
            pe.matmul(proj_bank[:, 0:P], ones_row[:, :], bo[:, :], start=True, stop=False)
            for c in range(NC):
                last = pe.matmul(proj_bank[:, 0:P], attnT[:, c, :], wo[:, c, :], start=False, stop=(c == NC - 1))
            last.then_inc(proj_done, 1)

        def take_attention(act, g, b, p):
            nch = min(4, NC - 4 * p)
            act.wait_ge(values_done, g * NU + (p + 1) * (NU // NP))
            act.copy(attnT[:, 4 * p:4 * p + nch, :],
                     out_bank[p][:, 0:nch * P].rearrange("p (c t) -> p c t", c=nch)
                     ).then_inc(attnT_ready, 1)

        def exponents(act, g, tile):
            flat = tile[:, :, :].rearrange("p h k -> p (h k)")
            act.wait_ge(shifted, (g + 1) * NU)
            act.activation(flat, flat, ACT.Exp, scale=scale).then_inc(exp_done, 1)

        def weigh(pool, g, tile, two):
            pool.wait_ge(inv_ready, g + 1)
            pool.tensor_tensor(tile[:, :, :], tile[:, :, :], rinv[two][:, :].unsqueeze(2).to_broadcast([P, heads, NK]),
                               ALU.mult).then_inc(probs_ready, 1)

        block = ctx.enter_context(nc.Block())

        @block.sync
        def _(sp):
            def load_context(turn, par):
                sp.dma_start(ctxg[par][:, :, :], w["ctxT"][:, bass.ds(turn * 4, 4), :]).then_inc(ctx_loaded[par], 16)

            if kind == "cross":
                load_context(0, 0)
            for dst_ap, src in loads:
                sp.dma_start(dst_ap, src).then_inc(loaded, 16)
            if kind == "cross":
                load_context(1, 1)
                with sp.Fori(1, NTURN // 2) as i:
                    for par in range(2):
                        sp.wait_ge(job_ready, (i * 2 + par - 1) * J)
                        load_context(i * 2 + par, par)

        @block.gpsimd
        def _(pool):
            def invert_root(turn):
                pool.wait_ge(var_ready, turn + 1)
                pool.tensor_tensor(rstd[:, :], rstd[:, :], net.minus_half[:, 0:4], ALU.pow).then_inc(rstd_ready, 1)

            for t in range(2):
                invert_root(t)
            pool.wait_ge(rstd_ready, 2)
            if hd == 8:
                pool.memset(vals[0][:, :, :, :], 0.0)
                pool.memset(vals[1][:, :, :, :], 0.0)
                pool.memset(kbd[1][:, :, :, :], 0.0).then_inc(constants, 1)
            else:
                for tile in kbd:
                    pool.memset(tile[0:64, :, :, 1, :], 0.0)
                    last = pool.memset(tile[64:P, :, :, 0, :], 0.0)
                last.then_inc(constants, 1)
            pool.wait_ge(constants, 1)
            weigh(pool, 0, soft[0], 0)

            def body(turn, par, pair, final):
                for b, _, one_more in steps(final):
                    if one_more:
                        weigh(pool, turn * 4 + b + 1, soft[(b + 1) % 4], (b + 1) % 2)
                    if b == 1 and final is None:
                        invert_root(turn + 2)

            over_turns(pool, body)

        @block.vector
        def _(dve):
            variances(dve, 0)
            normalize(dve, 0, 0)
            dve.wait_ge(normed, 1)
            variances(dve, 1)
            normalize(dve, 1, 1)
            if hd == 8:
                dve.memset(kbd[0][:, :, :, :], 0.0).then_inc(cleared, 1)
                dve.wait_ge(cleared, 1)
            dve.wait_ge(loaded, 16 * len(loads))
            dve.wait_ge(constants, 1)
            for job in jobs:
                take_keys(dve, 0, 0, job)
            for g in range(2):
                for u in range(NU):
                    shift(dve, g, u, soft[g], g > 0)
            row_sums(dve, 0, soft[0], 0, False)

            def body(turn, par, pair, final):
                for b, two_more, one_more in steps(final):
                    g = turn * 4 + b
                    slots = between(b, final)

                    def keys_in(slot):
                        if hd != 8:
                            for job in slots[slot]:
                                take_keys(dve, turn + 1, 1 - par, job)
                        elif final != 1 and b < 2:
                            since = b * 2 * NU + slot - KEYS_FROM
                            if since in (0, 1, 3, 5):
                                take_keys(dve, turn + 1, 1 - par, jobs[1], [(since + 1) // 2])

                    for u in range(NU):
                        if two_more and u:
                            shift(dve, g + 2, u - 1, soft[(b + 2) % 4], True)
                        keys_in(2 * u)
                        if u == 0 and one_more:
                            row_sums(dve, g + 1, soft[(b + 1) % 4], (b + 1) % 2, True)
                        if u < NU - 1:
                            keys_in(2 * u + 1)
                    if two_more:
                        shift(dve, g + 2, NU - 1, soft[(b + 2) % 4], True)
                    keys_in(2 * NU - 1)
                    dve.wait_ge(proj_done, g + 1)
                    inp = xn[par][:, b, :] if kind == "self" else x[:, g, :]
                    dve.tensor_tensor(dst[:, g, :], inp, proj_bank[:, 0:P], ALU.add).then_inc(added, 1)
                    if b == 1 and final is None:
                        dve.wait_ge(normed, turn + 2)
                        variances(dve, turn + 2)
                if final is None:
                    dve.wait_ge(added, (turn + 1) * 4)
                    normalize(dve, turn + 2, par)

            over_turns(dve, body)

        @block.scalar
        def _(act):
            act.wait_ge(loaded, 16 * len(loads))
            act.wait_ge(constants, 1)
            for job in jobs:
                take_others(act, 0, 0, job)
            for g in range(2):
                exponents(act, g, soft[g])

            def body(turn, par, pair, final):
                for b, two_more, _ in steps(final):
                    g = turn * 4 + b
                    slots = between(b, final)
                    for u in range(NU):
                        n = g * NU + u
                        act.wait_ge(turned, n + 1)
                        if u >= 2:
                            act.wait_ge(values_done, n - 1)
                        act.copy(probsT[u % 2][:, :, :], turn_bank[u % 2][0:NK, :].rearrange("p (m t) -> p m t", m=4)
                                 ).then_inc(turned_out, 1)
                        for job in slots[2 * u]:
                            take_others(act, turn + 1, 1 - par, job)
                        if NP == 2 and u == NU // 2:
                            take_attention(act, g, b, 0)
                        if u < NU - 1:
                            for job in slots[2 * u + 1]:
                                take_others(act, turn + 1, 1 - par, job)
                    take_attention(act, g, b, NP - 1)
                    for job in slots[-1]:
                        take_others(act, turn + 1, 1 - par, job)
                    if two_more:
                        exponents(act, g + 2, soft[(b + 2) % 4])

            over_turns(act, body)

        @block.tensor
        def _(pe):
            pe.wait_ge(loaded, 16 * len(loads))
            for job in jobs:
                do_job(pe, 0, 0, 0, job)
            for i in range(2):
                pe.wait_ge(job_out[i], taken(0, J)[i])
            for g in range(2):
                for u in range(NU):
                    scores(pe, g, g, 0, u, g > 0)

            def body(turn, par, pair, final):
                for b, two_more, _ in steps(final):
                    g = turn * 4 + b
                    slots = between(b, final)

                    def fill(slot):
                        for job in slots[slot]:
                            do_job(pe, turn + 1, 1 - par, pair + par, job)

                    if b == 2 and final != 1:
                        for i in range(2):
                            pe.wait_ge(job_out[i], taken(turn + 1, JF)[i])
                    if b == 0:
                        for i in range(2):
                            pe.wait_ge(job_out[i], taken(turn, J)[i])

                    def scores_ahead(u):
                        if two_more:
                            scores(pe, g + 2, (b + 2) % 4, par if b < 2 else 1 - par, u, True)

                    for u in range(NU):
                        turn_unit(pe, g, b, u)
                        if u:
                            scores_ahead(u - 1)
                        fill(2 * u)
                        if u:
                            values(pe, g, b, par, u - 1)
                        if u < NU - 1:
                            fill(2 * u + 1)
                    values(pe, g, b, par, NU - 1)
                    scores_ahead(NU - 1)
                    fill(2 * NU - 1)
                    project(pe, g)

            over_turns(pe, body)


def latent_stage(nc, net, spec, w):
    name, heads, hd = spec["name"], 2, 64
    scale = float(hd) ** -0.5
    NK = NKEY + P
    PARTS = [(0, NKEY), (NKEY, P)]
    PLACES = [(i, e) for i in range(heads) for e in range(2)]

    with ExitStack() as ctx:
        def sb(n, shape, dt=F32):
            return ctx.enter_context(nc.sbuf_tensor(f"{name}_{n}", shape, dt))

        def sem(n):
            return net.sem(f"{name}_{n}")

        x, ident, ones_row = net.x, net.ident, net.ones_row
        score_bank, turn_bank, out_bank, proj_bank = net.banks[0:2], net.banks[2], net.banks[3], net.banks[4]
        prep_bank = net.banks[5:8]

        wo = sb("wo", [P, P]); bo = sb("bo", [1, P])
        wqkv_lat = sb("wqkv_lat", [P, 3 * P]); wkv_ctx = sb("wkv_ctx", [CTX, 2 * P])
        gamma = sb("gamma", [P, 4, 64]); lat_g = sb("lat_g", [P, 1]); lat_b = sb("lat_b", [P, 1])
        ctx_g = sb("ctx_g", [CTX, 1]); ctx_b = sb("ctx_b", [CTX, 1])
        ctx_tok = sb("ctx_tok", [NKEY, NBATCH, CTX])
        mask8 = sb("mask8", [1, NBATCH * NKEY], U8); mask_row = sb("mask_row", [1, NBATCH, 2, NKEY])
        loads = [(wqkv_lat[:, 0:P], w["wq"]), (wqkv_lat[:, P:3 * P], w["wlkv"]),
                 (wkv_ctx[:, :], w["wkv"]), (gamma[:, :, :], w["gamma"]), (lat_g[:, :], w["lat_g"]),
                 (lat_b[:, :], w["lat_b"]), (ctx_g[:, :], w["ctx_g"]), (ctx_b[:, :], w["ctx_b"]),
                 (mask8[:, :], w["mask"]), (wo[:, :], w["wo"]), (bo[:, :], w["bo"])]

        stats = sb("stats", [P, 4, 6]); mean_var = sb("mean_var", [P, 4, 2]); rstd = sb("rstd", [P, 4])
        stats2 = sb("stats2", [P, 4, 6]); mean_var2 = sb("mean_var2", [P, 4, 2]); rstd2 = sb("rstd2", [P, 4])
        stats_ctx = sb("stats_ctx", [NKEY, 4, 6]); mv_ctx = sb("mv_ctx", [NKEY, 4, 2]); rstd_ctx = sb("rstd_ctx", [NKEY, 4])
        idle = sb("idle", [P, 1])
        xn = sb("xn", [P, 4, P]); xn2 = [sb(f"xn2{i}", [P, 4, P]) for i in range(2)]
        cn = [sb(f"cn{i}", [NKEY, 4, CTX]) for i in range(2)]
        xT = sb("xT", [P, 4 * P]); cT = sb("cT", [CTX, 4, NKEY])
        raw_lat = [sb(f"raw_lat{i}", [P, 4, 3 * P]) for i in range(2)]
        raw_ctx = [sb(f"raw_ctx{i}", [NKEY, 4, 2 * P]) for i in range(2)]
        sq_lat = sb("sq_lat", [P, 4, 2 * P]); sq_ctx = sb("sq_ctx", [NKEY, 4, P])
        rms_lat = sb("rms_lat", [P, 16]); rms_ctx = sb("rms_ctx", [NKEY, 8])
        qk_tok = sb("qk_tok", [P, 4, 4, 64]); kc_tok = sb("kc_tok", [NKEY, 4, 2, 64])
        qT = [sb(f"qT{i}", [P, 4 * P]) for i in range(2)]
        kbd = [sb(f"kbd{i}", [P, 4, 2, NK]) for i in range(2)]
        soft = [sb(f"soft{i}", [P, heads, NK]) for i in range(4)]
        mx, rsum, rinv = ([sb(f"{n}{i}", [P, heads]) for i in range(2)] for n in ("mx", "rsum", "rinv"))
        probsT = [sb(f"probsT{i}", [P, 4, P]) for i in range(2)]
        attnT = sb("attnT", [P, P])

        loaded, ctx_loaded, constants, mask_ready, chain, moments_ready = (
            sem(n) for n in ("loaded", "ctx_loaded", "constants", "mask_ready", "chain", "moments_ready"))
        var_ready, rstd_ready, var2_ready, rstd2_ready, normed = (
            sem(n) for n in ("var_ready", "rstd_ready", "var2_ready", "rstd2_ready", "normed"))
        job_ready, job_out = sem("job_ready"), [sem(f"job_out{i}") for i in range(3)]
        squared, squares_summed, rms_ready, rms_chain, qk_ready = (
            sem(n) for n in ("squared", "squares_summed", "rms_ready", "rms_chain", "qk_ready"))
        scores_ready, max_ready, shifted, exp_done = (
            sem(n) for n in ("scores_ready", "max_ready", "shifted", "exp_done"))
        sum_ready, inv_ready, probs_ready, turned, turned_out = (
            sem(n) for n in ("sum_ready", "inv_ready", "probs_ready", "turned", "turned_out"))
        values_done, attnT_ready, proj_done, added = (
            sem(n) for n in ("values_done", "attnT_ready", "proj_done", "added"))

        JOBS = ["x", "c", "lat0", "lat1", "lat2", "lat3", "con0", "con1", "qT", "kT", "kcT"]
        J, RAW = len(JOBS), 8

        def taken(turn, count):
            return [turn * ((J + 2 - i) // 3) + (count + 2 - i) // 3 for i in range(3)]

        def steps(final):
            return [(b, final != 1 or b < 2, final != 1 or b < 3)
                    for b in range(4)]


        def variances(dve, turn):
            link = Link(dve, chain, turn, 4)
            for b in range(4):
                dve.bn_stats(stats[:, b, :], x[:, turn * 4 + b, :])
                last = dve.bn_stats(stats_ctx[:, b, :], ctx_tok[:, turn * 4 + b, :])
            link(last)
            dve.memset(idle[:, :], 0.0)
            for b in range(4):
                dve.bn_aggr(mean_var[:, b, :], stats[:, b, :])
                last = dve.bn_aggr(mv_ctx[:, b, :], stats_ctx[:, b, :])
            link(last)
            dve.tensor_scalar(rstd[:, :], mean_var[:, :, 1], EPS, None, ALU.add)
            dve.tensor_scalar(rstd_ctx[:, :], mv_ctx[:, :, 1], EPS, None, ALU.add).then_inc(var_ready, 1)
            return link

        def normalize_once(dve, turn, par, link):
            dve.wait_ge(rstd_ready, turn + 1)
            for b in range(4):
                dve.tensor_scalar(cn[par][:, b, :], ctx_tok[:, turn * 4 + b, :], mv_ctx[:, b, 0:1],
                                  rstd_ctx[:, b:b + 1], ALU.subtract, ALU.mult)
            for b in range(4):
                last = dve.tensor_scalar(xn[:, b, :], x[:, turn * 4 + b, :], mean_var[:, b, 0:1],
                                         rstd[:, b:b + 1], ALU.subtract, ALU.mult)
            link(last)
            for b in range(4):
                last = dve.bn_stats(stats2[:, b, :], xn[:, b, :])
            link(last)
            link.end()
            dve.memset(idle[:, :], 0.0)
            for b in range(4):
                last = dve.bn_aggr(mean_var2[:, b, :], stats2[:, b, :])
            last.then_inc(moments_ready, 1)
            dve.wait_ge(moments_ready, turn + 1)
            dve.tensor_scalar(rstd2[:, :], mean_var2[:, :, 1], EPS, None, ALU.add).then_inc(var2_ready, 1)

        def normalize_again(dve, turn, par):
            dve.wait_ge(rstd2_ready, turn + 1)
            for b in range(4):
                last = dve.tensor_scalar(xn2[par][:, b, :], xn[:, b, :], mean_var2[:, b, 0:1],
                                         rstd2[:, b:b + 1], ALU.subtract, ALU.mult)
            last.then_inc(normed, 1)
            dve.wait_ge(normed, turn + 1)

        def sum_squares(dve, turn):
            dve.wait_ge(squared, turn + 1)
            dve.tensor_reduce(rms_lat[:, :], sq_lat[:, :, :].rearrange("p b (g d) -> p (b g) d", d=64), AX_X, ALU.add)
            dve.tensor_reduce(rms_ctx[:, :], sq_ctx[:, :, :].rearrange("p b (g d) -> p (b g) d", d=64),
                              AX_X, ALU.add).then_inc(squares_summed, 1)

        def scale_rows(dve, turn, par):
            link = Link(dve, rms_chain, turn, 3)
            dve.wait_ge(rms_ready, turn + 1)
            dve.tensor_scalar(rms_lat[:, :], rms_lat[:, :], 0.125, 1e-8, ALU.mult, ALU.max)
            link(dve.tensor_scalar(rms_ctx[:, :], rms_ctx[:, :], 0.125, 1e-8, ALU.mult, ALU.max))
            dve.reciprocal(rms_lat[:, :], rms_lat[:, :])
            link(dve.reciprocal(rms_ctx[:, :], rms_ctx[:, :]))
            dve.tensor_tensor(qk_tok[:, :, :, :], raw_lat[par][:, :, 0:2 * P].rearrange("p b (g d) -> p b g d", d=64),
                              rms_lat[:, :].rearrange("p (b g) -> p b g", b=4).unsqueeze(3).to_broadcast([P, 4, 4, 64]),
                              ALU.mult)
            link(dve.tensor_tensor(kc_tok[:, :, :, :], raw_ctx[par][:, :, 0:P].rearrange("p b (g d) -> p b g d", d=64),
                                   rms_ctx[:, :].rearrange("p (b g) -> p b g", b=4).unsqueeze(3).to_broadcast([NKEY, 4, 2, 64]),
                                   ALU.mult))
            link.end()
            dve.tensor_tensor(qk_tok[:, :, :, :], qk_tok[:, :, :, :],
                              gamma[:, :, :].unsqueeze(1).to_broadcast([P, 4, 4, 64]), ALU.mult)
            dve.tensor_tensor(kc_tok[:, :, :, :], kc_tok[:, :, :, :],
                              gamma[0:NKEY, 2:4, :].unsqueeze(1).to_broadcast([NKEY, 4, 2, 64]),
                              ALU.mult).then_inc(qk_ready, 1)

        def take_keys(dve, turn, par):
            for j in range(J - 2, J):
                dve.wait_ge(job_ready, turn * J + j + 1)
                at, n = PARTS[JOBS[j] == "kT"]
                ps = prep_bank[j % 3][:, 0:4 * n].rearrange("p (b t) -> p b t", b=4)
                for i in range(2):
                    last = dve.tensor_copy(kbd[par][64 * i:64 * i + 64, :, i, at:at + n], ps[64 * i:64 * i + 64, :, :])
                last.then_inc(job_out[j % 3], 1)

        def shift(dve, g, b, later):
            ps = score_bank[b % 2][:, 0:heads * NK].rearrange("p (h k) -> p h k", h=heads)
            dve.wait_ge(scores_ready, g + 1)
            if later:
                dve.wait_ge(shifted, g - 1)
            dve.tensor_reduce(mx[b % 2][:, :], ps, AX_X, ALU.max).then_inc(max_ready, 1)
            dve.wait_ge(max_ready, g + 1)
            dve.tensor_tensor(soft[b][:, :, :], ps, mx[b % 2][:, :].unsqueeze(2).to_broadcast([P, heads, NK]),
                              ALU.subtract).then_inc(shifted, 1)

        def row_sums(dve, g, b, later):
            dve.wait_ge(exp_done, g + 1)
            if later:
                dve.wait_ge(probs_ready, g - 1)
            dve.tensor_reduce(rsum[b % 2][:, :], soft[b][:, :, :], AX_X, ALU.add).then_inc(sum_ready, 1)
            dve.wait_ge(sum_ready, g + 1)
            dve.reciprocal(rinv[b % 2][:, :], rsum[b % 2][:, :]).then_inc(inv_ready, 1)


        def take_others(act, turn, par, js):
            for j in js:
                what, ps = JOBS[j], prep_bank[j % 3]
                act.wait_ge(job_ready, turn * J + j + 1)
                if what == "x":
                    last = act.activation(xT[:, :], ps[:, :], ACT.Identity, scale=lat_g[:, 0:1], bias=lat_b[:, 0:1])
                elif what == "c":
                    last = act.activation(cT[:, :, :], ps[0:CTX, 0:4 * NKEY].rearrange("p (b t) -> p b t", b=4),
                                          ACT.Identity, scale=ctx_g[:, 0:1], bias=ctx_b[:, 0:1])
                elif what == "qT":
                    last = act.copy(qT[par][:, :], ps[:, :])
                elif what[:3] == "lat":
                    last = act.copy(raw_lat[par][:, j - 2, :], ps[:, 0:3 * P])
                else:
                    i = j - 6
                    last = act.copy(raw_ctx[par][:, 2 * i:2 * i + 2, :], ps[0:NKEY, :].rearrange("p (b f) -> p b f", b=2))
                last.then_inc(job_out[j % 3], 1)

        def square(act, turn, par):
            for i in range(3):
                act.wait_ge(job_out[i], taken(turn, RAW)[i])
            act.wait_ge(squares_summed, turn)
            act.activation(sq_lat[:, :, :], raw_lat[par][:, :, 0:2 * P], ACT.Square)
            act.activation(sq_ctx[:, :, :], raw_ctx[par][:, :, 0:P], ACT.Square).then_inc(squared, 1)

        def take_turned(act, g, b):
            act.wait_ge(turned, g + 1)
            ps = turn_bank[:, :].rearrange("p (m t) -> p m t", m=4)
            for e, (_, n) in enumerate(PARTS):
                last = act.copy(probsT[b % 2][0:n, e:4:2, :], ps[0:n, e:4:2, :])
            last.then_inc(turned_out, 1)

        def exponents(act, g, b):
            flat = soft[b][:, :, :].rearrange("p h k -> p (h k)")
            act.wait_ge(shifted, g + 1)
            act.activation(flat, flat, ACT.Exp, scale=scale).then_inc(exp_done, 1)


        def invert_roots(pool, turn):
            pool.wait_ge(var_ready, turn + 1)
            pool.tensor_tensor(rstd[:, :], rstd[:, :], net.minus_half[:, 0:4], ALU.pow)
            pool.tensor_tensor(rstd_ctx[:, :], rstd_ctx[:, :], net.minus_half[0:NKEY, 0:4], ALU.pow).then_inc(rstd_ready, 1)

        def invert_roots_again(pool, turn):
            pool.wait_ge(var2_ready, turn + 1)
            pool.tensor_tensor(rstd2[:, :], rstd2[:, :], net.minus_half[:, 0:4], ALU.pow).then_inc(rstd2_ready, 1)

        def root_squares(pool, turn):
            pool.wait_ge(squares_summed, turn + 1)
            pool.tensor_tensor(rms_lat[:, :], rms_lat[:, :], net.plus_half[:, 0:16], ALU.pow)
            pool.tensor_tensor(rms_ctx[:, :], rms_ctx[:, :], net.plus_half[0:NKEY, 0:8], ALU.pow).then_inc(rms_ready, 1)

        def weigh(pool, g, b):
            pool.wait_ge(inv_ready, g + 1)
            pool.tensor_tensor(soft[b][:, :, :], soft[b][:, :, :],
                               rinv[b % 2][:, :].unsqueeze(2).to_broadcast([P, heads, NK]), ALU.mult).then_inc(probs_ready, 1)


        def do_jobs(pe, turn, par, js):
            for j in js:
                what, ps = JOBS[j], prep_bank[j % 3]
                pe.wait_ge(job_out[j % 3], taken(turn, j)[j % 3])
                if what == "x":
                    pe.wait_ge(normed, turn + 1)
                    for b in range(4):
                        last = pe.transpose(ps[:, b * P:(b + 1) * P], xn2[par][:, b, :], ident[:, :])
                elif what == "c":
                    for b in range(4):
                        last = pe.transpose(ps[0:CTX, b * NKEY:(b + 1) * NKEY], cn[par][:, b, :], ident[0:NKEY, 0:NKEY])
                elif what[:3] == "lat":
                    b = j - 2
                    pe.wait_ge(job_out[0], taken(turn, 1)[0])
                    last = pe.matmul(ps[:, 0:3 * P], xT[:, b * P:(b + 1) * P], wqkv_lat[:, :], start=True, stop=True)
                elif what[:3] == "con":
                    pe.wait_ge(job_out[1], taken(turn, 2)[1])
                    for i in range(2):
                        last = pe.matmul(ps[0:NKEY, i * 2 * P:(i + 1) * 2 * P], cT[:, 2 * (j - 6) + i, :], wkv_ctx[:, :],
                                         start=True, stop=True)
                else:
                    pe.wait_ge(qk_ready, turn + 1)
                    for b in range(4):
                        if what == "kcT":
                            last = pe.transpose(ps[:, b * NKEY:(b + 1) * NKEY],
                                                kc_tok[:, b, :, :].rearrange("p g d -> p (g d)"), ident[0:NKEY, 0:NKEY])
                        else:
                            g0 = 0 if what == "qT" else 2
                            last = pe.transpose(ps[:, b * P:(b + 1) * P],
                                                qk_tok[:, b, g0:g0 + 2, :].rearrange("p g d -> p (g d)"), ident[:, :])
                last.then_inc(job_ready, 1)

        def scores(pe, g, b, par, later):
            if later:
                pe.wait_ge(shifted, g - 1)
            ps = score_bank[b % 2][:, 0:2 * NK]
            pe.matmul(ps, qT[par][:, b * P:(b + 1) * P], kbd[par][:, b, :, :], start=True, stop=False)
            con = ps.rearrange("p (h k) -> p h k", h=heads)[:, :, 0:NKEY]
            pe.matmul(con, ones_row[:, :], mask_row[:, bass.ds(g, 1), :, :], start=False,
                      stop=True).then_inc(scores_ready, 1)

        def turn_probs(pe, g, b):
            pe.wait_ge(probs_ready, g + 1)
            for m, (i, e) in enumerate(PLACES):
                at, n = PARTS[e]
                last = pe.transpose(turn_bank[0:n, m * P:(m + 1) * P], soft[b][:, i, at:at + n], ident[:, :])
            last.then_inc(turned, 1)

        def values(pe, g, b, par):
            pe.wait_ge(turned_out, g + 1)
            for m, (i, e) in enumerate(PLACES):
                v = raw_lat[par][:, b, 2 * P + i * 64:2 * P + (i + 1) * 64] if e else \
                    raw_ctx[par][:, b, P + i * 64:P + (i + 1) * 64]
                last = pe.matmul(out_bank[64 * i:64 * i + 64, 0:P], v, probsT[b % 2][0:PARTS[e][1], m, :],
                                 start=(e == 0), stop=(e == 1))
            last.then_inc(values_done, 1)

        def project(pe, g):
            pe.wait_ge(attnT_ready, g + 1)
            pe.wait_ge(added, g)
            pe.matmul(proj_bank[:, 0:P], ones_row[:, :], bo[:, :], start=True, stop=False)
            pe.matmul(proj_bank[:, 0:P], attnT[:, :], wo[:, :], start=False, stop=True).then_inc(proj_done, 1)

        block = ctx.enter_context(nc.Block())

        @block.sync
        def _(sp):
            sp.dma_start(ctx_tok[:, :, :], w["ctx_tok"]).then_inc(ctx_loaded, 16)
            for dst_ap, src in loads:
                sp.dma_start(dst_ap, src).then_inc(loaded, 16)

        @block.gpsimd
        def _(pool):
            for t in range(2):
                invert_roots(pool, t)
                invert_roots_again(pool, t)
            pool.wait_ge(rstd2_ready, 2)
            for tile in kbd:
                pool.memset(tile[0:64, :, 1, :], 0.0)
                last = pool.memset(tile[64:P, :, 0, :], 0.0)
            last.then_inc(constants, 1)
            pool.wait_ge(constants, 1)
            root_squares(pool, 0)
            weigh(pool, 0, 0)

            def body(turn, par, pair, final):
                for b, _, one_more in steps(final):
                    if one_more:
                        weigh(pool, turn * 4 + b + 1, (b + 1) % 4)
                    if b == 0 and final != 1:
                        root_squares(pool, turn + 1)
                    if b == 1 and final is None:
                        invert_roots(pool, turn + 2)
                    if b == 2 and final is None:
                        invert_roots_again(pool, turn + 2)

            over_turns(pool, body)

        @block.vector
        def _(dve):
            dve.wait_ge(ctx_loaded, 16)
            for t in range(2):
                link = variances(dve, t)
                normalize_once(dve, t, t, link)
                normalize_again(dve, t, t)
            dve.wait_ge(loaded, 16 * len(loads))
            for i in range(2):
                dve.tensor_scalar(mask_row[:, :, i, :], mask8[:, :].rearrange("p (b t) -> p b t", t=NKEY),
                                  1.0, 1e30, ALU.subtract, ALU.mult).then_inc(mask_ready, 1)
            dve.wait_ge(constants, 1)
            sum_squares(dve, 0)
            scale_rows(dve, 0, 0)
            take_keys(dve, 0, 0)
            for g in range(2):
                shift(dve, g, g, False)
            row_sums(dve, 0, 0, False)

            def body(turn, par, pair, final):
                for b, two_more, one_more in steps(final):
                    g = turn * 4 + b
                    if b == 2 and final != 1:
                        take_keys(dve, turn + 1, 1 - par)
                    if one_more:
                        row_sums(dve, g + 1, (b + 1) % 4, True)
                    if b == 0 and final != 1:
                        sum_squares(dve, turn + 1)
                    if b == 1 and final != 1:
                        scale_rows(dve, turn + 1, 1 - par)
                    if two_more:
                        shift(dve, g + 2, (b + 2) % 4, True)
                    if b == 2 and final is None:
                        normalize_once(dve, turn + 2, par, link)
                    dve.wait_ge(proj_done, g + 1)
                    dve.tensor_tensor(x[:, g, :], x[:, g, :], proj_bank[:, 0:P], ALU.add).then_inc(added, 1)
                    if b == 0 and final is None:
                        link = variances(dve, turn + 2)
                    if b == 2 and final is None:
                        normalize_again(dve, turn + 2, par)

            over_turns(dve, body)

        @block.scalar
        def _(act):
            act.wait_ge(loaded, 16 * len(loads))
            take_others(act, 0, 0, range(RAW))
            square(act, 0, 0)
            take_others(act, 0, 0, [RAW])
            take_others(act, 1, 1, range(RAW))
            square(act, 1, 1)
            for g in range(2):
                exponents(act, g, g)
            take_turned(act, 0, 0)

            def body(turn, par, pair, final):
                for b, two_more, one_more in steps(final):
                    g = turn * 4 + b
                    if b == 2 and final != 1:
                        take_others(act, turn + 1, 1 - par, [RAW])
                    act.wait_ge(values_done, g + 1)
                    act.copy(attnT[:, :], out_bank[:, 0:P]).then_inc(attnT_ready, 1)
                    if one_more:
                        take_turned(act, g + 1, (b + 1) % 4)
                    if two_more:
                        exponents(act, g + 2, (b + 2) % 4)
                    if b == 3 and final is None:
                        take_others(act, turn + 2, par, range(RAW))
                        square(act, turn + 2, par)

            over_turns(act, body)

        @block.tensor
        def _(pe):
            pe.wait_ge(loaded, 16 * len(loads))
            do_jobs(pe, 0, 0, range(J))
            do_jobs(pe, 1, 1, range(RAW))
            for i in range(3):
                pe.wait_ge(job_out[i], taken(0, J)[i])
            pe.wait_ge(mask_ready, 2)
            for g in range(2):
                scores(pe, g, g, 0, False)
            turn_probs(pe, 0, 0)

            def body(turn, par, pair, final):
                for b, two_more, one_more in steps(final):
                    g = turn * 4 + b
                    if b == 2 and two_more:
                        do_jobs(pe, turn + 1, 1 - par, range(RAW, J))
                        for i in range(3):
                            pe.wait_ge(job_out[i], taken(turn + 1, J)[i])
                    if two_more:
                        scores(pe, g + 2, (b + 2) % 4, par if b < 2 else 1 - par, True)
                    values(pe, g, b, par)
                    if one_more:
                        turn_probs(pe, g + 1, (b + 1) % 4)
                    project(pe, g)
                    if b == 3 and final is None:
                        do_jobs(pe, turn + 2, par, range(RAW))

            over_turns(pe, body)


def top_two(dve, link, net, logits, n, experts, tiles):
    shape = [P, n, experts]
    index = net.index64[:, 0:experts].unsqueeze(1).to_broadcast(shape)
    left = logits
    for rank in range(2):
        top, hot, least = tiles["top"][rank], tiles["hot"][rank], tiles["least"]
        link(dve.tensor_reduce(top, left, AX_X, ALU.max))
        link(dve.tensor_tensor(hot, left, top.unsqueeze(2).to_broadcast(shape), ALU.is_equal))
        link(dve.tensor_tensor(hot, hot, index, ALU.mult))
        link(dve.tensor_reduce(least, hot, AX_X, ALU.min))
        link(dve.tensor_tensor(hot, index, least.unsqueeze(2).to_broadcast(shape), ALU.is_equal))
        if rank == 0:
            left = tiles["left"]
            link(dve.scalar_tensor_tensor(left, hot, -3e38, logits, ALU.mult, ALU.add))


TOP_TWO_LINKS = 11


def dense_moe_stage(nc, net, spec, w):
    name, FF, kind = spec["name"], spec["FF"], spec["kind"]
    E, FC = 8, FF // P
    func = ACT.Gelu if kind == "pre" else ACT.Relu
    post = kind == "post"
    with ExitStack() as ctx:
        def sb(n, shape, dt=F32):
            return ctx.enter_context(nc.sbuf_tensor(f"{name}_{n}", shape, dt))

        def sem(n):
            return net.sem(f"{name}_{n}")

        x, ident, ones_row = net.x, net.ident, net.ones_row
        src = net.x1 if post else net.x
        hid_bank, y_bank, turn_bank, gate_bank = net.banks[0:4], net.banks[4:6], net.banks[6], net.banks[7]
        w1 = sb("w1", [P, E, FF]); w2 = sb("w2", [P, E, FC, P]); b1 = sb("b1", [P, E * FC]); b2 = sb("b2", [E, P])
        wg = sb("wg", [P, E]); bg = sb("bg", [1, E]); g_col = sb("g_col", [P, 1]); b_col = sb("b_col", [P, 1])
        loads = [(wg[:, :], w["wg"]), (bg[:, :], w["bg"]), (g_col[:, :], w["g_col"]), (b_col[:, :], w["b_col"]),
                 (b1[:, :], w["b1"]), (b2[:, :], w["b2"])]
        if post:
            g1, be1, g2, be2 = (sb(n, [P, P]) for n in ("g1", "be1", "g2", "be2"))
            loads += [(g1[:, :], w["g1"]), (be1[:, :], w["be1"]), (g2[:, :], w["g2"]), (be2[:, :], w["be2"])]
            stats2 = sb("stats2", [P, 4, 6]); mv2 = sb("mv2", [P, 4, 2]); rstd2 = sb("rstd2", [P, 4])
            out_n = sb("out_n", [P, 4, P])
        stats = sb("stats", [P, 4, 6]); mean_var = sb("mean_var", [P, 4, 2]); rstd = sb("rstd", [P, 4])
        idle = sb("idle", [P, 1])
        xn = sb("xn", [P, 4, P]); xn2 = sb("xn2", [P, 4, P]); base = sb("base", [P, 4, P])
        xT = [sb(f"xT{i}", [P, 4 * P]) for i in range(2)]
        gates = [sb(f"gates{i}", [P, 4, E]) for i in range(2)]
        acc = [sb(f"acc{i}", [P, 4, P]) for i in range(2)]
        logits = sb("logits", [P, 4, E]); expd = sb("expd", [P, 4, E]); both = sb("both", [P, 4, E])
        small = {n: sb(n, [P, 4]) for n in ("top0", "top1", "least", "total", "gate0", "gate1", "gap")}
        tiles = dict(top=[small["top0"][:, :], small["top1"][:, :]], least=small["least"][:, :],
                     hot=[sb(f"hot{i}", [P, 4, E])[:, :, :] for i in range(2)], left=sb("left", [P, 4, E])[:, :, :])
        gatesT = sb("gatesT", [E, 4 * P]); hT = [sb(f"hT{i}", [P, FC, 4 * P]) for i in range(2)]

        loaded, w1_loaded, w2_loaded, chain = (sem(n) for n in ("loaded", "w1_loaded", "w2_loaded", "chain"))
        var_ready, rstd_ready, normed = sem("var_ready"), sem("rstd_ready"), sem("normed")
        affine_done = sem("affine_done")
        xT_ps, xT_ready, logits_ps = sem("xT_ps"), sem("xT_ready"), sem("logits_ps")
        less_top, exp_done, gates_ready = sem("less_top"), sem("exp_done"), sem("gates_ready")
        gatesT_ps, gatesT_ready, bias_ps, acc_ready = sem("gatesT_ps"), sem("gatesT_ready"), sem("bias_ps"), sem("acc_ready")
        hid_ready, hid_out, y_ready, y_added = sem("hid_ready"), sem("hid_out"), sem("y_ready"), sem("y_added")
        var2_ready, rstd2_ready, finished = sem("var2_ready"), sem("rstd2_ready"), sem("finished")
        NORMS = 1 if post else 2
        LINKS = 1 + TOP_TWO_LINKS + (2 + 4 if post else 6 + 8)
        post_chain = sem("post_chain")

        def norm_dve(dve, t, link, out, inp, i):
            for b in range(4):
                last = dve.bn_stats(stats[:, b, :], inp(b))
            link(last)
            dve.memset(idle[:, :], 0.0)
            for b in range(4):
                last = dve.bn_aggr(mean_var[:, b, :], stats[:, b, :])
            link(last)
            dve.tensor_scalar(rstd[:, :], mean_var[:, :, 1], EPS, None, ALU.add).then_inc(var_ready, 1)
            dve.wait_ge(rstd_ready, t * NORMS + i + 1)
            for b in range(4):
                last = dve.tensor_scalar(out[:, b, :], inp(b), mean_var[:, b, 0:1], rstd[:, b:b + 1],
                                         ALU.subtract, ALU.mult)
            return last

        def prep_dve(dve, t, par, part, link):
            if part == "norm":
                norm_part(dve, t, link)
            elif part == "gates":
                gates_part(dve, t, par, link)
            else:
                start_part(dve, t, par, link)

        def norm_part(dve, t, link):
            last = norm_dve(dve, t, link, xn, lambda b: src[:, t * 4 + b, :], 0)
            if post:
                last.then_inc(normed, 1)
            else:
                link(last)
                norm_dve(dve, t, link, xn2, lambda b: xn[:, b, :], 1).then_inc(normed, 1)
                link(dve.tensor_tensor(base[:, :, :], x[:, bass.ds(t * 4, 4), :], xn[:, :, :], ALU.add))

        def gates_part(dve, t, par, link):
            dve.wait_ge(logits_ps, t + 1)
            link(dve.tensor_copy(logits[:, :, :], gate_bank[:, 0:4 * E].rearrange("p (b e) -> p b e", b=4)))
            top_two(dve, link, net, logits[:, :, :], 4, E, tiles)
            shape = [P, 4, E]
            dve.tensor_tensor(expd[:, :, :], logits[:, :, :], tiles["top"][0].unsqueeze(2).to_broadcast(shape),
                              ALU.subtract).then_inc(less_top, 1)
            dve.wait_ge(exp_done, t + 1)
            link(dve.tensor_reduce(small["total"][:, :], expd[:, :, :], AX_X, ALU.add))
            link(dve.reciprocal(small["gate0"][:, :], small["total"][:, :]))
            link(dve.tensor_tensor(expd[:, :, :], expd[:, :, :],
                                   small["gate0"][:, :].unsqueeze(2).to_broadcast(shape), ALU.mult))
            link(dve.tensor_tensor(both[:, :, :], tiles["hot"][0], tiles["hot"][1], ALU.add))
            gate = gates[par][:, :, :]
            if post:
                dve.tensor_tensor(gate, expd[:, :, :], both[:, :, :], ALU.mult).then_inc(gates_ready, 1)
            else:
                link(dve.tensor_tensor(gate, expd[:, :, :], both[:, :, :], ALU.mult))
                link(dve.tensor_reduce(small["total"][:, :], gate, AX_X, ALU.add))
                link(dve.tensor_scalar(small["total"][:, :], small["total"][:, :], 1e-8, None, ALU.add))
                link(dve.reciprocal(small["gap"][:, :], small["total"][:, :]))
                dve.tensor_tensor(gate, gate, small["gap"][:, :].unsqueeze(2).to_broadcast(shape),
                                  ALU.mult).then_inc(gates_ready, 1)

        def start_part(dve, t, par, link):
            link.end()
            dve.wait_ge(bias_ps, t + 1)
            if post:
                dve.wait_ge(affine_done, t + 1)
            dve.tensor_tensor(acc[par][:, :, :], turn_bank[:, :].rearrange("p (b f) -> p b f", b=4),
                              (xn2 if post else base)[:, :, :], ALU.add).then_inc(acc_ready, 1)

        def prep_pool(pool, t):
            for i in range(NORMS):
                pool.wait_ge(var_ready, t * NORMS + i + 1)
                pool.tensor_tensor(rstd[:, :], rstd[:, :], net.minus_half[:, 0:4], ALU.pow).then_inc(rstd_ready, 1)
            if post:
                pool.wait_ge(normed, t + 1)
                shape = [P, 4, P]
                pool.wait_ge(acc_ready, t)
                pool.tensor_tensor(xn2[:, :, :], xn[:, :, :], g1[:, :].unsqueeze(1).to_broadcast(shape),
                                   ALU.mult).then_inc(affine_half, 1)
                pool.wait_ge(affine_half, t + 1)
                pool.tensor_tensor(xn2[:, :, :], xn2[:, :, :], be1[:, :].unsqueeze(1).to_broadcast(shape),
                                   ALU.add).then_inc(affine_done, 1)

        affine_half, out_half = sem("affine_half"), sem("out_half")

        def prep_act(act, t, par, part):
            if part == "tokens":
                act.wait_ge(xT_ps, t + 1)
                act.activation(xT[par][:, :], turn_bank[:, :], ACT.Identity, scale=g_col[:, 0:1],
                               bias=b_col[:, 0:1]).then_inc(xT_ready, 1)
            elif part == "exp":
                act.wait_ge(less_top, t + 1)
                act.activation(expd[:, :, :], expd[:, :, :], ACT.Exp).then_inc(exp_done, 1)
            else:
                act.wait_ge(gatesT_ps, t + 1)
                act.copy(gatesT[:, :], gate_bank[0:E, :]).then_inc(gatesT_ready, 1)

        def prep_pe(pe, t, par, part):
            if part == 0:
                pe.wait_ge(normed, t + 1)
                for b in range(4):
                    last = pe.transpose(turn_bank[:, b * P:(b + 1) * P], (xn if post else xn2)[:, b, :], ident[:, :])
                last.then_inc(xT_ps, 1)
            if part == 1:
                pe.wait_ge(xT_ready, t + 1)
                for b in range(4):
                    out = gate_bank[:, b * E:(b + 1) * E]
                    pe.matmul(out, xT[par][:, b * P:(b + 1) * P], wg[:, :], start=True, stop=False)
                    last = pe.matmul(out, ones_row[:, :], bg[:, :], start=False, stop=True)
                last.then_inc(logits_ps, 1)
            if part == 2:
                pe.wait_ge(gates_ready, t + 1)
                for b in range(4):
                    last = pe.transpose(gate_bank[0:E, b * P:(b + 1) * P], gates[par][:, b, :], ident[:, :])
                last.then_inc(gatesT_ps, 1)
            if part == 3:
                pe.wait_ge(gatesT_ready, t + 1)
                for b in range(4):
                    last = pe.matmul(turn_bank[:, b * P:(b + 1) * P], gatesT[:, b * P:(b + 1) * P], b2[:, :],
                                     start=True, stop=True)
                last.then_inc(bias_ps, 1)

        def hidden_pe(pe, t, par, e):
            for c in range(FC):
                n = e * FC + c
                if n >= 4:
                    pe.wait_ge(hid_out, t * E * FC + n - 3)
                pe.matmul(hid_bank[n % 4][:, :], w1[:, e, c * P:(c + 1) * P], xT[par][:, :],
                          start=True, stop=True).then_inc(hid_ready, 1)

        def output_pe(pe, t, e):
            pe.wait_ge(hid_out, (t * E + e + 1) * FC)
            pe.wait_ge(y_added, t * E + max(e - 1, 0))
            for b in range(4):
                for c in range(FC):
                    last = pe.matmul(y_bank[e % 2][:, b * P:(b + 1) * P], hT[e % 2][:, c, b * P:(b + 1) * P],
                                     w2[:, e, c, :], start=(c == 0), stop=(c == FC - 1))
            last.then_inc(y_ready, 1)

        def experts_act(act, t, e):
            for c in range(FC):
                n = e * FC + c
                act.wait_ge(hid_ready, t * E * FC + n + 1)
                if c == 0 and e >= 2:
                    act.wait_ge(y_ready, t * E + e - 1)
                act.activation(hT[e % 2][:, c, :], hid_bank[n % 4][:, :], func,
                               bias=b1[:, n:n + 1]).then_inc(hid_out, 1)

        def add_dve(dve, t, par, e):
            dve.wait_ge(y_ready, t * E + e + 1)
            if e == 0:
                dve.wait_ge(acc_ready, t + 1)
            else:
                dve.wait_ge(y_added, t * E + e)
            for b in range(4):
                out = x[:, t * 4 + b, :] if e == E - 1 and not post else acc[par][:, b, :]
                last = dve.scalar_tensor_tensor(out, y_bank[e % 2][:, b * P:(b + 1) * P], gates[par][:, b, e:e + 1],
                                                acc[par][:, b, :], ALU.mult, ALU.add)
            last.then_inc(y_added, 1)

        def finish_dve(dve, t, par):
            link = Link(dve, post_chain, t, 2)
            dve.wait_ge(y_added, (t + 1) * E)
            for b in range(4):
                last = dve.bn_stats(stats2[:, b, :], acc[par][:, b, :])
            link(last)
            dve.memset(idle[:, :], 0.0)
            for b in range(4):
                last = dve.bn_aggr(mv2[:, b, :], stats2[:, b, :])
            link(last)
            dve.tensor_scalar(rstd2[:, :], mv2[:, :, 1], EPS, None, ALU.add).then_inc(var2_ready, 1)
            dve.wait_ge(rstd2_ready, t + 1)
            dve.wait_ge(finished, t)
            for b in range(4):
                last = dve.tensor_scalar(out_n[:, b, :], acc[par][:, b, :], mv2[:, b, 0:1], rstd2[:, b:b + 1],
                                         ALU.subtract, ALU.mult)
            last.then_inc(out_normed, 1)
            link.end()

        out_normed = sem("out_normed")

        def finish_pool(pool, t):
            shape = [P, 4, P]
            pool.wait_ge(var2_ready, t + 1)
            pool.tensor_tensor(rstd2[:, :], rstd2[:, :], net.minus_half[:, 0:4], ALU.pow).then_inc(rstd2_ready, 1)
            pool.wait_ge(out_normed, t + 1)
            pool.tensor_tensor(out_n[:, :, :], out_n[:, :, :], g2[:, :].unsqueeze(1).to_broadcast(shape),
                               ALU.mult).then_inc(out_half, 1)
            pool.wait_ge(out_half, t * 2 + 1)
            pool.tensor_tensor(out_n[:, :, :], out_n[:, :, :], be2[:, :].unsqueeze(1).to_broadcast(shape),
                               ALU.add).then_inc(out_half, 1)
            pool.wait_ge(out_half, t * 2 + 2)
            tokens = x[:, bass.ds(t * 4, 4), :]
            pool.tensor_tensor(tokens, tokens, out_n[:, :, :], ALU.add).then_inc(finished, 1)

        def turns(eng, body, prep):
            prep(0, 0)
            with eng.Fori(0, NTURN // 2 - 1) as i:
                body(i * 2, 0, True)
                body(i * 2 + 1, 1, True)
            body(NTURN - 2, 0, True)
            body(NTURN - 1, 1, False)

        block = ctx.enter_context(nc.Block())

        @block.sync
        def _(sp):
            for dst_ap, s in loads:
                sp.dma_start(dst_ap, s).then_inc(loaded, 16)
            sp.dma_start(w1[:, :, :], w["w1"]).then_inc(w1_loaded, 16)
            sp.dma_start(w2[:, :, :, :], w["w2"]).then_inc(w2_loaded, 16)

        @block.gpsimd
        def _(pool):
            pool.wait_ge(loaded, 16 * len(loads))

            def body(t, par, more):
                if more:
                    prep_pool(pool, t + 1)
                if post:
                    finish_pool(pool, t)

            turns(pool, body, lambda t, par: prep_pool(pool, t))

        @block.vector
        def _(dve):
            dve.wait_ge(loaded, 16 * len(loads))

            def body(t, par, more):
                link = Link(dve, chain, t + 1, LINKS)
                for e in range(E):
                    add_dve(dve, t, par, e)
                    if more and e in (0, 3, 6):
                        prep_dve(dve, t + 1, 1 - par, {0: "norm", 3: "gates", 6: "start"}[e], link)
                if post:
                    finish_dve(dve, t, par)

            def first(t, par):
                link = Link(dve, chain, t, LINKS)
                for part in ("norm", "gates", "start"):
                    prep_dve(dve, t, par, part, link)

            turns(dve, body, first)

        @block.scalar
        def _(act):
            act.wait_ge(loaded, 16 * len(loads))

            def body(t, par, more):
                for e in range(E):
                    experts_act(act, t, e)
                    if more and e in (3, 4, 6):
                        prep_act(act, t + 1, 1 - par, {3: "tokens", 4: "exp", 6: "gates"}[e])

            def first(t, par):
                for part in ("tokens", "exp", "gates"):
                    prep_act(act, t, par, part)

            turns(act, body, first)

        @block.tensor
        def _(pe):
            pe.wait_ge(loaded, 16 * len(loads))

            def body(t, par, more):
                hidden_pe(pe, t, par, 0)
                for e in range(E):
                    if e + 1 < E:
                        hidden_pe(pe, t, par, e + 1)
                    output_pe(pe, t, e)
                    if more and e in (2, 3, 5, 6):
                        prep_pe(pe, t + 1, 1 - par, (2, 3, 5, 6).index(e))

            def first(t, par):
                for part in range(4):
                    prep_pe(pe, t, par, part)
                pe.wait_ge(w1_loaded, 16)
                pe.wait_ge(w2_loaded, 16)

            turns(pe, body, first)


SLOTS_1 = 24 * 384
SLOTS_2 = 2 * NBATCH * P


class Routed:

    def __init__(self, nc, ctx, name):
        def sb(n, shape, dt=F32):
            return ctx.enter_context(nc.sbuf_tensor(f"{name}_{n}", shape, dt))

        self.xn = sb("xn_all", [P, NBATCH, P])
        self.gate = sb("gate", [P, 2, NBATCH])
        self.write = sb("slot_write", [P, NBATCH, 2], U32)
        self.read = sb("slot_read", [P, NBATCH, 2], U32)


def norm_and_logits(nc, net, name, E, wg_dram, routed, logits, fill=False):
    with ExitStack() as ctx:
        def sb(n, shape, dt=F32):
            return ctx.enter_context(nc.sbuf_tensor(f"{name}n_{n}", shape, dt))

        def sem(n):
            return net.sem(f"{name}n_{n}")

        x, xn, HALF = net.x, routed.xn, NTURN // 2
        wg = sb("wg", [P, E])
        stats = sb("stats", [P, NBATCH, 6]); mean_var = sb("mean_var", [P, NBATCH, 2]); rstd = sb("rstd", [P, NBATCH])
        xT = [sb(f"xT{i}", [P, 4 * P]) for i in range(2)]
        turn_bank, logit_bank = net.banks[0:2], net.banks[2:4]
        loaded, chain = sem("loaded"), sem("chain")
        var_ready, rstd_ready, normed = sem("var_ready"), sem("rstd_ready"), sem("normed")
        xT_ps, xT_ready, logits_ps = sem("xT_ps"), sem("xT_ready"), sem("logits_ps")

        block = ctx.enter_context(nc.Block())

        @block.sync
        def _(sp):
            sp.dma_start(wg[:, :], wg_dram).then_inc(loaded, 16)
            if fill:
                fill_zeros(net, None, sp)
            sp.wait_ge(loaded, 16)

        @block.gpsimd
        def _(pool):
            if fill:
                fill_zeros(net, pool, None)
            pool.wait_ge(var_ready, 1)
            pool.tensor_tensor(rstd[:, :], rstd[:, :], net.minus_half[:, :], ALU.pow).then_inc(rstd_ready, 1)

        @block.vector
        def _(dve):
            link = Link(dve, chain, 0, 2)
            for b in range(NBATCH):
                last = dve.bn_stats(stats[:, b, :], x[:, b, :])
            link(last)
            for b in range(NBATCH):
                last = dve.bn_aggr(mean_var[:, b, :], stats[:, b, :])
            link(last)
            link.end()
            dve.tensor_scalar(rstd[:, :], mean_var[:, :, 1], EPS, None, ALU.add).then_inc(var_ready, 1)
            dve.wait_ge(rstd_ready, 1)
            for t in range(NTURN):
                for b in range(t * 4, t * 4 + 4):
                    last = dve.tensor_scalar(xn[:, b, :], x[:, b, :], mean_var[:, b, 0:1], rstd[:, b:b + 1],
                                             ALU.subtract, ALU.mult)
                last.then_inc(normed, 1)
            for h in range(2):
                dve.wait_ge(logits_ps, h + 1)
                dve.tensor_copy(logits[:, :, h * 16:h * 16 + 16],
                                logit_bank[h][:, 0:16 * E].rearrange("p (b e) -> p e b", b=16))

        @block.scalar
        def _(act):
            for t in range(NTURN):
                act.wait_ge(xT_ps, t + 1)
                act.copy(xT[t % 2][:, :], turn_bank[t % 2][:, :]).then_inc(xT_ready, 1)

        @block.tensor
        def _(pe):
            def turn(t):
                pe.wait_ge(normed, t + 1)
                for b in range(4):
                    last = pe.transpose(turn_bank[t % 2][:, b * P:(b + 1) * P], xn[:, t * 4 + b, :], net.ident[:, :])
                last.then_inc(xT_ps, 1)

            pe.wait_ge(loaded, 16)
            turn(0)
            for t in range(NTURN):
                if t + 1 < NTURN:
                    turn(t + 1)
                pe.wait_ge(xT_ready, t + 1)
                for b in range(4):
                    at = (t % HALF * 4 + b) * E
                    last = pe.matmul(logit_bank[t // HALF][:, at:at + E], xT[t % 2][:, b * P:(b + 1) * P],
                                     wg[:, :], start=True, stop=True)
                if t % HALF == HALF - 1:
                    last.then_inc(logits_ps, 1)


def route(nc, net, name, E, capacity, consts, routed, logits):
    grouped = capacity is not None
    with ExitStack() as ctx:
        def sb(n, shape, dt=F32):
            return ctx.enter_context(nc.sbuf_tensor(f"{name}r_{n}", shape, dt))

        def sem(n):
            return net.sem(f"{name}r_{n}")

        B, W = NBATCH, E * NBATCH
        lower = sb("lower", [P, P]); whole = sb("whole", [P, P]); reset = sb("reset", [P, E, B])
        base = sb("base", [P, E]); one = sb("one", [P, E])
        hot = [sb(f"hot{i}", [P, E, B]) for i in range(2)]
        left = sb("left", [P, E, B]); count = [sb(f"count{i}", [P, E, B]) for i in range(2)]
        top = [sb(f"top{i}", [P, B]) for i in range(2)]
        least = sb("least", [P, B]); gap = sb("gap", [P, 2, B]); total = sb("total", [P, B])
        rank = sb("rank", [P, 2, B]); start = sb("start", [P, 2, B]); keep = sb("keep", [P, 2, B])
        slot = sb("slot", [P, 2, B]); sizes = sb("sizes", [P, E])
        loaded, chain = sem("loaded"), sem("chain")
        less_top, exp_done, counts_ready, ranks_ps = (
            sem("less_top"), sem("exp_done"), sem("counts_ready"), sem("ranks_ps"))
        shape = [P, B, E]

        def by_token(tile):
            return tile[:, :, :].rearrange("p e b -> p b e")

        def flat(tile):
            return tile[:, :, :].rearrange("p e b -> p (e b)")

        sets = hot if grouped else [left]
        half = W // 2 if grouped else W
        banks = [net.banks[2 * r:2 * r + 2] if grouped else [net.banks[0]] for r in range(len(sets))]

        block = ctx.enter_context(nc.Block())

        @block.sync
        def _(sp):
            for dst_ap, s in ((lower[:, :], consts["lower"]), (whole[:, :], consts["whole"]),
                              (reset[:, :, :], consts["reset"]), (base[:, :], consts["base"])):
                sp.dma_start(dst_ap, s).then_inc(loaded, 16)
            sp.wait_ge(loaded, 64)

        @block.scalar
        def _(act):
            act.wait_ge(less_top, 1)
            if grouped:
                act.activation(flat(left), flat(left), ACT.Exp)
            act.activation(gap[:, 0, :], gap[:, 0, :], ACT.Exp).then_inc(exp_done, 1)

        @block.vector
        def _(dve):
            link = Link(dve, chain, 0, 0)
            dve.wait_ge(loaded, 64)
            top_two(dve, link, net, by_token(logits), B, E,
                    dict(top=[top[0][:, :], top[1][:, :]], hot=[by_token(hot[0]), by_token(hot[1])],
                         least=least[:, :], left=by_token(left)))
            if grouped:
                link(dve.tensor_tensor(by_token(left), by_token(logits),
                                       top[0][:, :].unsqueeze(2).to_broadcast(shape), ALU.subtract))
            dve.tensor_tensor(gap[:, 0, :], top[1][:, :], top[0][:, :], ALU.subtract).then_inc(less_top, 1)
            dve.wait_ge(exp_done, 1)
            if grouped:
                link(dve.tensor_reduce(total[:, :], by_token(left), AX_X, ALU.add))
            else:
                link(dve.tensor_scalar(total[:, :], gap[:, 0, :], 1.0, None, ALU.add))
            link(dve.reciprocal(routed.gate[:, 0, :], total[:, :]))
            link(dve.tensor_tensor(routed.gate[:, 1, :], gap[:, 0, :], routed.gate[:, 0, :], ALU.mult))
            if not grouped:
                link(dve.tensor_tensor(flat(left), flat(hot[0]), flat(hot[1]), ALU.add))
                link(dve.memset(one[:, :], 1.0))
            for r, s in enumerate(sets):
                link(dve.tensor_tensor_scan(flat(count[r]), flat(reset), flat(s), 0.0, ALU.mult, ALU.add))
            link(dve.tensor_copy(sizes[:, :], count[0][:, :, B - 1]))
            for r, s in enumerate(sets):
                link(dve.tensor_tensor(flat(count[r]), flat(count[r]), flat(s), ALU.subtract))
            if grouped:
                link(dve.tensor_tensor(count[1][:, :, :], count[1][:, :, :],
                                       sizes[:, :].unsqueeze(2).to_broadcast([P, E, B]), ALU.add))
            dve.sem_inc(counts_ready, 1)
            dve.wait_ge(ranks_ps, 1)
            if not grouped:
                link(dve.tensor_copy(sizes[:, :], net.banks[1][:, 0:E]))
                link(dve.tensor_tensor_scan(base[:, :], one[:, :], sizes[:, :], 0.0, ALU.mult, ALU.add))
                link(dve.tensor_tensor(base[:, :], base[:, :], sizes[:, :], ALU.subtract))
            for r in range(2):
                n = r if grouped else 0
                step = half // B
                for i, bank in enumerate(banks[n]):
                    link(dve.tensor_tensor(left[:, i * step:(i + 1) * step, :], hot[r][:, i * step:(i + 1) * step, :],
                                           bank[:, 0:half].rearrange("p (e b) -> p e b", b=B), ALU.mult))
                link(dve.tensor_reduce(rank[:, r, :], by_token(left), AX_X, ALU.add))
                link(dve.tensor_tensor(left[:, :, :], hot[r][:, :, :],
                                       base[:, :].unsqueeze(2).to_broadcast([P, E, B]), ALU.mult))
                link(dve.tensor_reduce(start[:, r, :], by_token(left), AX_X, ALU.add))
            link(dve.tensor_tensor(slot[:, :, :], rank[:, :, :], start[:, :, :], ALU.add))
            if grouped:
                link(dve.tensor_scalar(keep[:, :, :], rank[:, :, :], float(capacity), None, ALU.is_lt))
                link(dve.tensor_tensor(routed.gate[:, :, :], routed.gate[:, :, :], keep[:, :, :], ALU.mult))
                link(dve.tensor_tensor(total[:, :], routed.gate[:, 0, :], routed.gate[:, 1, :], ALU.add))
                link(dve.tensor_scalar(total[:, :], total[:, :], 1e-9, None, ALU.max))
                link(dve.reciprocal(least[:, :], total[:, :]))
                link(dve.tensor_tensor(routed.gate[:, :, :], routed.gate[:, :, :],
                                       least[:, :].unsqueeze(1).to_broadcast([P, 2, B]), ALU.mult))
                for out, other in ((routed.write, SLOTS_1 + 1), (routed.read, SLOTS_1)):
                    link(dve.tensor_scalar(start[:, :, :], slot[:, :, :], -float(other), None, ALU.add))
                    link(dve.tensor_tensor(start[:, :, :], start[:, :, :], keep[:, :, :], ALU.mult))
                    link(dve.tensor_scalar(out[:, :, :].rearrange("p b r -> p r b"), start[:, :, :],
                                           float(other), None, ALU.add))
            else:
                link(dve.tensor_copy(routed.write[:, :, :].rearrange("p b r -> p r b"), slot[:, :, :]))
                link(dve.tensor_copy(routed.read[:, :, :].rearrange("p b r -> p r b"), slot[:, :, :]))

        @block.tensor
        def _(pe):
            pe.wait_ge(counts_ready, 1)
            for r, s in enumerate(sets):
                for i, bank in enumerate(banks[r]):
                    at = slice(i * half, (i + 1) * half)
                    pe.matmul(bank[:, 0:half], lower[:, :], flat(s)[:, at], start=True, stop=False)
                    last = pe.matmul(bank[:, 0:half], whole[:, :], flat(count[r])[:, at], start=False, stop=True)
            if not grouped:
                last = pe.matmul(net.banks[1][:, 0:E], whole[:, :], sizes[:, :], start=True, stop=True)
            last.then_inc(ranks_ps, 1)


def carry_wait(pool, net, idle, carried, before):
    pool.wait_ge(carried, before)
    pool.tensor_tensor(idle[:, :], net.plus_half[:, 0:1], net.plus_half[:, 0:1], ALU.mult).then_inc(carried, 1)


def scatter_rows(nc, net, name, routed, slots_dram, n_slots):
    with ExitStack() as ctx:
        def sb(n, shape, dt=F32):
            return ctx.enter_context(nc.sbuf_tensor(f"{name}s_{n}", shape, dt))

        rows = [sb(f"rows{i}", [P, 4, P]) for i in range(2)]
        where = [sb(f"where{i}", [P, 4, 2], U32) for i in range(2)]
        idle = sb("idle", [P, 1])
        staged, carried = net.sem(f"{name}s_staged"), net.sem(f"{name}s_carried")
        written = [net.sem(f"{name}s_written{i}") for i in range(2)]
        block = ctx.enter_context(nc.Block())

        @block.vector
        def _(dve):
            with dve.Fori(0, NTURN // 2) as i:
                for par in range(2):
                    t = i * 2 + par
                    dve.wait_ge(written[par], i * 8 * 16)
                    dve.tensor_copy(rows[par][:, :, :], routed.xn[:, bass.ds(t * 4, 4), :])
                    dve.tensor_copy(where[par][:, :, :], routed.write[:, bass.ds(t * 4, 4), :]).then_inc(staged, 1)

        @block.gpsimd
        def _(pool):
            with pool.Fori(0, NTURN // 2) as i:
                for par in range(2):
                    pool.wait_ge(staged, i * 2 + par + 1)
                    carry_wait(pool, net, idle, carried, i * 2 + par)
                    for b in range(4):
                        for r in range(2):
                            pool.indirect_dma_start(
                                slots_dram[:, :], bass.IndirectOffsetOnAxis(where[par][:, b, r:r + 1], 0),
                                rows[par][:, b, :], None, bounds_check=n_slots - 1,
                                oob_is_err=False).then_inc(written[par], 16)
            for par in range(2):
                pool.wait_ge(written[par], NTURN // 2 * 8 * 16)


def combine_rows(nc, net, name, routed, rows_dram, n_rows, final):
    with ExitStack() as ctx:
        def sb(n, shape, dt=F32):
            return ctx.enter_context(nc.sbuf_tensor(f"{name}c_{n}", shape, dt))

        def sem(n):
            return net.sem(f"{name}c_{n}")

        x = net.x
        got = [[sb(f"got{i}{r}", [P, 4, P]) for r in range(2)] for i in range(2)]
        where = [sb(f"where{i}", [P, 4, 2], U32) for i in range(2)]
        acc = sb("acc", [P, 4, P]); stats = sb("stats", [P, 4, 6]); mean_var = sb("mean_var", [P, 4, 2])
        rstd = sb("rstd", [P, 4]); idle = sb("idle", [P, 1]); pool_idle = sb("pool_idle", [P, 1])
        gain = sb("gain", [P, P]); offset = sb("offset", [P, P])
        loaded, staged, chain, used = sem("loaded"), sem("staged"), sem("chain"), sem("used")
        var_ready, rstd_ready = sem("var_ready"), sem("rstd_ready")
        chain2, carried = sem("chain2"), sem("carried")
        gathered = [sem(f"gathered{i}") for i in range(2)]
        LINKS = 7 if final else 2
        block = ctx.enter_context(nc.Block())

        if final:
            @block.sync
            def _(sp):
                sp.dma_start(gain[:, :], final[0]).then_inc(loaded, 16)
                sp.dma_start(offset[:, :], final[1]).then_inc(loaded, 16)
                sp.wait_ge(loaded, 32)

        @block.scalar
        def _(act):
            with act.Fori(0, NTURN // 2) as i:
                for par in range(2):
                    act.wait_ge(gathered[par], i * 8 * 16)
                    act.copy(where[par][:, :, :],
                             routed.read[:, bass.ds((i * 2 + par) * 4, 4), :]).then_inc(staged, 1)

        @block.gpsimd
        def _(pool):
            def gather(par):
                for b in range(4):
                    for r in range(2):
                        pool.indirect_dma_start(
                            got[par][r][:, b, :], None, rows_dram[:, :],
                            bass.IndirectOffsetOnAxis(where[par][:, b, r:r + 1], 0),
                            bounds_check=n_rows - 1, oob_is_err=False).then_inc(gathered[par], 16)

            def body(t, par, pair, last):
                if last != 1:
                    pool.wait_ge(used, t)
                    pool.wait_ge(staged, t + 2)
                    carry_wait(pool, net, pool_idle, carried, t)
                    gather(1 - par)
                if final:
                    pool.wait_ge(var_ready, t + 1)
                    pool.tensor_tensor(rstd[:, :], rstd[:, :], net.minus_half[:, 0:4], ALU.pow).then_inc(rstd_ready, 1)

            pool.wait_ge(staged, 1)
            gather(0)
            over_turns(pool, body)

        @block.vector
        def _(dve):
            if final:
                dve.wait_ge(loaded, 32)
            with dve.Fori(0, NTURN // 2) as i:
                link = Link(dve, chain, i, 2 * LINKS)
                for par in range(2):
                    t = i * 2 + par
                    dve.wait_ge(gathered[par], (i + 1) * 8 * 16)
                    start = routed.xn if final else x
                    for b in range(4):
                        last = dve.scalar_tensor_tensor(acc[:, b, :], got[par][0][:, b, :],
                                                        routed.gate[:, 0, bass.ds(t * 4 + b, 1)],
                                                        start[:, t * 4 + b, :], ALU.mult, ALU.add)
                    link(last)
                    for b in range(4):
                        out = acc[:, b, :] if final else x[:, t * 4 + b, :]
                        last = dve.scalar_tensor_tensor(out, got[par][1][:, b, :],
                                                        routed.gate[:, 1, bass.ds(t * 4 + b, 1)],
                                                        acc[:, b, :], ALU.mult, ALU.add)
                    link(last)
                    dve.sem_inc(used, 1)
                    if final:
                        shape = [P, 4, P]
                        for b in range(4):
                            last = dve.bn_stats(stats[:, b, :], acc[:, b, :])
                        link(last)
                        dve.memset(idle[:, :], 0.0)
                        for b in range(4):
                            last = dve.bn_aggr(mean_var[:, b, :], stats[:, b, :])
                        link(last)
                        dve.tensor_scalar(rstd[:, :], mean_var[:, :, 1], 1e-6, None, ALU.add).then_inc(var_ready, 1)
                        dve.wait_ge(rstd_ready, t + 1)
                        for b in range(4):
                            last = dve.tensor_scalar(acc[:, b, :], acc[:, b, :], mean_var[:, b, 0:1],
                                                     rstd[:, b:b + 1], ALU.subtract, ALU.mult)
                        link(last)
                        link(dve.tensor_tensor(acc[:, :, :], acc[:, :, :],
                                               gain[:, :].unsqueeze(1).to_broadcast(shape), ALU.mult))
                        link(dve.tensor_tensor(acc[:, :, :], acc[:, :, :],
                                               offset[:, :].unsqueeze(1).to_broadcast(shape), ALU.add))
                        tokens = x[:, bass.ds(t * 4, 4), :]
                        dve.tensor_tensor(tokens, tokens, acc[:, :, :], ALU.add).then_inc(chain2, 1)
                        dve.wait_ge(chain2, t + 1)
                link.end()


def chunk_experts(nc, net, w1_dram, w2_dram, slots_dram, rows_dram):
    E, FC = 8, 4
    with ExitStack() as ctx:
        def sb(n, shape, dt=F32):
            return ctx.enter_context(nc.sbuf_tensor(f"L2e_{n}", shape, dt))

        def sem(n):
            return net.sem(f"L2e_{n}")

        w1 = [sb(f"w1{i}", [P, FC * P]) for i in range(2)]; w2 = [sb(f"w2{i}", [P, FC, P]) for i in range(2)]
        rows = [sb(f"rows{i}", [P, 4, P]) for i in range(2)]; xT = [sb(f"xT{i}", [P, 4 * P]) for i in range(2)]
        hT = [sb(f"hT{i}", [P, FC, 4 * P]) for i in range(2)]; y = [sb(f"y{i}", [P, 4, P]) for i in range(2)]
        hid_bank, y_bank, turn_bank = net.banks[0:4], net.banks[4:6], net.banks[6:8]
        w_loaded = [sem(f"w_loaded{i}") for i in range(2)]
        rows_loaded = [sem(f"rows_loaded{i}") for i in range(2)]
        stored = [sem(f"stored{i}") for i in range(2)]
        xT_ps, xT_ready, hid_ready, hid_out, y_ready, y_out = (
            sem(n) for n in ("xT_ps", "xT_ready", "hid_ready", "hid_out", "y_ready", "y_out"))
        slots = slots_dram.rearrange("(h p q) d -> h p q d", p=P, q=4)
        outs = rows_dram.rearrange("(h p q) d -> h p q d", p=P, q=4)
        NI = E // 2
        block = ctx.enter_context(nc.Block())

        @block.sync
        def _(sp):
            def load_rows(h, par):
                sp.dma_start(rows[par][:, :, :], slots[h, :, :, :]).then_inc(rows_loaded[par], 16)

            def load_weights(i, e):
                sp.dma_start(w1[e][:, :], w1_dram[:, i * 2 + e, :]).then_inc(w_loaded[e], 16)
                sp.dma_start(w2[e][:, :, :], w2_dram[:, i * 2 + e, :, :]).then_inc(w_loaded[e], 16)

            def load_ahead(i, n, more):
                sp.wait_ge(xT_ps, i * 4 + n + 1)
                load_rows(i * 4 + n + 2, n % 2)
                if more and n % 2:
                    sp.wait_ge(y_ready, i * 4 + n + 1)
                    load_weights(i + 1, n // 2)

            load_rows(0, 0)
            load_weights(0, 0)
            load_rows(1, 1)
            load_weights(0, 1)
            with sp.Fori(0, NI - 1) as i:
                for n in range(4):
                    load_ahead(i, n, True)
            for n in range(2):
                load_ahead(NI - 1, n, False)

        @block.gpsimd
        def _(pool):
            with pool.Fori(0, NI) as i:
                for n in range(4):
                    pool.wait_ge(y_out, i * 4 + n + 1)
                    pool.dma_start(outs[i * 4 + n, :, :, :], y[n % 2][:, :, :]).then_inc(stored[n % 2], 16)
            for par in range(2):
                pool.wait_ge(stored[par], NI * 2 * 16)

        @block.scalar
        def _(act):
            with act.Fori(0, NI) as i:
                for n in range(4):
                    h = i * 4 + n
                    for c in range(FC):
                        act.wait_ge(hid_ready, h * FC + c + 1)
                        if c == 0 and n >= 2:
                            act.wait_ge(y_ready, h - 1)
                        elif c == 0:
                            act.wait_ge(y_ready, i * 4)
                        act.activation(hT[n % 2][:, c, :], hid_bank[c][:, :], ACT.Gelu).then_inc(hid_out, 1)

        @block.vector
        def _(dve):
            with dve.Fori(0, NI) as i:
                for n in range(5):
                    if n < 4:
                        h = i * 4 + n
                        dve.wait_ge(xT_ps, h + 1)
                        dve.tensor_copy(xT[n % 2][:, :], turn_bank[n % 2][:, :]).then_inc(xT_ready, 1)
                    if n:
                        h, par = i * 4 + n - 1, (n - 1) % 2
                        dve.wait_ge(y_ready, h + 1)
                        dve.wait_ge(stored[par], 16 * (i * 2 + (n - 1) // 2))
                        dve.tensor_copy(y[par][:, :, :],
                                        y_bank[par][:, :].rearrange("p (q d) -> p q d", q=4)).then_inc(y_out, 1)

        @block.tensor
        def _(pe):
            def turn(i, n):
                h = i * 4 + n
                pe.wait_ge(rows_loaded[n % 2], 16 * (i * 2 + n // 2 + 1))
                for q in range(4):
                    last = pe.transpose(turn_bank[n % 2][:, q * P:(q + 1) * P], rows[n % 2][:, q, :], net.ident[:, :])
                last.then_inc(xT_ps, 1)

            def hidden(i, n):
                h, e = i * 4 + n, n // 2
                pe.wait_ge(xT_ready, h + 1)
                if n % 2 == 0:
                    pe.wait_ge(w_loaded[e], 32 * (i + 1))
                for c in range(FC):
                    pe.wait_ge(hid_out, i * 4 * FC + max(n * FC + c - 3, 0))
                    pe.matmul(hid_bank[c][:, :], w1[e][:, c * P:(c + 1) * P], xT[n % 2][:, :],
                              start=True, stop=True).then_inc(hid_ready, 1)

            def output(i, n):
                h, e = i * 4 + n, n // 2
                pe.wait_ge(hid_out, (h + 1) * FC)
                pe.wait_ge(y_out, i * 4 + max(n - 1, 0))
                for q in range(4):
                    for c in range(FC):
                        last = pe.matmul(y_bank[n % 2][:, q * P:(q + 1) * P], hT[n % 2][:, c, q * P:(q + 1) * P],
                                         w2[e][:, c, :], start=(c == 0), stop=(c == FC - 1))
                last.then_inc(y_ready, 1)

            with pe.Fori(0, NI) as i:
                turn(i, 0)
                hidden(i, 0)
                for n in range(4):
                    if n + 1 < 4:
                        turn(i, n + 1)
                        hidden(i, n + 1)
                    output(i, n)


def chunked_moe_stage(nc, net):
    with ExitStack() as ctx:
        routed = Routed(nc, ctx, "L2f")
        with ExitStack() as part:
            logits = part.enter_context(nc.sbuf_tensor("L2f_logits", [P, 8, NBATCH], F32))
            norm_and_logits(nc, net, "L2f", 8, net.t["L2f_wg"], routed, logits)
            route(nc, net, "L2f", 8, None, dict(lower=net.t["lower"], whole=net.t["ones"], reset=net.t["reset8"],
                                                base=net.t["base8"]), routed, logits)
        scatter_rows(nc, net, "L2f", routed, net.slots2, SLOTS_2)
        chunk_experts(nc, net, net.t["L2f_w1"], net.t["L2f_w2"], net.slots2, net.rows2)
        combine_rows(nc, net, "L2f", routed, net.rows2, SLOTS_2, None)


def hidden_experts(nc, net, w1_dram, b1_dram, slots_dram, rows_dram, routed, ids_dram, token_of):
    E, FF, Q, N = 24, 512, 3, 4
    with ExitStack() as ctx:
        def sb(n, shape, dt=F32):
            return ctx.enter_context(nc.sbuf_tensor(f"L1h_{n}", shape, dt))

        def sem(n):
            return net.sem(f"L1h_{n}")

        w1 = [sb(f"w1{i}", [P, FF]) for i in range(N)]; b1 = [sb(f"b1{i}", [P, FF]) for i in range(N)]
        rows = [sb(f"rows{i}", [P, Q, P]) for i in range(N)]; xT = [sb(f"xT{i}", [P, Q * P]) for i in range(2)]
        hid = [sb(f"hid{i}", [P, Q, FF]) for i in range(N)]
        ids = sb("ids", [P, NBATCH], U32); id_now = [sb(f"id_now{i}", [P, 4], U32) for i in range(2)]
        where = [sb(f"where{i}", [P, 4, 2], U32) for i in range(2)]; idle = sb("idle", [P, 1])
        hid_bank, turn_bank = net.banks[0:6], net.banks[6:8]
        ids_loaded, staged, carried, listed = sem("ids_loaded"), sem("staged"), sem("carried"), [sem(f"listed{i}") for i in range(2)]
        loaded, stored, taken = ([sem(f"{n}{i}") for i in range(N)] for n in ("loaded", "stored", "taken"))
        xT_ps, xT_ready, hid_ready = (sem(n) for n in ("xT_ps", "xT_ready", "hid_ready"))
        slots = slots_dram.rearrange("(e p q) d -> e p q d", p=P, q=Q)
        outs = rows_dram[0:SLOTS_1, :].rearrange("(e p q) f -> e p q f", p=P, q=Q)
        block = ctx.enter_context(nc.Block())

        @block.sync
        def _(sp):
            sp.dma_start(ids[:, :], ids_dram).then_inc(ids_loaded, 16)

            def load(e, n):
                sp.dma_start(rows[n][:, :, :], slots[e, :, :, :]).then_inc(loaded[n], 16)
                sp.dma_start(w1[n][:, :], w1_dram[:, e, :]).then_inc(loaded[n], 16)
                sp.dma_start(b1[n][:, :], b1_dram[bass.ds(e, 1), :].to_broadcast([P, FF])).then_inc(loaded[n], 16)

            def store(e, n):
                sp.dma_start(outs[e, :, :, :], hid[n][:, :, :]).then_inc(stored[n], 16)

            for n in range(N):
                load(n, n)
            with sp.Fori(1, E // N) as i:
                for n in range(N):
                    sp.wait_ge(taken[n], i)
                    store((i - 1) * N + n, n)
                    load(i * N + n, n)
            for n in range(N):
                sp.wait_ge(taken[n], E // N)
                store(E - N + n, n)
            for n in range(N):
                sp.wait_ge(stored[n], E // N * 16)

        @block.gpsimd
        def _(pool):
            pool.wait_ge(ids_loaded, 16)
            with pool.Fori(0, NTURN // 2) as i:
                for par in range(2):
                    t = i * 2 + par
                    pool.wait_ge(listed[par], i * 8 * 16)
                    pool.tensor_copy(id_now[par][:, :], ids[:, bass.ds(t * 4, 4)])
                    pool.tensor_copy(where[par][:, :, :], routed.write[:, bass.ds(t * 4, 4), :]).then_inc(staged, 1)
                    pool.wait_ge(staged, t + 1)
                    carry_wait(pool, net, idle, carried, t)
                    for b in range(4):
                        for r in range(2):
                            pool.indirect_dma_start(
                                token_of[:, :], bass.IndirectOffsetOnAxis(where[par][:, b, r:r + 1], 0),
                                id_now[par][:, b:b + 1], None, bounds_check=SLOTS_1 - 1,
                                oob_is_err=False).then_inc(listed[par], 16)
            for par in range(2):
                pool.wait_ge(listed[par], NTURN // 2 * 8 * 16)

        @block.scalar
        def _(act):
            with act.Fori(0, E // N) as i:
                for n in range(N):
                    act.wait_ge(xT_ps, i * N + n + 1)
                    act.copy(xT[n % 2][:, :], turn_bank[n % 2][:, 0:Q * P]).then_inc(xT_ready, 1)

        @block.vector
        def _(dve):
            with dve.Fori(0, E // N) as i:
                for n in range(N):
                    dve.wait_ge(stored[n], i * 16)
                    for q in range(Q):
                        dve.wait_ge(hid_ready, (i * N + n) * Q + q + 1)
                        last = dve.tensor_tensor(hid[n][:, q, :], hid_bank[n % 2 * Q + q][:, :], b1[n][:, :], ALU.add)
                    last.then_inc(taken[n], 1)

        @block.tensor
        def _(pe):
            def turn(i, n):
                pe.wait_ge(loaded[n], 48 * (i + 1))
                for q in range(Q):
                    last = pe.transpose(turn_bank[n % 2][:, q * P:(q + 1) * P], rows[n][:, q, :], net.ident[:, :])
                last.then_inc(xT_ps, 1)

            def hidden(i, n):
                pe.wait_ge(xT_ready, i * N + n + 1)
                pe.wait_ge(taken[(n - 2) % N], i + (n >= 2))
                for q in range(Q):
                    pe.matmul(hid_bank[n % 2 * Q + q][:, :], xT[n % 2][:, q * P:(q + 1) * P], w1[n][:, :],
                              start=True, stop=True).then_inc(hid_ready, 1)

            with pe.Fori(0, E // N) as i:
                turn(i, 0)
                for n in range(N):
                    if n + 1 < N:
                        turn(i, n + 1)
                    hidden(i, n)


def mix_hidden(nc, net, gain_dram, offset_dram, routed, rows_dram, mixed_dram):
    FF = 512
    with ExitStack() as ctx:
        def sb(n, shape, dt=F32):
            return ctx.enter_context(nc.sbuf_tensor(f"L1m_{n}", shape, dt))

        def sem(n):
            return net.sem(f"L1m_{n}")

        gain = sb("gain", [P, FF]); offset = sb("offset", [P, FF])
        got = [[[sb(f"got{i}{b}{r}", [P, FF]) for r in range(2)] for b in range(4)] for i in range(2)]
        read = [sb(f"read{i}", [P, 4, 2], U32) for i in range(2)]
        mixed = [sb(f"mixed{b}", [P, FF]) for b in range(4)]; out = [sb(f"out{b}", [P, FF]) for b in range(4)]
        stats = sb("stats", [P, 4, 6]); mean_var = sb("mean_var", [P, 4, 2]); rstd = sb("rstd", [P, 4])
        idle = sb("idle", [P, 1]); pool_idle = sb("pool_idle", [P, 1])
        loaded, read_staged, chain = sem("loaded"), sem("read_staged"), sem("chain")
        scaled, mixed_ready, var_ready, rstd_ready = (
            sem(n) for n in ("scaled", "mixed_ready", "var_ready", "rstd_ready"))
        gained, affine, out_ready, carried = sem("gained"), sem("affine"), sem("out_ready"), sem("carried")
        mixed_by_batch = mixed_dram.rearrange("(b p) f -> b p f", p=P)
        gathered = [[sem(f"gathered{i}{b}") for b in range(4)] for i in range(2)]
        written = [sem(f"written{b}") for b in range(4)]
        block = ctx.enter_context(nc.Block())

        @block.sync
        def _(sp):
            sp.dma_start(gain[:, :], gain_dram).then_inc(loaded, 16)
            sp.dma_start(offset[:, :], offset_dram).then_inc(loaded, 16)
            with sp.Fori(0, NTURN) as t:
                for b in range(4):
                    sp.wait_ge(out_ready, t * 4 + b + 1)
                    sp.dma_start(mixed_by_batch[t * 4 + b, :, :], out[b][:, :]).then_inc(written[b], 16)
            for b in range(4):
                sp.wait_ge(written[b], NTURN * 16)

        @block.gpsimd
        def _(pool):
            def gather(par):
                for b in range(4):
                    for r in range(2):
                        pool.indirect_dma_start(got[par][b][r][:, :], None, rows_dram[:, :],
                                                bass.IndirectOffsetOnAxis(read[par][:, b, r:r + 1], 0),
                                                bounds_check=SLOTS_1, oob_is_err=False).then_inc(gathered[par][b], 16)

            def body(t, par, pair, final):
                if final != 1:
                    pool.wait_ge(mixed_ready, t * 4)
                    pool.wait_ge(read_staged, t + 2)
                    carry_wait(pool, net, pool_idle, carried, t)
                    gather(1 - par)
                for b in range(4):
                    pool.wait_ge(var_ready, t * 4 + b + 1)
                    pool.tensor_tensor(rstd[:, b:b + 1], rstd[:, b:b + 1], net.minus_half[:, 0:1],
                                       ALU.pow).then_inc(rstd_ready, 1)

            pool.wait_ge(read_staged, 1)
            gather(0)
            over_turns(pool, body)

        @block.scalar
        def _(act):
            def stage(t, par):
                act.copy(read[par][:, :, :], routed.read[:, bass.ds(t * 4, 4), :]).then_inc(read_staged, 1)

            stage(0, 0)
            stage(1, 1)

            def body(t, par, pair, final):
                for b in range(4):
                    act.wait_ge(gathered[par][b], (pair + 1) * 32)
                    act.wait_ge(out_ready, t * 4)
                    act.activation(mixed[b][:, :], got[par][b][0][:, :], ACT.Copy,
                                   scale=routed.gate[:, 0, bass.ds(t * 4 + b, 1)]).then_inc(scaled, 1)
                if final is None:
                    stage(t + 2, par)
                for b in range(4):
                    act.wait_ge(affine, t * 4 + b + 1)
                    act.wait_ge(written[b], t * 16)
                    act.activation(out[b][:, :], mixed[b][:, :], ACT.Relu).then_inc(out_ready, 1)

            over_turns(act, body)

        @block.vector
        def _(dve):
            dve.wait_ge(loaded, 32)

            def body(t, par, pair, final):
                link = Link(dve, chain, t, 2 * 4)
                for b in range(4):
                    dve.wait_ge(scaled, t * 4 + b + 1)
                    dve.scalar_tensor_tensor(mixed[b][:, :], got[par][b][1][:, :], routed.gate[:, 1, bass.ds(t * 4 + b, 1)],
                                             mixed[b][:, :], ALU.mult, ALU.add).then_inc(mixed_ready, 1)
                    dve.wait_ge(mixed_ready, t * 4 + b + 1)
                    link(dve.bn_stats(stats[:, b, :], mixed[b][:, :]))
                    dve.memset(idle[:, :], 0.0)
                    link(dve.bn_aggr(mean_var[:, b, :], stats[:, b, :]))
                    dve.tensor_scalar(rstd[:, b:b + 1], mean_var[:, b, 1:2], 1e-6, None, ALU.add).then_inc(var_ready, 1)
                    dve.scalar_tensor_tensor(mixed[b][:, :], mixed[b][:, :], mean_var[:, b, 0:1], gain[:, :],
                                             ALU.subtract, ALU.mult).then_inc(gained, 1)
                link.end()
                for b in range(4):
                    dve.wait_ge(rstd_ready, t * 4 + b + 1)
                    dve.wait_ge(gained, t * 4 + b + 1)
                    dve.scalar_tensor_tensor(mixed[b][:, :], mixed[b][:, :], rstd[:, b:b + 1], offset[:, :],
                                             ALU.mult, ALU.add).then_inc(affine, 1)

            over_turns(dve, body)


def output_experts(nc, net, w2_dram, b2_dram, mixed_dram, token_of, rows_dram):
    E, FF, Q, FC, N = 24, 512, 3, 4, 4
    with ExitStack() as ctx:
        def sb(n, shape, dt=F32):
            return ctx.enter_context(nc.sbuf_tensor(f"L1o_{n}", shape, dt))

        def sem(n):
            return net.sem(f"L1o_{n}")

        w2 = [sb(f"w2{i}", [P, FC, P]) for i in range(N)]; b2 = [sb(f"b2{i}", [P, P]) for i in range(N)]
        hid = [sb(f"hid{i}", [P, Q, FF]) for i in range(N)]
        hT = [sb(f"hT{i}", [P, Q, FC, P]) for i in range(2)]; y = [sb(f"y{i}", [P, Q, P]) for i in range(N)]
        turn_bank, y_bank = net.banks[0:6], net.banks[6:8]
        loaded, stored, taken = ([sem(f"{n}{i}") for i in range(N)] for n in ("loaded", "stored", "taken"))
        hT_ps, hT_ready, y_ready = (sem(n) for n in ("hT_ps", "hT_ready", "y_ready"))
        who = [sb(f"who{i}", [P, Q], U32) for i in range(N)]; idle = sb("idle", [P, 1])
        who_loaded, gathered = ([sem(f"{n}{i}") for i in range(N)] for n in ("who_loaded", "gathered"))
        carried = sem("carried")
        lists = token_of.rearrange("(e p q) o -> e p (q o)", p=P, q=Q)
        outs = rows_dram[0:SLOTS_1, :].rearrange("(e p q) d -> e p q d", p=P, q=Q)
        block = ctx.enter_context(nc.Block())

        @block.sync
        def _(sp):
            def load(e, n):
                sp.dma_start(who[n][:, :], lists[e, :, :]).then_inc(who_loaded[n], 16)
                sp.dma_start(w2[n][:, :, :], w2_dram[:, e, :, :]).then_inc(loaded[n], 16)
                sp.dma_start(b2[n][:, :], b2_dram[bass.ds(e, 1), :].to_broadcast([P, P])).then_inc(loaded[n], 16)

            def store(e, n):
                sp.dma_start(outs[e, :, :, :], y[n][:, :, :]).then_inc(stored[n], 16)

            for n in range(N):
                load(n, n)
            with sp.Fori(1, E // N) as i:
                for n in range(N):
                    sp.wait_ge(taken[n], i)
                    store((i - 1) * N + n, n)
                    load(i * N + n, n)
            for n in range(N):
                sp.wait_ge(taken[n], E // N)
                store(E - N + n, n)
            for n in range(N):
                sp.wait_ge(stored[n], E // N * 16)

        @block.gpsimd
        def _(pool):
            def gather(n):
                for q in range(Q):
                    pool.indirect_dma_start(hid[n][:, q, :], None, mixed_dram[:, :],
                                            bass.IndirectOffsetOnAxis(who[n][:, q:q + 1], 0),
                                            bounds_check=NBATCH * P - 1, oob_is_err=False).then_inc(gathered[n], 16)

            with pool.Fori(0, E // N) as i:
                for n in range(N):
                    pool.wait_ge(who_loaded[n], 16 * (i + 1))
                    pool.wait_ge(taken[n], i)
                    carry_wait(pool, net, idle, carried, i * N + n)
                    gather(n)

        @block.scalar
        def _(act):
            with act.Fori(0, E // N) as i:
                for n in range(N):
                    for q in range(Q):
                        act.wait_ge(hT_ps, (i * N + n) * Q + q + 1)
                        act.copy(hT[n % 2][:, q, :, :], turn_bank[n % 2 * Q + q][:, :].rearrange("p (c t) -> p c t", c=FC)
                                 ).then_inc(hT_ready, 1)

        @block.vector
        def _(dve):
            with dve.Fori(0, E // N) as i:
                for n in range(N):
                    dve.wait_ge(stored[n], i * 16)
                    dve.wait_ge(y_ready, i * N + n + 1)
                    dve.tensor_tensor(y[n][:, :, :], y_bank[n % 2][:, 0:Q * P].rearrange("p (q d) -> p q d", q=Q),
                                      b2[n][:, :].unsqueeze(1).to_broadcast([P, Q, P]), ALU.add).then_inc(taken[n], 1)

        @block.tensor
        def _(pe):
            def turn(i, n):
                pe.wait_ge(gathered[n], 48 * (i + 1))
                for q in range(Q):
                    for c in range(FC):
                        last = pe.transpose(turn_bank[n % 2 * Q + q][:, c * P:(c + 1) * P],
                                            hid[n][:, q, c * P:(c + 1) * P], net.ident[:, :])
                    last.then_inc(hT_ps, 1)

            def output(i, n):
                pe.wait_ge(loaded[n], 32 * (i + 1))
                pe.wait_ge(hT_ready, (i * N + n + 1) * Q)
                pe.wait_ge(taken[(n - 2) % N], i + (n >= 2))
                for q in range(Q):
                    for c in range(FC):
                        last = pe.matmul(y_bank[n % 2][:, q * P:(q + 1) * P], hT[n % 2][:, q, c, :], w2[n][:, c, :],
                                         start=(c == 0), stop=(c == FC - 1))
                last.then_inc(y_ready, 1)

            with pe.Fori(0, E // N) as i:
                turn(i, 0)
                for n in range(N):
                    if n + 1 < N:
                        turn(i, n + 1)
                    output(i, n)


def capacity_moe_stage(nc, net):
    with ExitStack() as ctx:
        t = net.t
        routed = Routed(nc, ctx, "L1f")
        with ExitStack() as part:
            logits = part.enter_context(nc.sbuf_tensor("L1f_logits", [P, 24, NBATCH], F32))
            net.zeros = part.enter_context(nc.sbuf_tensor("L1f_zeros", [P, SLOTS_1 // 4], F32))
            net.zeroed, net.filled = net.sem("L1f_zeroed"), net.sem("L1f_filled")
            norm_and_logits(nc, net, "L1f", 24, t["L1f_wg"], routed, logits, fill=True)
            route(nc, net, "L1f", 24, 86, dict(lower=t["lower32"], whole=t["ones32"], reset=t["reset24"],
                                               base=t["base24"]), routed, logits)
        scatter_rows(nc, net, "L1f", routed, net.slots1, SLOTS_1)
        hidden_experts(nc, net, t["L1f_w1"], t["L1f_b1"], net.slots1, net.hidden1, routed, t["token_ids"], net.token_of)
        mix_hidden(nc, net, t["L1f_gain"], t["L1f_offset"], routed, net.hidden1, net.mixed1)
        output_experts(nc, net, t["L1f_w2"], t["L1f_b2"], net.mixed1, net.token_of, net.rows1)
        combine_rows(nc, net, "L1f", routed, net.rows1, SLOTS_1 + 1, (t["L1f_out_w"], t["L1f_out_b"]))


def fill_zeros(net, pool, sp):
    if pool is not None:
        pool.memset(net.zeros[:, :], 0.0).then_inc(net.zeroed, 1)
        pool.wait_ge(net.zeroed, 1)
    if sp is not None:
        sp.wait_ge(net.zeroed, 1)
        slots = net.slots1.rearrange("(a p r) d -> a p (r d)", a=4, p=P)
        for a in range(4):
            sp.dma_start(slots[a, :, :], net.zeros[:, :]).then_inc(net.filled, 16)
        sp.dma_start(net.token_of.rearrange("(p r) o -> p (r o)", p=P),
                     net.zeros[:, 0:SLOTS_1 // P].bitcast(U32)).then_inc(net.filled, 16)
        sp.dma_start(net.hidden1[SLOTS_1:SLOTS_1 + 1, :], net.zeros[0:1, 0:512]).then_inc(net.filled, 16)
        sp.dma_start(net.rows1[SLOTS_1:SLOTS_1 + 1, :], net.zeros[0:1, 0:P]).then_inc(net.filled, 16)
        sp.wait_ge(net.filled, 112)




def build(nc, t, out, stages):
    with ExitStack() as ctx:
        net = Net(nc, ctx)
        net.x = net.sb("x", [P, NBATCH, P])
        net.ident = net.sb("ident", [P, P])
        net.index64 = net.sb("index64", [P, 24])
        net.ones_row = net.sb("ones_row", [1, P])
        net.minus_half = net.sb("minus_half", [P, NBATCH])
        net.plus_half = net.sb("plus_half", [P, NBATCH])
        banks = [ctx.enter_context(nc.psum_tensor(f"bank{i}", [P, 512], F32)) for i in range(8)]
        net.banks = banks
        net.t = t
        net.slots2 = nc.dram_tensor("slots2", (SLOTS_2, P), F32).ap()
        net.slots1 = nc.dram_tensor("slots1", (SLOTS_1, P), F32).ap()
        net.hidden1 = nc.dram_tensor("hidden1", (SLOTS_1 + 1, 512), F32).ap()
        net.token_of = nc.dram_tensor("token_of", (SLOTS_1, 1), U32).ap()
        net.mixed1 = nc.dram_tensor("mixed1", (NBATCH * P, 512), F32).ap()
        net.rows1 = nc.dram_tensor("rows1", (SLOTS_1 + 1, P), F32).ap()
        net.rows2 = nc.dram_tensor("rows2", (SLOTS_2, P), F32).ap()
        loaded = net.sem("start_loaded")
        with nc.Block() as block:
            @block.sync
            def _(sp):
                sp.dma_start(net.x[:, :, :], t["x"]).then_inc(loaded, 16)
                sp.dma_start(net.ident[:, :], t["ident"]).then_inc(loaded, 16)
                sp.dma_start(net.index64[:, :], t["index64"]).then_inc(loaded, 16)
                sp.wait_ge(loaded, 48)

            @block.vector
            def _(dve):
                dve.memset(net.ones_row[:, :], 1.0)
                dve.memset(net.minus_half[:, :], -0.5)
                dve.memset(net.plus_half[:, :], 0.5)

        def attention(layer, kind, heads, hd, biased, names):
            spec = dict(name=layer, kind=kind, heads=heads, hd=hd, biased=biased)
            w = {k: t[v] for k, v in names.items()}
            w["diag"], w["ctxT"] = t["diag"], t["ctxT"]
            (latent_stage if kind == "latent" else attention_stage)(nc, net, spec, w)

        if "L0x" in stages:
            attention("L0x", "cross", 16, 8, True,
                      dict(wq="L0_xattn_q_w", wk="L0k", wv="L0v", wo="L0o", bo="L0_xattn_proj_b",
                           bq="L0_xattn_q_b", bk="L0kb", bv="L0vb"))
        net.release_semaphores()
        if "L0f" in stages:
            dense_moe_stage(nc, net, dict(name="L0f", FF=512, kind="pre"), {k: t["L0f_" + k] for k in (
                "w1", "w2", "b1", "b2", "wg", "bg", "g_col", "b_col")})
        net.release_semaphores()
        if "L1x" in stages:
            attention("L1x", "cross", 16, 64, False,
                      dict(wq="L1_xattn_Wq", wk="L1_xattn_Wk", wv="L1_xattn_Wv", wo="L1o", bo="L1_xattn_bo"))
        net.release_semaphores()
        if "L1f" in stages:
            capacity_moe_stage(nc, net)
        net.release_semaphores()
        if "L2x" in stages:
            attention("L2x", "latent", 2, 64, False,
                      dict(wq="L2q", wlkv="L2lkv", wkv="L2kv", gamma="L2gamma", lat_g="L2lg", lat_b="L2lb",
                           ctx_g="L2xg", ctx_b="L2xb", ctx_tok="ctx_tok", mask="mask", wo="L2o", bo="L2_xattn_bo"))
        net.release_semaphores()
        if "L2f" in stages:
            chunked_moe_stage(nc, net)
        net.release_semaphores()
        if "L3x" in stages:
            attention("L3x", "cross", 8, 64, False,
                      dict(wq="L3_xattn_Wq", wk="L3_xattn_Wk", wv="L3_xattn_Wv", wo="L3o", bo="L3_xattn_bo"))
        net.release_semaphores()
        if "L3f" in stages:
            with ExitStack() as part:
                net.x1 = part.enter_context(nc.sbuf_tensor("x1", [P, NBATCH, P], F32))
                attention("L3s", "self", 16, 8, True,
                          {k: "L3s_" + k for k in ("wq", "wk", "wv", "wo", "bo", "bq", "bk", "bv")})
                dense_moe_stage(nc, net, dict(name="L3f", FF=256, kind="post"), {k: t["L3f_" + k] for k in (
                    "w1", "w2", "b1", "b2", "wg", "bg", "g_col", "b_col", "g1", "be1", "g2", "be2")})
        net.release_semaphores()
        stored = net.sem("stored")
        with nc.Block() as block:
            @block.sync
            def _(sp):
                sp.dma_start(out, net.x[:, :, :]).then_inc(stored, 16)
                sp.wait_ge(stored, 16)


def constants():
    p = np.arange(P)
    c = {"ident": np.eye(P, dtype=np.float32)}
    c["diag"] = (p[:, None] // 8 % 4 == np.arange(4)[None, :]).astype(np.float32)

    group = p // 32
    c["lower"] = (p[:, None] < p[None, :]).astype(np.float32)
    c["ones"] = np.ones((P, P), np.float32)
    c["lower32"] = c["lower"] * (group[:, None] == group[None, :])
    c["ones32"] = (group[:, None] == group[None, :]).astype(np.float32)
    for e in (8, 24):
        c[f"reset{e}"] = np.broadcast_to((np.arange(NBATCH) > 0).astype(np.float32), (P, e, NBATCH))
    c["base8"] = np.zeros((P, 8), np.float32)
    c["base24"] = (np.arange(24)[None, :] * 384 + group[:, None] * 86).astype(np.float32)
    c["token_ids"] = (np.arange(NBATCH)[None, :] * P + p[:, None]).astype(np.uint32)
    c["index64"] = np.broadcast_to(np.arange(24, dtype=np.float32) - 64, (P, 24))
    return c


def layouts(i):
    a = {"x": i["x"].transpose(1, 0, 2), "ctxT": i["ctx_768"].transpose(2, 0, 1)}
    a["L0_xattn_q_w"] = i["L0_xattn_q_w"]
    a["L0k"], a["L0v"] = i["L0_xattn_kv_w"][:, :P], i["L0_xattn_kv_w"][:, P:]
    a["L0kb"], a["L0vb"] = i["L0_xattn_kv_b"][:P, None], i["L0_xattn_kv_b"][None, P:]
    a["L0_xattn_q_b"] = i["L0_xattn_q_b"][:, None]
    a["L0o"] = i["L0_xattn_proj_w"][:, None, :]
    a["L0_xattn_proj_b"] = i["L0_xattn_proj_b"][None, :]
    for n, key in (("L1", "L1o"), ("L3", "L3o")):
        for k in ("Wq", "Wk", "Wv"):
            a[f"{n}_xattn_{k}"] = i[f"{n}_xattn_{k}"]
        wo = i[f"{n}_xattn_Wo"]
        a[key] = wo.reshape(-1, P, P).transpose(1, 0, 2)
        a[f"{n}_xattn_bo"] = i[f"{n}_xattn_bo"][None, :]
    f = {k: i[f"L0_ffn_{k}"] for k in ("W1", "W2", "b1", "b2", "Wg", "bg", "gamma", "beta")}
    a["L0f_w1"] = f["W1"].transpose(2, 0, 1)
    a["L0f_w2"] = f["W2"].reshape(8, P, 4, P).transpose(3, 0, 2, 1)
    a["L0f_b1"] = f["b1"].reshape(8 * 4, P).T
    a["L0f_b2"], a["L0f_wg"], a["L0f_bg"] = f["b2"], f["Wg"].T, f["bg"][None, :]
    a["L0f_g_col"], a["L0f_b_col"] = f["gamma"][:, None], f["beta"][:, None]
    s = {k[7:]: v for k, v in i.items() if k.startswith("L3_ffn_")}
    for k in ("q", "k", "v"):
        a[f"L3s_w{k}"] = s[f"W{k}"]
        a[f"L3s_b{k}"] = s[f"b{k}"][None, :] if k == "v" else s[f"b{k}"][:, None]
    a["L3s_wo"], a["L3s_bo"] = s["Wo"][:, None, :], s["bo"][None, :]
    a["L3f_w1"] = s["W1"].transpose(1, 0, 2)
    a["L3f_w2"] = s["W2"].reshape(8, 2, P, P).transpose(2, 0, 1, 3)
    a["L3f_b1"] = s["b1"].reshape(8 * 2, P).T
    a["L3f_b2"], a["L3f_wg"], a["L3f_bg"] = s["b2"], s["gW"], s["gb"][None, :]
    a["L3f_g_col"], a["L3f_b_col"] = s["ln1_g"][:, None], s["ln1_b"][:, None]
    for k, n in (("g1", "ln1_g"), ("be1", "ln1_b"), ("g2", "ln2_g"), ("be2", "ln2_b")):
        a["L3f_" + k] = np.broadcast_to(s[n], (P, P))
    a["L2f_wg"] = i["L2_ffn_router_w"].T
    a["L2f_w1"] = i["L2_ffn_w1"].transpose(1, 0, 2)
    a["L2f_w2"] = i["L2_ffn_w2"].reshape(8, 4, P, P).transpose(2, 0, 1, 3)
    s = {k[7:]: v for k, v in i.items() if k.startswith("L1_ffn_")}
    a["L1f_wg"], a["L1f_w1"], a["L1f_b1"], a["L1f_b2"] = s["Wg"], s["W1"].transpose(1, 0, 2), s["b1"], s["b2"]
    a["L1f_w2"] = s["W2"].reshape(24, 4, P, P).transpose(2, 0, 1, 3)
    a["L1f_gain"], a["L1f_offset"] = (np.repeat(s[n], 32, axis=0) for n in ("ln_hid_w", "ln_hid_b"))
    a["L1f_out_w"], a["L1f_out_b"] = (np.broadcast_to(s[n], (P, P)) for n in ("ln_out_w", "ln_out_b"))
    a["ctx_tok"] = i["ctx_768"].transpose(1, 0, 2)
    a["mask"] = i["mask_BxS2_bk0"].reshape(1, -1)
    a["L2q"], a["L2kv"], a["L2lkv"] = i["L2_xattn_Wq"].T, i["L2_xattn_Wkv"].T, i["L2_xattn_Wlkv"].T
    a["L2o"] = i["L2_xattn_Wo"].T[:, None, :]
    a["L2_xattn_bo"] = i["L2_xattn_bo"][None, :]
    gq, gk = i["L2_xattn_qn_g"], i["L2_xattn_kn_g"]
    a["L2gamma"] = np.broadcast_to(np.stack([gq, gq, gk, gk]), (P, 4, 64))
    for key, n in (("L2lg", "ln_l_g"), ("L2lb", "ln_l_b"), ("L2xg", "ln_x_g"), ("L2xb", "ln_x_b")):
        a[key] = i[f"L2_xattn_{n}"][:, None]
    return a


STAGES = ("L0x", "L0f", "L1x", "L1f", "L2x", "L2f", "L3x", "L3f")


def program(nc, arrays, stages=STAGES):
    t = {n: nc.dram_tensor(f"in_{n}", a.shape, mybir.dt.from_np(a.dtype), kind="ExternalInput").ap()
         for n, a in arrays.items()}
    out = nc.dram_tensor("out_x", (P, NBATCH, P), F32, kind="ExternalOutput").ap()
    build(nc, t, out, stages)


def kernel(**inputs):
    import concourse.bacc as _bacc
    from concourse.bass_utils import run_bass_kernel_spmd as _run

    arrays = {n: np.ascontiguousarray(a) for n, a in {**layouts(inputs), **constants()}.items()}
    nc = _bacc.Bacc("TRN2", target_bir_lowering=False, num_devices=1)
    program(nc, arrays)
    r = _run(nc, [{f"in_{n}": a for n, a in arrays.items()}], core_ids=[0])
    return np.ascontiguousarray(r.results[0]["out_x"].transpose(1, 0, 2))
```
